# Optimizing a Trainium2 kernel written in Bass

```python
import numpy as np
import jax
import jax.numpy as jnp

def _softmax(x, axis=-1):
    return jax.nn.softmax(x, axis=axis)

def _gelu(x):
    return jax.nn.gelu(x, approximate=True)

def _silu(x):
    return jax.nn.silu(x)

def _sigmoid(x):
    return jax.nn.sigmoid(x)

def _layernorm(x, axis=-1, eps=1e-05):
    m = jnp.mean(x, axis=axis, keepdims=True)
    v = jnp.var(x, axis=axis, keepdims=True)
    return (x - m) / jnp.sqrt(v + eps)

def _scatter_add(tgt, idx, src, axis=0):
    return tgt.at[idx].add(src)

def _segment_sum(src, seg, n):
    return jax.ops.segment_sum(src, seg, n)
kernel_name = 'mk_gnn_resnorm_d2_gnn_r64_334504'

def setup_inputs(seed: int=0):
    np.random.seed(seed)
    _w = jnp.asarray

    def _rec_inputs():
        import jax
        import jax.numpy as jnp
        _gk = jax.random.key(seed)
        x = -0.0002117 + 1 * jax.random.normal(jax.random.fold_in(_gk, 1), (10000, 512), jnp.float32)
        src = jax.random.randint(jax.random.fold_in(_gk, 2), (5000,), 0, 10000, jnp.int32)
        dst = jax.random.randint(jax.random.fold_in(_gk, 3), (5000,), 0, 10000, jnp.int32)
        _o = jnp.argsort(dst, stable=True)
        src = src[_o]
        dst = dst[_o]
        edge_attr_20 = jax.random.uniform(jax.random.fold_in(_gk, 12), (5000, 20), jnp.float32, 0.0, 0.999999)
        edge_attr_3 = -0.0005747 + 0.998114 * jax.random.normal(jax.random.fold_in(_gk, 13), (5000, 3), jnp.float32)
        edge_weight = jax.random.uniform(jax.random.fold_in(_gk, 15), (5000,), jnp.float32, 0.0, 0.999973)
        return (x, src, dst, edge_attr_20, edge_attr_3, edge_weight)
    x, src, dst, edge_attr_20, edge_attr_3, edge_weight = _rec_inputs()

    def _L0_gnn_setup():
        import jax, jax.numpy as jnp
        import numpy as np
        BN_EPS = 1e-05
        N_NODES, N_EDGES, D, N_LAYERS = (50000, 6250, 512, 3)
        key = jax.random.key(seed)
        k_x, k_e, k_w = jax.random.split(key, 3)
        x = jax.random.normal(k_x, (N_NODES, D), dtype=jnp.float32)
        edge_index = jax.random.randint(k_e, (2, N_EDGES), 0, N_NODES, dtype=jnp.int64)
        W = jax.random.normal(k_w, (N_LAYERS, D, D), dtype=jnp.float32) * (1.0 / np.sqrt(D))
        b = jnp.zeros((N_LAYERS, D), dtype=jnp.float32)
        gamma = jnp.ones((N_LAYERS, D), dtype=jnp.float32)
        beta = jnp.zeros((N_LAYERS, D), dtype=jnp.float32)
        return {'x': x, 'edge_index': edge_index, 'W': W, 'b': b, 'gamma': gamma, 'beta': beta}
    _L0_gnn_all = _L0_gnn_setup()
    _L0_gnn_in = {k: v for k, v in _L0_gnn_all.items() if k in ('W', 'b', 'gamma', 'beta')}
    del _L0_gnn_all

    def _L1_gnn_setup():
        import jax, jax.numpy as jnp
        import numpy as np
        N_ATOMS = 5000
        N_EDGES = 50000
        C = 128
        F = 128
        N_RBF = 20
        LOG2 = float(np.log(2.0))
        Y0 = float(1.0 / np.sqrt(4.0 * np.pi))
        Y1_SCALE = float(np.sqrt(3.0 / (4.0 * np.pi)))

        def shifted_softplus(x):
            return jax.nn.softplus(x) - LOG2

        def _forward(x, idx_i, idx_j, f_ij, rcut_ij, r_ij, W_in2f_s, W_in2f_v, Wf1, bf1, Wf2, bf2, W1_s, W1_v, W2_s, W2_v):
            n = x.shape[0]
            e = r_ij.shape[0]
            xs = x[:, :C] @ (W_in2f_s / np.sqrt(C))
            xv = jnp.einsum('nci,cf->nfi', x[:, C:].reshape(n, C, 3), W_in2f_v) / np.sqrt(C)
            sj = xs[idx_j]
            vj = xv[idx_j]
            u = r_ij / jnp.linalg.norm(r_ij, axis=-1, keepdims=True)
            Yv = Y1_SCALE * u
            o0a = sj * Y0
            o0b = jnp.einsum('efi,ei->ef', vj, Yv) / np.sqrt(3.0)
            s2 = jnp.stack([o0a, o0b], axis=-1).reshape(e, 2 * F)
            ova = sj[:, :, None] * Yv[:, None, :]
            ovb = vj * Y0
            v2 = jnp.stack([ova, ovb], axis=2)
            w1 = jnp.cross(vj, Yv[:, None, :]) / np.sqrt(2.0)
            ax, ay, az = (vj[..., 0], vj[..., 1], vj[..., 2])
            bx, by, bz = (Yv[:, None, 0], Yv[:, None, 1], Yv[:, None, 2])
            t = jnp.stack([(ax * by + ay * bx) / np.sqrt(2.0), (ay * bz + az * by) / np.sqrt(2.0), (2.0 * az * bz - ax * bx - ay * by) / np.sqrt(6.0), (az * bx + ax * bz) / np.sqrt(2.0), (ax * bx - ay * by) / np.sqrt(2.0)], axis=-1)
            h = shifted_softplus(f_ij @ Wf1 + bf1)
            W = (h @ Wf2 + bf2) * rcut_ij[:, None]
            m_s = s2 * W[:, :2 * F]
            m_v = (v2.reshape(e, 2 * F, 3) * W[:, 2 * F:4 * F, None]).reshape(e, 6 * F)
            m_w = (w1 * W[:, 4 * F:5 * F, None]).reshape(e, 3 * F)
            m_t = (t * W[:, 5 * F:6 * F, None]).reshape(e, 5 * F)
            x_ij = jnp.concatenate([m_s, m_v, m_w, m_t], axis=1)
            agg = jax.ops.segment_sum(x_ij, idx_i, num_segments=n)
            S = agg[:, :2 * F] @ (W1_s / np.sqrt(2 * F))
            V = jnp.einsum('nmi,mc->nci', agg[:, 2 * F:8 * F].reshape(n, 2 * F, 3), W1_v) / np.sqrt(2 * F)
            S = shifted_softplus(S)
            S = S @ (W2_s / np.sqrt(C))
            V = jnp.einsum('nci,cd->ndi', V, W2_v) / np.sqrt(C)
            return jnp.concatenate([S, V.reshape(n, 3 * C)], axis=1)
        key = jax.random.key(seed)
        ks = jax.random.split(key, 16)
        f32 = jnp.float32
        x = jax.random.normal(ks[0], (N_ATOMS, 4 * C), f32)
        idx_i = jnp.sort(jax.random.randint(ks[1], (N_EDGES,), 0, N_ATOMS))
        idx_j = jax.random.randint(ks[2], (N_EDGES,), 0, N_ATOMS)
        f_ij = jax.random.uniform(ks[3], (N_EDGES, N_RBF), f32)
        rcut_ij = jax.random.uniform(ks[4], (N_EDGES,), f32)
        r_ij = jax.random.normal(ks[5], (N_EDGES, 3), f32)
        W_in2f_s = jax.random.normal(ks[6], (C, F), f32)
        W_in2f_v = jax.random.normal(ks[7], (C, F), f32)
        Wf1 = jax.random.normal(ks[8], (N_RBF, F), f32) / np.sqrt(N_RBF)
        bf1 = 0.1 * jax.random.normal(ks[9], (F,), f32)
        Wf2 = jax.random.normal(ks[10], (F, 6 * F), f32) / np.sqrt(F)
        bf2 = 0.1 * jax.random.normal(ks[11], (6 * F,), f32)
        W1_s = jax.random.normal(ks[12], (2 * F, C), f32)
        W1_v = jax.random.normal(ks[13], (2 * F, C), f32)
        W2_s = jax.random.normal(ks[14], (C, C), f32)
        W2_v = jax.random.normal(ks[15], (C, C), f32)
        return dict(x=x, idx_i=idx_i, idx_j=idx_j, f_ij=f_ij, rcut_ij=rcut_ij, r_ij=r_ij, W_in2f_s=W_in2f_s, W_in2f_v=W_in2f_v, Wf1=Wf1, bf1=bf1, Wf2=Wf2, bf2=bf2, W1_s=W1_s, W1_v=W1_v, W2_s=W2_s, W2_v=W2_v)
    _L1_gnn_all = _L1_gnn_setup()
    _L1_gnn_in = {k: v for k, v in _L1_gnn_all.items() if k in ('W_in2f_s', 'W_in2f_v', 'Wf1', 'bf1', 'Wf2', 'bf2', 'W1_s', 'W1_v', 'W2_s', 'W2_v')}
    del _L1_gnn_all
    return {'x': x, 'src': src, 'dst': dst, 'edge_attr_20': edge_attr_20, 'edge_attr_3': edge_attr_3, 'edge_weight': edge_weight, 'L0_gnn_W': _L0_gnn_in['W'], 'L0_gnn_b': _L0_gnn_in['b'], 'L0_gnn_gamma': _L0_gnn_in['gamma'], 'L0_gnn_beta': _L0_gnn_in['beta'], 'L1_gnn_W_in2f_s': _L1_gnn_in['W_in2f_s'], 'L1_gnn_W_in2f_v': _L1_gnn_in['W_in2f_v'], 'L1_gnn_Wf1': _L1_gnn_in['Wf1'], 'L1_gnn_bf1': _L1_gnn_in['bf1'], 'L1_gnn_Wf2': _L1_gnn_in['Wf2'], 'L1_gnn_bf2': _L1_gnn_in['bf2'], 'L1_gnn_W1_s': _L1_gnn_in['W1_s'], 'L1_gnn_W1_v': _L1_gnn_in['W1_v'], 'L1_gnn_W2_s': _L1_gnn_in['W2_s'], 'L1_gnn_W2_v': _L1_gnn_in['W2_v']}

def reference(x, src, dst, edge_attr_20, edge_attr_3, edge_weight, L0_gnn_W, L0_gnn_b, L0_gnn_gamma, L0_gnn_beta, L1_gnn_W_in2f_s, L1_gnn_W_in2f_v, L1_gnn_Wf1, L1_gnn_bf1, L1_gnn_Wf2, L1_gnn_bf2, L1_gnn_W1_s, L1_gnn_W1_v, L1_gnn_W2_s, L1_gnn_W2_v):
    import jax
    import jax.numpy as jnp

    def _L0_gnn_ref(x, W, b, gamma, beta, edge_index):
        import jax, jax.numpy as jnp
        import numpy as np
        BN_EPS = 1e-05
        N_NODES, N_EDGES, D, N_LAYERS = (50000, 6250, 512, 3)
        N = x.shape[0]
        loops = jnp.arange(N, dtype=edge_index.dtype)
        src = jnp.concatenate([edge_index[0], loops])
        dst = jnp.concatenate([edge_index[1], loops])
        deg = jax.ops.segment_sum(jnp.ones(src.shape, jnp.float32), dst, num_segments=N)
        dinv = jax.lax.rsqrt(deg)
        norm = dinv[src] * dinv[dst]
        for l in range(W.shape[0]):
            h = x @ W[l].T
            agg = jax.ops.segment_sum(h[src] * norm[:, None], dst, num_segments=N) + b[l]
            mean = jnp.mean(agg, axis=0)
            var = jnp.mean((agg - mean) ** 2, axis=0)
            xn = (agg - mean) * jax.lax.rsqrt(var + BN_EPS)
            x = jax.nn.relu(gamma[l] * xn + beta[l])
        return x

    def _L1_gnn_ref(x, idx_i, idx_j, f_ij, rcut_ij, r_ij, W_in2f_s, W_in2f_v, Wf1, bf1, Wf2, bf2, W1_s, W1_v, W2_s, W2_v):
        import jax, jax.numpy as jnp
        import numpy as np
        N_ATOMS = 5000
        N_EDGES = 50000
        C = 128
        F = 128
        N_RBF = 20
        LOG2 = float(np.log(2.0))
        Y0 = float(1.0 / np.sqrt(4.0 * np.pi))
        Y1_SCALE = float(np.sqrt(3.0 / (4.0 * np.pi)))

        def shifted_softplus(x):
            return jax.nn.softplus(x) - LOG2

        def _forward(x, idx_i, idx_j, f_ij, rcut_ij, r_ij, W_in2f_s, W_in2f_v, Wf1, bf1, Wf2, bf2, W1_s, W1_v, W2_s, W2_v):
            n = x.shape[0]
            e = r_ij.shape[0]
            xs = x[:, :C] @ (W_in2f_s / np.sqrt(C))
            xv = jnp.einsum('nci,cf->nfi', x[:, C:].reshape(n, C, 3), W_in2f_v) / np.sqrt(C)
            sj = xs[idx_j]
            vj = xv[idx_j]
            u = r_ij / jnp.linalg.norm(r_ij, axis=-1, keepdims=True)
            Yv = Y1_SCALE * u
            o0a = sj * Y0
            o0b = jnp.einsum('efi,ei->ef', vj, Yv) / np.sqrt(3.0)
            s2 = jnp.stack([o0a, o0b], axis=-1).reshape(e, 2 * F)
            ova = sj[:, :, None] * Yv[:, None, :]
            ovb = vj * Y0
            v2 = jnp.stack([ova, ovb], axis=2)
            w1 = jnp.cross(vj, Yv[:, None, :]) / np.sqrt(2.0)
            ax, ay, az = (vj[..., 0], vj[..., 1], vj[..., 2])
            bx, by, bz = (Yv[:, None, 0], Yv[:, None, 1], Yv[:, None, 2])
            t = jnp.stack([(ax * by + ay * bx) / np.sqrt(2.0), (ay * bz + az * by) / np.sqrt(2.0), (2.0 * az * bz - ax * bx - ay * by) / np.sqrt(6.0), (az * bx + ax * bz) / np.sqrt(2.0), (ax * bx - ay * by) / np.sqrt(2.0)], axis=-1)
            h = shifted_softplus(f_ij @ Wf1 + bf1)
            W = (h @ Wf2 + bf2) * rcut_ij[:, None]
            m_s = s2 * W[:, :2 * F]
            m_v = (v2.reshape(e, 2 * F, 3) * W[:, 2 * F:4 * F, None]).reshape(e, 6 * F)
            m_w = (w1 * W[:, 4 * F:5 * F, None]).reshape(e, 3 * F)
            m_t = (t * W[:, 5 * F:6 * F, None]).reshape(e, 5 * F)
            x_ij = jnp.concatenate([m_s, m_v, m_w, m_t], axis=1)
            agg = jax.ops.segment_sum(x_ij, idx_i, num_segments=n)
            S = agg[:, :2 * F] @ (W1_s / np.sqrt(2 * F))
            V = jnp.einsum('nmi,mc->nci', agg[:, 2 * F:8 * F].reshape(n, 2 * F, 3), W1_v) / np.sqrt(2 * F)
            S = shifted_softplus(S)
            S = S @ (W2_s / np.sqrt(C))
            V = jnp.einsum('nci,cd->ndi', V, W2_v) / np.sqrt(C)
            return jnp.concatenate([S, V.reshape(n, 3 * C)], axis=1)
        return _forward(x, idx_i, idx_j, f_ij, rcut_ij, r_ij, W_in2f_s, W_in2f_v, Wf1, bf1, Wf2, bf2, W1_s, W1_v, W2_s, W2_v)
    edge_index = jnp.stack([src, dst])
    x = _layernorm(x + _L0_gnn_ref(x, L0_gnn_W, L0_gnn_b, L0_gnn_gamma, L0_gnn_beta, edge_index), axis=-1)
    x = _layernorm(x + _L1_gnn_ref(x, src, dst, edge_attr_20, edge_weight, edge_attr_3, L1_gnn_W_in2f_s, L1_gnn_W_in2f_v, L1_gnn_Wf1, L1_gnn_bf1, L1_gnn_Wf2, L1_gnn_bf2, L1_gnn_W1_s, L1_gnn_W1_v, L1_gnn_W2_s, L1_gnn_W2_v), axis=-1)
    return x

_drawn_inputs = setup_inputs


def setup_inputs(seed=0):
    import zlib

    import numpy as np

    out = dict(_drawn_inputs(seed))
    spreads = {'L0_gnn_b': (0.0, 0.8), 'L0_gnn_gamma': (1.0, 0.2), 'L0_gnn_beta': (0.0, 0.1)}
    factors = {'edge_attr_20': 3.585,
     'edge_weight': 3.428,
     'L1_gnn_bf1': 8.0,
     'L1_gnn_bf2': 5.435,
     'L1_gnn_W1_s': 5.763,
     'L1_gnn_W2_s': 5.736}
    for name, (base, spread) in spreads.items():
        noise = np.random.default_rng([zlib.crc32(name.encode()), seed]).standard_normal(out[name].shape)
        drawn = base * np.exp(spread * noise) if base else spread * noise
        out[name] = jnp.asarray(drawn.astype(out[name].dtype))
    for name, factor in factors.items():
        out[name] = (out[name] * factor).astype(out[name].dtype)
    return out
```

```python
from contextlib import ExitStack

import numpy as np
import concourse.bass as bass
from concourse import mybir

F32, F32R = mybir.dt.float32, mybir.dt.float32r
BF16, I32 = mybir.dt.bfloat16, mybir.dt.int32
ALU, ACT, AX = mybir.AluOpType, mybir.ActivationFunctionType, mybir.AxisListType

P = 128
BN_EPS = LN_EPS = 1e-5
LOG2 = float(np.log(2.0))
Y0 = float(1.0 / np.sqrt(4.0 * np.pi))
Y1_SCALE = float(np.sqrt(3.0 / (4.0 * np.pi)))
SKIP = 1 << 20


class Steps:

    def __init__(self, engine, sem, base=0):
        self.engine, self.sem, self.base, self.n = engine, sem, base, 0

    def link(self, instruction):
        instruction.then_inc(self.sem, 1)
        self.n += 1
        self.engine.wait_ge(self.sem, self.base + self.n)


class Machine:

    def __init__(self, nc, ctx, n_nodes, n_edges, d):
        self.nc, self.ctx = nc, ctx
        self.N, self.E, self.D = n_nodes, n_edges, d
        self.C = d // P
        self.BLK = 4 * P
        self.NB = -(-n_nodes // self.BLK)
        self.NPAD = self.NB * self.BLK
        self.NCOL = self.NB * 4
        self.TP = (n_nodes - (self.NB - 1) * self.BLK) // 4
        self.ET = -(-n_edges // P)
        self.EPAD = self.ET * P
        self.EP = n_edges // self.ET
        assert self.EP * self.ET == n_edges and self.TP * 4 + (self.NB - 1) * self.BLK == n_nodes
        assert self.ET % 4 == 0 and self.NB % 4 == 0

    def sb(self, name, shape, dt=F32):
        return self.ctx.enter_context(self.nc.sbuf_tensor(name, shape, dt))

    def ps(self, name, shape, dt=F32):
        return self.ctx.enter_context(self.nc.psum_tensor(name, shape, dt))

    def sem(self, name):
        self.counters.append(self.nc.alloc_semaphore(name=name))
        return self.counters[-1]

    def dram(self, name, shape, dt=F32):
        return self.nc.dram_tensor(name, shape, dt).ap()


def stage(function):
    def run(m, *args):
        m.counters = []
        function(m, *args)
        m.nc.clear_and_free_semaphores(m.counters)
        m.nc.all_engine_barrier()
    return run


def block_rows(table, m):
    return table.rearrange("(b p j) f -> b p (j f)", p=P, j=4)


def at(view, i):
    if isinstance(i, int):
        return view[i]
    return view[bass.ds(i, 1)].rearrange("a p f -> (a p) f")


@stage
def constants(m, k):
    nc = m.nc
    filled, made = m.sem("const_filled"), m.sem("const_made")
    with nc.Block() as block:
        @block.gpsimd
        def _(pool):
            nc.gpsimd.memset(k.ident[:], 0.0).then_inc(filled, 1)
            nc.gpsimd.memset(k.ones[:], 1.0).then_inc(filled, 1)
            nc.gpsimd.iota(k.count[:], [[1, P]], base=0, channel_multiplier=0,
                           allow_small_or_imprecise_dtypes=True).then_inc(made, 1)
            nc.gpsimd.iota(k.part[:], [[0, 1]], base=0, channel_multiplier=1,
                           allow_small_or_imprecise_dtypes=True).then_inc(made, 1)
            ge(pool, filled, 2)
            nc.gpsimd.affine_select(out=k.ident[:], in_=k.ident[:], compare_op=ALU.not_equal, fill=1.0,
                                    base=0, pattern=[[-1, P]], channel_multiplier=1).then_inc(made, 1)
            nc.gpsimd.affine_select(out=k.before[:], in_=k.ones[:], compare_op=ALU.is_gt, fill=0.0,
                                    base=0, pattern=[[1, P]], channel_multiplier=-1).then_inc(made, 1)
            nc.gpsimd.affine_select(out=k.after[:], in_=k.ones[:], compare_op=ALU.is_gt, fill=0.0,
                                    base=0, pattern=[[-1, P]], channel_multiplier=1).then_inc(made, 1)
            ge(pool, made, 5)


@stage
def sort_by(m, k, tag, key_dram, payload, width, sorted_dram, table):
    nc, ET, NC = m.nc, m.ET, m.NCOL
    w = k.sort
    loaded, filled, cols, hot = (m.sem(f"{tag}_{s}") for s in ("loaded", "filled", "cols", "hot"))
    diag, row_ps, row_out = (m.sem(f"{tag}_{s}") for s in ("diag", "row_ps", "row_out"))
    counted, pre_in, pre_ps, base0 = (m.sem(f"{tag}_{s}") for s in ("counted", "pre_in", "pre_ps", "base0"))
    lt, cnt_ps, base, look_ps, looked = (m.sem(f"{tag}_{s}") for s in ("lt", "cnt_ps", "base", "look_ps", "looked"))
    vec, place, staged = m.sem(f"{tag}_vec"), m.sem(f"{tag}_place"), m.sem(f"{tag}_staged")
    sent = [m.sem(f"{tag}_sent{q}") for q in range(2)]
    root_in, root = m.sem(f"{tag}_root_in"), m.sem(f"{tag}_root")
    rows4 = ET // 4
    ident4 = k.ident[:].unsqueeze(1).to_broadcast([P, 4, P])

    def spread_out(dve, n):
        q, which = divmod(n, 2)
        dve.wait_ge(row_ps, n + 1)
        span = slice(q * 4 * P, (q + 1) * 4 * P)
        if which == 0:
            nc.vector.tensor_copy(w.keyrow[:, span], w.ps_row[0][:]).then_inc(row_out, 1)
        else:
            nc.vector.tensor_scalar(w.hot_loT[:, span], w.ps_row[1][:], k.part[:, 0:1], None,
                                    ALU.is_equal).then_inc(row_out, 1)

    with nc.Block() as block:
        @block.sync
        def _(sp):
            sp.wait_ge(filled, 1)
            sp.dma_start(w.key[0:m.EP, :], key_dram.rearrange("(p t) -> p t", t=ET)).then_inc(loaded, 16)

        @block.vector
        def _(dve):
            v = Steps(dve, vec)
            nc.vector.memset(w.key[:], m.NPAD - 1).then_inc(filled, 1)
            dve.wait_ge(loaded, 16)
            v.link(nc.vector.tensor_scalar(w.tmp[:], w.key[:], 9, 2, ALU.logical_shift_right, ALU.logical_shift_left))
            v.link(nc.vector.tensor_scalar(w.tmp2[:], w.key[:], 3, None, ALU.bitwise_and))
            v.link(nc.vector.tensor_tensor(w.tmp[:], w.tmp[:], w.tmp2[:], ALU.bitwise_or))
            v.link(nc.vector.tensor_copy(w.colf[:], w.tmp[:]))
            v.link(nc.vector.tensor_scalar(w.tmp[:], w.key[:], 2, P - 1, ALU.logical_shift_right, ALU.bitwise_and))
            v.link(nc.vector.tensor_copy(w.lof[:], w.tmp[:]))
            v.link(nc.vector.tensor_copy(w.keyf[:], w.key[:]))
            nc.vector.tensor_tensor(w.hot_col[:], k.count[:, 0:NC].unsqueeze(1).to_broadcast([P, ET, NC]),
                                    w.colf[:].unsqueeze(2).to_broadcast([P, ET, NC]), ALU.is_equal).then_inc(hot, 1)
            nc.vector.tensor_tensor(w.hot_lo[:], k.count[:].unsqueeze(1).to_broadcast([P, ET, P]),
                                    w.lof[:].unsqueeze(2).to_broadcast([P, ET, P]), ALU.is_equal).then_inc(hot, 1)
            for q in range(rows4):
                for which, src in enumerate((w.keyf, w.lof)):
                    n = 2 * q + which
                    if n >= 2:
                        dve.wait_ge(row_ps, n - 1)
                    nc.vector.tensor_tensor(w.diag[n % 2][:], ident4,
                                            src[:, 4 * q:4 * q + 4].unsqueeze(2).to_broadcast([P, 4, P]),
                                            ALU.mult).then_inc(diag, 1)
                    if n >= 1:
                        spread_out(dve, n - 1)
            spread_out(dve, 2 * rows4 - 1)
            dve.wait_ge(counted, 1)
            cnt4 = w.cnt[:].rearrange("p (b j) -> p b j", j=4)
            v.link(nc.vector.tensor_copy(w.cnt[:], w.ps_cnt[:, 0:NC]))
            v.link(nc.vector.tensor_reduce(w.rowsum[:], cnt4, axis=AX.X, op=ALU.add))
            nc.vector.tensor_copy(w.rowsum2[:], w.rowsum[:]).then_inc(pre_in, 1)
            dve.wait_ge(pre_ps, 1)
            v.link(nc.vector.tensor_copy(w.pre[:], w.ps_pre[:, 0:2 * m.NB]))
            total = w.pre[:, m.NB:2 * m.NB]
            v.link(nc.vector.tensor_tensor_scan(w.scan[:], k.ones[:, 0:m.NB], total, 0.0, ALU.mult, ALU.add))
            v.link(nc.vector.tensor_tensor(w.scan[:], w.scan[:], total, ALU.subtract))
            start4 = w.base[0][:].rearrange("p (b j) -> p b j", j=4)
            v.link(nc.vector.tensor_tensor(start4[:, :, 0], w.pre[:, 0:m.NB], w.scan[:], ALU.add))
            for j in range(1, 4):
                v.link(nc.vector.tensor_tensor(start4[:, :, j], start4[:, :, j - 1], cnt4[:, :, j - 1], ALU.add))
            v.link(nc.vector.tensor_tensor(w.end[:], w.base[0][:], w.cnt[:], ALU.add))
            v.link(nc.vector.tensor_scalar(w.has[:], w.cnt[:], 0.0, None, ALU.is_gt))
            if table is not None:
                v.link(nc.vector.tensor_scalar(w.tmpn[:], w.has[:], -float(SKIP), float(SKIP) - 1.0, ALU.mult, ALU.add))
                v.link(nc.vector.tensor_tensor(w.tmpn[:], w.tmpn[:], w.end[:], ALU.add))
                nc.vector.tensor_copy(table.row[:], w.tmpn[:]).then_inc(root_in, 1)
                dve.wait_ge(root, 1)
                v.link(nc.vector.reciprocal(table.dinv[:], w.tmpn2[:]))
                for dst, a in ((table.self_w, table.dinv), (table.edge_w, w.has)):
                    v.link(nc.vector.tensor_tensor(dst[:], a[:], table.dinv[:], ALU.mult))
            nc.vector.memset(w.rank[:], 0.0).then_inc(base0, 1)
            dve.wait_ge(base0, 1)
            dve.wait_ge(hot, 2)
            dve.wait_ge(row_out, 2 * rows4)

            def tile_place(t, q, first):
                if not first:
                    dve.wait_ge(look_ps, t - 0)
                dve.wait_ge(cnt_ps, t + 1)
                nc.vector.tensor_tensor(w.base[1 - q][:], w.base[q][:], w.ps_new[q][:, 0:NC], ALU.add).then_inc(base, 1)
                nc.vector.scalar_tensor_tensor(w.junk[:], w.keyrow[:, bass.ds(t * P, P)], w.keyf[:, bass.ds(t, 1)],
                                               k.after[:], ALU.is_equal, ALU.mult,
                                               accum_out=w.rank[:, bass.ds(t, 1)]).then_inc(looked, 1)
                dve.wait_ge(look_ps, t + 1)
                nc.vector.scalar_tensor_tensor(w.junk2[:], w.ps_look[q][:, 0:NC], 1.0,
                                               w.hot_col[:, bass.ds(t, 1), :].rearrange("p a c -> p (a c)"),
                                               ALU.mult, ALU.mult, accum_out=w.pos[:, bass.ds(t, 1)]).then_inc(looked, 1)
                dve.wait_ge(looked, 2 * t + 2)

            tile_place(0, 0, True)
            tile_place(1, 1, False)
            with dve.Fori(1, ET // 2) as g:
                tile_place(2 * g, 0, False)
                tile_place(2 * g + 1, 1, False)
            v.link(nc.vector.tensor_tensor(w.pos[:], w.pos[:], w.rank[:], ALU.add))
            nc.vector.tensor_copy(w.place[:], w.pos[:]).then_inc(place, 1)

        @block.tensor
        def _(pe):
            for n in range(2 * rows4):
                pe.wait_ge(diag, n + 1)
                if n >= 2:
                    pe.wait_ge(row_out, n - 1)
                nc.tensor.matmul(w.ps_row[n % 2][:], k.ones[:], w.diag[n % 2][:].rearrange("p a b -> p (a b)"),
                                 start=True, stop=True).then_inc(row_ps, 1)
            pe.wait_ge(hot, 2)

            def count(out, t, start, stop):
                return nc.tensor.matmul(out, w.hot_lo[:, bass.ds(t, 1), :].rearrange("p a c -> p (a c)"),
                                        w.hot_col[:, bass.ds(t, 1), :].rearrange("p a c -> p (a c)"),
                                        start=start, stop=stop)
            count(w.ps_cnt[:, 0:NC], 0, True, False)
            with pe.Fori(1, ET - 1) as t:
                count(w.ps_cnt[:, 0:NC], t, False, False)
            count(w.ps_cnt[:, 0:NC], ET - 1, False, True).then_inc(counted, 1)
            pe.wait_ge(pre_in, 1)
            nc.tensor.matmul(w.ps_pre[:, 0:m.NB], k.before[:], w.rowsum2[:], start=True, stop=True)
            nc.tensor.matmul(w.ps_pre[:, m.NB:2 * m.NB], k.ones[:], w.rowsum2[:], start=True, stop=True).then_inc(pre_ps, 1)

            def tile(t, q, first):
                if not first:
                    pe.wait_ge(base, t - 1)
                count(w.ps_new[q][:, 0:NC], t, True, True).then_inc(cnt_ps, 1)
                pe.wait_ge(lt, t + 1)
                if first is True:
                    pe.wait_ge(base0, 1)
                else:
                    pe.wait_ge(base, t)
                    pe.wait_ge(looked, 2 * t - 2)
                nc.tensor.matmul(w.ps_look[q][:, 0:NC], w.lt[q][:], w.base[q][:], start=True, stop=True).then_inc(look_ps, 1)
            tile(0, 0, True)
            tile(1, 1, False)
            with pe.Fori(1, ET // 2) as g:
                tile(2 * g, 0, False)
                tile(2 * g + 1, 1, False)

        @block.scalar
        def _(act):
            if table is not None:
                act.wait_ge(root_in, 1)
                nc.scalar.activation(w.tmpn2[:], w.cnt[:], ACT.Sqrt, bias=k.ones[:, 0:1]).then_inc(root, 1)
            act.wait_ge(row_out, 2 * rows4)

            def stage(t, q, first):
                if not first:
                    act.wait_ge(look_ps, t - 1)
                nc.scalar.copy(w.lt[q][:], w.hot_loT[:, bass.ds(t * P, P)]).then_inc(lt, 1)
            stage(0, 0, True)
            stage(1, 1, True)
            with act.Fori(1, ET // 2) as g:
                stage(2 * g, 0, False)
                stage(2 * g + 1, 1, False)

        @block.gpsimd
        def _(pool):
            ge(pool, place, 1)

            def fill(t, q, gen):
                if not isinstance(t, int) or t > 0:
                    ge(pool, staged, 2 * t)
                if gen is not None:
                    ge(pool, sent[q], 16 * gen)
                nc.gpsimd.tensor_copy(w.idx[q][:], w.place[:, bass.ds(t, 1)]).then_inc(staged, 1)
                nc.gpsimd.tensor_copy(w.pay[q][:, 0:width],
                                      payload[:, bass.ds(t, 1), 0:width].rearrange("p a w -> p (a w)")).then_inc(staged, 1)

            def scatter(q):
                pool.indirect_dma_start(sorted_dram, bass.IndirectOffsetOnAxis(ap=w.idx[q][:, 0:1], axis=0),
                                        w.pay[q][:, 0:width], None).then_inc(sent[q], 16)
            fill(0, 0, None)
            fill(1, 1, None)
            scatter(0)
            with pool.Fori(1, ET // 2) as g:
                fill(2 * g, 0, g)
                scatter(1)
                fill(2 * g + 1, 1, g)
                scatter(0)
            ge(pool, staged, 2 * ET)
            scatter(1)
            for q in range(2):
                ge(pool, sent[q], 16 * (ET // 2))


class Turn:

    def __init__(self, group, s, last):
        self.group, self.s, self.last = group, s, last

    def block(self, off=0):
        return self.group * 4 + (self.s + off)

    def slot(self, off, ring):
        return (self.s + off) % ring

    def round(self, off, ring):
        return self.group * (4 // ring) + (self.s + off) // ring

    def runs(self, off):
        return not isinstance(self.group, int) or 0 <= self.block(off) <= self.last


def turns(engine, body, first, last, loop_from, loop_groups, blocks):
    for b in range(first, loop_from):
        body(Turn(0, b, blocks - 1))
    with engine.Fori(0, loop_groups) as g:
        for u in range(4):
            body(Turn(g, loop_from + u, blocks - 1))
    for b in range(loop_from + 4 * loop_groups, last + 1):
        body(Turn(0, b, blocks - 1))


def ge(engine, sem, value):
    if not isinstance(value, int) or value > 0:
        engine.wait_ge(sem, value)


@stage
def sorted_edges(m, k, tag, sorted_dram, width, key_word, rows, skey, sbuf):
    nc, ET = m.nc, m.ET
    loaded, vec, diag, out_ps, out = (m.sem(f"{tag}_{s}") for s in ("re_loaded", "re_vec", "re_diag", "re_ps", "re_out"))
    ident4 = k.ident[:].unsqueeze(1).to_broadcast([P, 4, P])
    w = k.sort
    with nc.Block() as block:
        @block.sync
        def _(sp):
            sp.dma_start(sbuf[:, :, 0:width], sorted_dram.rearrange("(t p) w -> p t w", p=P)).then_inc(loaded, 16)

        @block.vector
        def _(dve):
            v = Steps(dve, vec)
            dve.wait_ge(loaded, 16)
            v.link(nc.vector.tensor_copy(skey[:], sbuf[:, :, key_word]))
            for q in range(ET // 4):
                ge(dve, out_ps, q - 1)
                nc.vector.tensor_tensor(w.diag[q % 2][:], ident4,
                                        skey[:, 4 * q:4 * q + 4].unsqueeze(2).to_broadcast([P, 4, P]),
                                        ALU.mult).then_inc(diag, 1)

        @block.tensor
        def _(pe):
            for q in range(ET // 4):
                pe.wait_ge(diag, q + 1)
                ge(pe, out, q - 1)
                nc.tensor.matmul(w.ps_row[q % 2][:], k.ones[:], w.diag[q % 2][:].rearrange("p a b -> p (a b)"),
                                 start=True, stop=True).then_inc(out_ps, 1)

        @block.scalar
        def _(act):
            for q in range(ET // 4):
                act.wait_ge(out_ps, q + 1)
                nc.scalar.copy(rows[:, q * 4 * P:(q + 1) * 4 * P], w.ps_row[q % 2][:]).then_inc(out, 1)
            act.wait_ge(out, ET // 4)


@stage
def edge_tables(m, k, dinv_dram, sorted_dram):
    nc, ET = m.nc, m.ET
    e = k.edge
    stored, loaded, staged, vec = (m.sem(f"edge_{s}") for s in ("stored", "loaded", "staged", "vec"))
    got = [m.sem(f"edge_got{q}") for q in range(2)]
    kept, srcs = m.sem("edge_kept"), m.sem("edge_srcs")
    with nc.Block() as block:
        @block.sync
        def _(sp):
            sp.dma_start(dinv_dram.rearrange("(b p j) o -> p b (j o)", p=P, j=4),
                         k.node.dinv[:].rearrange("p (b j) -> p b j", j=4)).then_inc(stored, 16)
            sp.dma_start(e.tiles[:], sorted_dram.rearrange("(t p) w -> t (p w)", p=P)).then_inc(loaded, 16)
            sp.wait_ge(stored, 16)

        @block.gpsimd
        def _(pool):
            nc.gpsimd.tensor_scalar(e.src[:], e.pair[:, :, 0], m.N - 1, None, ALU.min).then_inc(srcs, 1)
            ge(pool, srcs, 1)
            ge(pool, stored, 16)

            def point(t, q):
                ge(pool, staged, t)
                ge(pool, kept, t - 1)
                nc.gpsimd.tensor_copy(e.idx[q][:], e.src[:, bass.ds(t, 1)]).then_inc(staged, 1)

            def fetch(q):
                pool.indirect_dma_start(e.val[q][:], None, dinv_dram,
                                        bass.IndirectOffsetOnAxis(ap=e.idx[q][:, 0:1], axis=0)).then_inc(got[q], 16)
            point(0, 0)
            point(1, 1)
            fetch(0)
            with pool.Fori(1, ET // 2) as g:
                point(2 * g, 0)
                fetch(1)
                point(2 * g + 1, 1)
                fetch(0)
            ge(pool, staged, ET)
            fetch(1)

        @block.vector
        def _(dve):
            v = Steps(dve, vec)
            dve.wait_ge(loaded, 16)
            keys = e.tiles[:].rearrange("t (p w) -> t p w", w=2)[:, :, 1]
            v.link(nc.vector.tensor_copy(e.tkey[:], keys))
            v.link(nc.vector.tensor_scalar(e.tjunk[:], e.tkey[:], e.tkey[:, 0:1], 0.0, ALU.is_equal, ALU.add,
                                           accum_out=e.run[:]))
            v.link(nc.vector.tensor_scalar(e.run2[:], k.part[0:ET, 0:1], float(P), -1.0, ALU.mult, ALU.add))
            v.link(nc.vector.tensor_tensor(e.run2[:], e.run2[:], e.run[:], ALU.add))
            v.link(nc.vector.tensor_copy(e.fix_row[:], e.run2[:]))
            firsts = e.rows[0:ET, :].rearrange("q (t p) -> q t p", p=P)[:, :, 0]
            v.link(nc.vector.tensor_scalar(e.lacks[:], firsts, e.tkey[:, P - 1:P], None, ALU.is_equal))
            v.link(nc.vector.tensor_tensor(e.lacks[:], e.lacks[:], k.before[0:ET, 0:ET], ALU.mult))

            def keep(t, q, gen):
                dve.wait_ge(got[q], 16 * (gen + 1))
                nc.vector.tensor_copy(e.dsrc[:, bass.ds(t, 1)], e.val[q][:]).then_inc(kept, 1)
            with dve.Fori(0, ET // 2) as g:
                keep(2 * g, 0, g)
                keep(2 * g + 1, 1, g)
            dve.wait_ge(kept, ET)


@stage
def prepare(m, k, layer, w_dram):
    nc, C, tag = m.nc, m.C, f"prep{layer}"
    loaded, tps, hi, lo = (m.sem(f"{tag}_{s}") for s in ("loaded", "tps", "hi", "lo"))
    vec, var, root, diag, spread, out = (m.sem(f"{tag}_{s}") for s in ("vec", "var", "root", "diag", "spread", "out"))
    raw = k.R[0][:].rearrange("p (c f) -> p c f", c=C)
    stats, weights = layer > 0, w_dram is not None
    s = k.bn
    with nc.Block() as block:
        @block.sync
        def _(sp):
            if weights:
                sp.dma_start(raw, w_dram[layer].rearrange("(c p) f -> p c f", p=P)).then_inc(loaded, 16)

        @block.tensor
        def _(pe):
            if weights:
                pe.wait_ge(loaded, 16)
                for q in range(C):
                    ge(pe, lo, q - 1)
                    for c in range(C):
                        t = nc.tensor.transpose(k.ps_a[q % 2][:, c * P:(c + 1) * P], raw[:, c, q * P:(q + 1) * P], k.ident[:])
                    t.then_inc(tps, 1)
            if stats:
                for i in range(2):
                    pe.wait_ge(diag, i + 1)
                    nc.tensor.matmul(k.ps_b[i][:], k.ones[:], k.R[1 + i][:, 0:m.D], start=True, stop=True).then_inc(spread, 1)

        @block.scalar
        def _(act):
            if stats:
                act.wait_ge(var, 1)
                nc.scalar.activation(s.std[:], s.mv[:, :, 1], ACT.Sqrt, bias=k.eps[:, 0:1]).then_inc(root, 1)
            if weights:
                for q in range(C):
                    act.wait_ge(tps, q + 1)
                    nc.scalar.copy(k.whi[:, q, :], k.ps_a[q % 2][:]).then_inc(hi, 1)
            if stats:
                for i, dst in enumerate((k.scale, k.shift)):
                    act.wait_ge(spread, i + 1)
                    nc.scalar.copy(dst[:], k.ps_b[i][:]).then_inc(out, 1)
                act.wait_ge(out, 2)

        @block.vector
        def _(dve):
            v = Steps(dve, vec)
            if stats:
                prm = k.param[:, :, (layer - 1) * C:layer * C]
                for c in range(C):
                    last = nc.vector.bn_aggr(s.mv[:, c, :], k.stat[:, c, :])
                    last.then_inc(var if c == C - 1 else vec, 1)
                v.n = C - 1
                dve.wait_ge(vec, C - 1)
                dve.wait_ge(var, 1)
                v.link(nc.vector.tensor_tensor(s.mean[:], s.mv[:, :, 0], prm[:, 0, :], ALU.add))
                v.link(nc.vector.tensor_tensor(s.mean[:], prm[:, 0, :], s.mean[:], ALU.subtract))
                dve.wait_ge(root, 1)
                v.link(nc.vector.reciprocal(s.scale[:], s.std[:]))
                v.link(nc.vector.tensor_tensor(s.scale[:], s.scale[:], prm[:, 1, :], ALU.mult))
                v.link(nc.vector.tensor_tensor(s.shift[:], s.scale[:], s.mean[:], ALU.mult))
                v.link(nc.vector.tensor_tensor(s.shift[:], s.shift[:], prm[:, 2, :], ALU.add))
                for i, col in enumerate((s.scale, s.shift)):
                    nc.vector.tensor_tensor(k.R[1 + i][:, 0:m.D].rearrange("p (c f) -> p c f", c=C),
                                            k.ident[:].unsqueeze(1).to_broadcast([P, C, P]),
                                            col[:].unsqueeze(2).to_broadcast([P, C, P]), ALU.mult).then_inc(diag, 1)
            if weights:
                for q in range(C):
                    dve.wait_ge(hi, q + 1)
                    nc.vector.tensor_tensor(k.wlo[:, q, :], k.ps_a[q % 2][:], k.whi[:, q, :].bitcast(F32),
                                            ALU.subtract).then_inc(lo, 1)
                dve.wait_ge(lo, C)


@stage
def merge(m, k, layer, table, merged_dram):
    nc, ET, D, tag = m.nc, m.ET, m.D, f"merge{layer}"
    e, norm = k.edge, layer > 0
    staged, scaled, shifted, weighted, sel = (m.sem(f"{tag}_{s}") for s in ("staged", "scaled", "shifted", "weighted", "sel"))
    merged, copied = m.sem(f"{tag}_merged"), m.sem(f"{tag}_copied")
    got = [m.sem(f"{tag}_got{r}") for r in range(4)]
    put = [m.sem(f"{tag}_put{r}") for r in range(4)]
    lasts, lacking, fix_ps, fixed, sent = (m.sem(f"{tag}_{s}") for s in ("lasts", "lacking", "fix_ps", "fixed", "sent"))
    m_rows = merged_dram.rearrange("(t p) f -> t p f", p=P)
    G = [k.R[r][:, 0:D] for r in range(4)]
    O = [k.rows_out[r // 2][:, (r % 2) * D:(r % 2 + 1) * D] for r in range(4)]
    last_rows, fix = k.Cb[0][0:ET, 0:D], k.Cb[1][0:ET, 0:D]
    group = ET // 4

    def run(engine, body, extra=0):
        turns(engine, body, 0, ET - 1 + extra, 4, group - 2, ET)

    with nc.Block() as block:
        @block.gpsimd
        def _(pool):
            def body(t):
                b, r = t.block(), t.slot(0, 4)
                ge(pool, staged, b + 1)
                ge(pool, merged, b - 2)
                if t.runs(1):
                    nc.gpsimd.tensor_copy(e.idx[t.slot(1, 4)][:], e.src[:, bass.ds(t.block(1), 1)]).then_inc(staged, 1)
                pool.indirect_dma_start(G[r], None, table,
                                        bass.IndirectOffsetOnAxis(ap=e.idx[r][:, 0:1], axis=0)).then_inc(got[r], 16)
            nc.gpsimd.tensor_copy(e.idx[0][:], e.src[:, 0:1]).then_inc(staged, 1)
            run(pool, body)
            ge(pool, lacking, 16)
            pool.indirect_dma_start(fix, None, merged_dram,
                                    bass.IndirectOffsetOnAxis(ap=e.fix_row[:, 0:1], axis=0)).then_inc(lasts, 16)
            ge(pool, fixed, 1)
            pool.indirect_dma_start(merged_dram, bass.IndirectOffsetOnAxis(ap=e.fix_row[:, 0:1], axis=0),
                                    fix, None).then_inc(sent, 16)
            ge(pool, sent, 16)

        @block.vector
        def _(dve):
            def body(t):
                b, r = t.block(), t.slot(0, 4)
                if norm:
                    dve.wait_ge(got[r], 16 * (t.round(0, 4) + 1))
                    nc.vector.tensor_tensor(G[r], G[r], k.scale[:], ALU.mult).then_inc(scaled, 1)
                ge(dve, merged, b - 1)
                nc.vector.tensor_scalar(e.same[r % 2][:], e.rows[:, bass.ds(b * P, P)], e.skey[:, bass.ds(b, 1)],
                                        None, ALU.is_equal).then_inc(sel, 1)
                if norm:
                    dve.wait_ge(scaled, b + 1)
                    nc.vector.tensor_tensor(G[r], G[r], k.shift[:], ALU.add).then_inc(shifted, 1)
            run(dve, body)
            dve.wait_ge(fix_ps, 1)
            dve.wait_ge(lasts, 16)
            nc.vector.tensor_tensor(fix, fix, k.ps_b[0][0:ET, :], ALU.add).then_inc(fixed, 1)

        @block.scalar
        def _(act):
            def body(t):
                if t.runs(0):
                    b, r = t.block(), t.slot(0, 4)
                    if norm:
                        act.wait_ge(shifted, b + 1)
                    else:
                        act.wait_ge(got[r], 16 * (t.round(0, 4) + 1))
                    nc.scalar.activation(G[r], G[r], ACT.Relu if norm else ACT.Copy,
                                         scale=e.dsrc[:, bass.ds(b, 1)]).then_inc(weighted, 1)
                if t.runs(-1):
                    b, r = t.block(-1), t.slot(-1, 4)
                    act.wait_ge(merged, b + 1)
                    ge(act, put[r], 16 * t.round(-1, 4))
                    nc.scalar.copy(O[r], k.ps_a[r % 2][:]).then_inc(copied, 1)
            run(act, body, 1)

        @block.tensor
        def _(pe):
            def body(t):
                b, r = t.block(), t.slot(0, 4)
                pe.wait_ge(weighted, b + 1)
                pe.wait_ge(sel, b + 1)
                ge(pe, copied, b - 1)
                nc.tensor.matmul(k.ps_a[r % 2][:], e.same[r % 2][:], G[r], start=True, stop=True).then_inc(merged, 1)
            run(pe, body)
            pe.wait_ge(lacking, 16)
            nc.tensor.matmul(k.ps_b[0][0:ET, :], e.lacks[:], last_rows, start=True, stop=True).then_inc(fix_ps, 1)

        @block.sync
        def _(sp):
            def body(t):
                b, r = t.block(), t.slot(0, 4)
                sp.wait_ge(copied, b + 1)
                sp.dma_start(at(m_rows, b), O[r]).then_inc(put[r], 16)
            run(sp, body)
            for r in range(4):
                sp.wait_ge(put[r], 16 * group)
            sp.dma_start(last_rows, m_rows[:, P - 1, :]).then_inc(lacking, 16)
            sp.wait_ge(lacking, 16)


@stage
def dense(m, k, layer, table, out_table, merged_dram):
    nc, C, D, NB, tag = m.nc, m.C, m.D, m.NB, f"dense{layer}"
    norm = layer > 0
    n = k.node
    scaled, shifted, weighted, joined = (m.sem(f"{tag}_{s}") for s in ("scaled", "shifted", "weighted", "joined"))
    turned, hi, lo, product = (m.sem(f"{tag}_{s}") for s in ("turned", "hi", "lo", "product"))
    copied, counted, back, rows = (m.sem(f"{tag}_{s}") for s in ("copied", "counted", "back", "rows"))
    staged = m.sem(f"{tag}_staged")
    read = [m.sem(f"{tag}_read{r}") for r in range(4)]
    got = [m.sem(f"{tag}_got{r}") for r in range(2)]
    put = [m.sem(f"{tag}_put{r}") for r in range(2)]
    src = block_rows(table[0:(NB - 1) * m.BLK, :], m) if layer == 0 else block_rows(table, m)
    dst = block_rows(out_table, m)
    quarter = [slice(j * D, (j + 1) * D) for j in range(4)]

    def run(engine, body):
        turns(engine, body, -4, NB, 4, (NB - 8) // 4, NB)

    with nc.Block() as block:
        @block.sync
        def _(sp):
            def body(t):
                if t.runs(4):
                    r = t.slot(4, 4)
                    ge(sp, turned, 4 * (t.block() + 1))
                    if layer == 0 and isinstance(t.group, int) and t.block(4) == NB - 1:
                        sp.dma_start(k.R[r][0:m.TP, :], table[(NB - 1) * m.BLK:m.N, :]
                                     .rearrange("(p j) f -> p (j f)", j=4)).then_inc(read[r], 16)
                    else:
                        sp.dma_start(k.R[r][:], at(src, t.block(4))).then_inc(read[r], 16)
                if t.runs(-1):
                    q = t.slot(-1, 2)
                    sp.wait_ge(rows, 4 * (t.block(-1) + 1))
                    sp.dma_start(at(dst, t.block(-1)), k.rows_out[q][:]).then_inc(put[q], 16)
            turns(sp, body, -4, NB, 4, (NB - 12) // 4, NB)
            for q in range(2):
                sp.wait_ge(put[q], 16 * (NB // 2))

        @block.gpsimd
        def _(pool):
            def body(t):
                if not t.runs(3):
                    return
                b, q = t.block(3), t.slot(3, 2)
                ge(pool, staged, b + 1)
                ge(pool, joined, 4 * (b - 1))
                if t.runs(4):
                    nc.gpsimd.tensor_copy(n.idx[t.slot(4, 4)][:], n.row[:, bass.ds(4 * (b + 1), 4)]).then_inc(staged, 1)
                for j in range(4):
                    pool.indirect_dma_start(k.Cb[q][:, quarter[j]], None, merged_dram,
                                            bass.IndirectOffsetOnAxis(ap=n.idx[t.slot(3, 4)][:, j:j + 1], axis=0),
                                            bounds_check=m.EPAD - 1, oob_is_err=False).then_inc(got[q], 16)
                if norm:
                    r = t.slot(3, 4)
                    for j in range(4):
                        ge(pool, scaled, 4 * b + j + 1)
                        nc.gpsimd.tensor_tensor(k.R[r][:, quarter[j]], k.R[r][:, quarter[j]], k.shift[:],
                                                ALU.add).then_inc(shifted, 1)
            nc.gpsimd.tensor_copy(n.idx[0][:], n.row[:, 0:4]).then_inc(staged, 1)
            run(pool, body)

        @block.vector
        def _(dve):
            def body(t):
                for j in range(4):
                    if t.runs(1):
                        b, q = t.block(1), t.slot(1, 2)
                        dve.wait_ge(hi, 4 * b + j + 1)
                        nc.vector.tensor_tensor(k.ylo[q][:, :, j * P:(j + 1) * P],
                                                k.ps_a[j % 2][:].rearrange("p (c n) -> p c n", c=C),
                                                k.yhi[q][:, :, j * P:(j + 1) * P].bitcast(F32),
                                                ALU.subtract).then_inc(lo, 1)
                    if norm and t.runs(3):
                        r = t.slot(3, 4)
                        if j == 0:
                            dve.wait_ge(read[r], 16 * (t.round(3, 4) + 1))
                        nc.vector.tensor_tensor(k.R[r][:, quarter[j]], k.R[r][:, quarter[j]], k.scale[:],
                                                ALU.mult).then_inc(scaled, 1)
                    if t.runs(2):
                        b, r, q = t.block(2), t.slot(2, 4), t.slot(2, 2)
                        if j == 0:
                            dve.wait_ge(got[q], 64 * (t.round(2, 2) + 1))
                        dve.wait_ge(weighted, 4 * b + j + 1)
                        nc.vector.scalar_tensor_tensor(k.R[r][:, quarter[j]], k.Cb[q][:, quarter[j]],
                                                       n.edge_w[:, bass.ds(4 * b + j, 1)], k.R[r][:, quarter[j]],
                                                       ALU.mult, ALU.add).then_inc(joined, 1)
                    if t.runs(0):
                        b = t.block()
                        dve.wait_ge(copied, 4 * b + j + 1)
                        view = k.aggT[t.slot(0, 2)][:, j, :]
                        if isinstance(t.group, int) and b == NB - 1:
                            view = view.rearrange("p (j n) -> p j n", j=4)[:, :, 0:m.TP]
                        nc.vector.bn_stats(k.stat[:, j, bass.ds(6 * b, 6)], view).then_inc(counted, 1)
            run(dve, body)
            dve.wait_ge(counted, 4 * NB)

        @block.scalar
        def _(act):
            def body(t):
                for j in range(4):
                    if t.runs(1):
                        b, q = t.block(1), t.slot(1, 2)
                        act.wait_ge(turned, 4 * b + j + 1)
                        ge(act, product, 4 * (b - 1))
                        nc.scalar.copy(k.yhi[q][:, :, j * P:(j + 1) * P],
                                       k.ps_a[j % 2][:].rearrange("p (c n) -> p c n", c=C)).then_inc(hi, 1)
                    if t.runs(2):
                        b, r = t.block(2), t.slot(2, 4)
                        if norm:
                            act.wait_ge(shifted, 4 * b + j + 1)
                        else:
                            act.wait_ge(read[r], 16 * (t.round(2, 4) + 1))
                        nc.scalar.activation(k.R[r][:, quarter[j]], k.R[r][:, quarter[j]],
                                             ACT.Relu if norm else ACT.Copy,
                                             scale=n.self_w[:, bass.ds(4 * b + j, 1)]).then_inc(weighted, 1)
                    if t.runs(0):
                        b, q = t.block(), t.slot(0, 2)
                        act.wait_ge(product, 4 * b + j + 1)
                        ge(act, back, 4 * (b - 1))
                        ge(act, counted, 4 * (b - 1))
                        nc.scalar.copy(k.aggT[q][:, j, :], k.ps_b[j % 2][:]).then_inc(copied, 1)
                    if t.runs(-1):
                        b, q = t.block(-1), t.slot(-1, 2)
                        act.wait_ge(back, 4 * b + j + 1)
                        ge(act, put[q], 16 * t.round(-1, 2))
                        nc.scalar.copy(k.rows_out[q][:, quarter[j]], k.ps_c[j % 2][:]).then_inc(rows, 1)
            run(act, body)

        @block.tensor
        def _(pe):
            def body(t):
                for j in range(4):
                    if t.runs(1):
                        b, r = t.block(1), t.slot(1, 4)
                        pe.wait_ge(joined, 4 * b + j + 1)
                        ge(pe, lo, 4 * b + j - 1)
                        for c in range(C):
                            i = nc.tensor.transpose(k.ps_a[j % 2][:, c * P:(c + 1) * P],
                                                    k.R[r][:, j * D + c * P:j * D + (c + 1) * P], k.ident[:])
                        i.then_inc(turned, 1)
                    if t.runs(0):
                        b, q = t.block(), t.slot(0, 2)
                        if j == 0:
                            pe.wait_ge(lo, 4 * (b + 1))
                        ge(pe, copied, 4 * b + j - 1)
                        parts = [(k.whi, k.yhi[q]), (k.whi, k.ylo[q]), (k.wlo, k.yhi[q])]
                        for c in range(C):
                            for i, (wt, y) in enumerate(parts):
                                mm = nc.tensor.matmul(k.ps_b[j % 2][:], wt[:, c, j * P:(j + 1) * P], y[:, c, :],
                                                      start=(c == 0 and i == 0), stop=(c == C - 1 and i == 2))
                        mm.then_inc(product, 1)
                    if t.runs(-1):
                        b, q = t.block(-1), t.slot(-1, 2)
                        if j == 0:
                            pe.wait_ge(copied, 4 * (b + 1))
                        ge(pe, rows, 4 * b + max(j - 1, 0))
                        for c in range(C):
                            i = nc.tensor.transpose(k.ps_c[j % 2][:, c * P:(c + 1) * P],
                                                    k.aggT[q][:, c, j * P:(j + 1) * P], k.ident[:])
                        i.then_inc(back, 1)
            run(pe, body)


@stage
def finish_gcn(m, k, table, x_dram, x2_dram, out_dram):
    nc, D, NB = m.nc, m.D, m.NB
    f = k.fin
    tag = "fin"
    scaled, shifted, relued, summed, meas = (m.sem(f"{tag}_{s}") for s in ("scaled", "shifted", "relued", "summed", "meas"))
    moments, root1, small, var2, root2, ready = (m.sem(f"{tag}_{s}") for s in ("moments", "root1", "small", "var2", "root2", "ready"))
    normed, outed = m.sem(f"{tag}_normed"), m.sem(f"{tag}_outed")
    read = [m.sem(f"{tag}_read{r}") for r in range(4)]
    xread = [m.sem(f"{tag}_xread{r}") for r in range(2)]
    put = [m.sem(f"{tag}_put{r}") for r in range(2)]
    src, x2 = block_rows(table, m), block_rows(x2_dram, m)
    full = (NB - 1) * m.BLK
    x_full, out_full = block_rows(x_dram[0:full, :], m), block_rows(out_dram[0:full, :], m)
    x_tail, out_tail = (a[full:m.N, :].rearrange("(p j) f -> p (j f)", j=4) for a in (x_dram, out_dram))
    quarter = [slice(j * D, (j + 1) * D) for j in range(4)]

    def tail(t, off):
        return isinstance(t.group, int) and t.block(off) == NB - 1

    def run(engine, body):
        turns(engine, body, -2, NB - 1, 4, (NB - 8) // 4, NB)

    with nc.Block() as block:
        @block.sync
        def _(sp):
            def body(t):
                if t.runs(2):
                    r, q = t.slot(2, 4), t.slot(2, 2)
                    ge(sp, normed, 4 * (t.block(2) - 3))
                    sp.dma_start(k.R[r][:], at(src, t.block(2))).then_inc(read[r], 16)
                    ge(sp, summed, 4 * (t.block(2) - 1))
                    if tail(t, 2):
                        sp.dma_start(k.Cb[q][0:m.TP, :], x_tail).then_inc(xread[q], 16)
                    else:
                        sp.dma_start(k.Cb[q][:], at(x_full, t.block(2))).then_inc(xread[q], 16)
                if t.runs(0):
                    q = t.slot(0, 2)
                    sp.wait_ge(normed, 4 * (t.block() + 1))
                    sp.dma_start(at(x2, t.block()), k.rows_out[q][:]).then_inc(put[q], 16)
                    sp.wait_ge(outed, 4 * (t.block() + 1))
                    if tail(t, 0):
                        sp.dma_start(out_tail, f.out[q][0:m.TP, :]).then_inc(put[q], 16)
                    else:
                        sp.dma_start(at(out_full, t.block()), f.out[q][:]).then_inc(put[q], 16)
            turns(sp, body, -2, NB - 1, 4, (NB - 8) // 4, NB)
            for q in range(2):
                sp.wait_ge(put[q], 32 * (NB // 2))

        @block.gpsimd
        def _(pool):
            def body(t):
                if t.runs(2):
                    r = t.slot(2, 4)
                    for j in range(4):
                        ge(pool, scaled, 4 * t.block(2) + j + 1)
                        nc.gpsimd.tensor_tensor(k.R[r][:, quarter[j]], k.R[r][:, quarter[j]], k.shift[:],
                                                ALU.add).then_inc(shifted, 1)
            run(pool, body)

        @block.vector
        def _(dve):
            def body(t):
                if t.runs(2):
                    r = t.slot(2, 4)
                    dve.wait_ge(read[r], 16 * (t.round(2, 4) + 1))
                    for j in range(4):
                        nc.vector.tensor_tensor(k.R[r][:, quarter[j]], k.R[r][:, quarter[j]], k.scale[:],
                                                ALU.mult).then_inc(scaled, 1)
                if t.runs(1):
                    b, r, q = t.block(1), t.slot(1, 4), t.slot(1, 2)
                    dve.wait_ge(xread[q], 16 * (t.round(1, 2) + 1))
                    for j in range(4):
                        dve.wait_ge(relued, 4 * b + j + 1)
                        nc.vector.tensor_tensor(k.R[r][:, quarter[j]], k.R[r][:, quarter[j]], k.Cb[q][:, quarter[j]],
                                                ALU.add).then_inc(summed, 1)
                    for j in range(4):
                        dve.wait_ge(summed, 4 * b + j + 1)
                        if j == 0:
                            ge(dve, normed, 4 * (b - 1))
                            ge(dve, outed, 4 * (b - 1))
                        nc.vector.bn_stats(f.st[:, j, :], k.R[r][:, quarter[j]]).then_inc(meas, 1)
                    dve.drain()
                    for j in range(4):
                        nc.vector.bn_aggr(f.mv[q][:, j, :], f.st[:, j, :]).then_inc(moments, 1)
                    dve.wait_ge(root1, b + 1)
                    nc.vector.reciprocal(f.rstd[q][:], f.std[q][:]).then_inc(small, 1)
                    dve.wait_ge(small, 3 * b + 1)
                    nc.vector.scalar_tensor_tensor(f.nmr[q][:], f.mv[q][:, :, 0], -1.0, f.rstd[q][:],
                                                   ALU.mult, ALU.mult).then_inc(small, 1)
                    nc.vector.tensor_tensor(f.v2[q][:], f.mv[q][:, :, 1], f.rstd[q][:], ALU.mult).then_inc(small, 1)
                    dve.wait_ge(small, 3 * b + 3)
                    nc.vector.tensor_tensor(f.v2[q][:], f.v2[q][:], f.rstd[q][:], ALU.mult).then_inc(var2, 1)
                    dve.wait_ge(root2, b + 1)
                    nc.vector.reciprocal(f.rstd2[q][:], f.std2[q][:]).then_inc(ready, 1)
            run(dve, body)

        @block.scalar
        def _(act):
            def body(t):
                if t.runs(1):
                    b, r, q = t.block(1), t.slot(1, 4), t.slot(1, 2)
                    for j in range(4):
                        act.wait_ge(shifted, 4 * b + j + 1)
                        nc.scalar.activation(k.R[r][:, quarter[j]], k.R[r][:, quarter[j]], ACT.Relu).then_inc(relued, 1)
                    act.wait_ge(moments, 4 * b + 4)
                    nc.scalar.activation(f.std[q][:], f.mv[q][:, :, 1], ACT.Sqrt, bias=k.eps[:, 0:1]).then_inc(root1, 1)
                    act.wait_ge(var2, b + 1)
                    nc.scalar.activation(f.std2[q][:], f.v2[q][:], ACT.Sqrt, bias=k.eps[:, 0:1]).then_inc(root2, 1)
                if t.runs(0):
                    b, r, q = t.block(), t.slot(0, 4), t.slot(0, 2)
                    act.wait_ge(ready, b + 1)
                    ge(act, put[q], 32 * t.round(0, 2))
                    for j in range(4):
                        nc.scalar.activation(k.rows_out[q][:, quarter[j]], k.R[r][:, quarter[j]], ACT.Identity,
                                             scale=f.rstd[q][:, j:j + 1], bias=f.nmr[q][:, j:j + 1]).then_inc(normed, 1)
                    for j in range(4):
                        act.wait_ge(normed, 4 * b + j + 1)
                        nc.scalar.activation(f.out[q][:, quarter[j]], k.rows_out[q][:, quarter[j]], ACT.Copy,
                                             scale=f.rstd2[q][:, j:j + 1]).then_inc(outed, 1)
            run(act, body)


@stage
def edge_net(m, k, l, w):
    nc, ET, C = m.nc, m.ET, P
    nbr, f_in = w["Wf1"].shape[0], 6
    loaded, zeroed, vec, sc = (m.sem(f"net_{s}") for s in ("loaded", "zeroed", "vec", "sc"))
    sq, root, wt, wps, wout, wprod = (m.sem(f"net_{s}") for s in ("sq", "root", "wt", "wps", "wout", "wprod"))
    staged, turned, tout, hps, absd, relu = (m.sem(f"net_{s}") for s in ("staged", "turned", "tout", "hps", "absd", "relu"))
    groups = ET // 4
    with nc.Block() as block:
        @block.sync
        def _(sp):
            n = 0
            sp.wait_ge(zeroed, 1)
            loads = [(l.Ws[:], w["W_in2f_s"]), (l.Wv[:], w["W_in2f_v"]), (l.W2s[:], w["W2_s"]), (l.W2v[:], w["W2_v"]),
                     (l.W1s[:], w["W1_s"].rearrange("(f c) o -> f c o", c=2)),
                     (l.W1v[:], w["W1_v"].rearrange("(f c) o -> f c o", c=2)),
                     (l.Wf2[:], w["Wf2"][:, 0:4 * P]), (l.bf1[:], w["bf1"].rearrange("(f o) -> f o", o=1)),
                     (l.bf2[:], w["bf2"][0:4 * P].rearrange("(o f) -> o f", o=1).to_broadcast([P, 4 * P]))]
            loads += [(l.Wf1[32 * g:32 * g + nbr, g, :], w["Wf1"]) for g in range(4)]
            for dst, src in loads:
                sp.dma_start(dst, src).then_inc(loaded, 16)
                n += 16
            m.net_loads = n

        @block.vector
        def _(dve):
            v = Steps(dve, vec)
            nc.vector.memset(l.Wf1[:], 0.0).then_inc(zeroed, 1)
            v.link(nc.vector.memset(l.fst[0][:], 0.0))
            v.link(nc.vector.memset(l.fst[1][:], 0.0))
            r = l.pay[:, :, 3:6]
            v.link(nc.vector.tensor_tensor(l.yv[:], r, r, ALU.mult))
            nc.vector.tensor_reduce(l.n2[:], l.yv[:], axis=AX.X, op=ALU.add).then_inc(sq, 1)
            dve.wait_ge(root, 1)
            v.link(nc.vector.reciprocal(l.n2[:], l.norm[:]))
            v.link(nc.vector.tensor_tensor(l.yv[:], r, l.n2[:].unsqueeze(2).to_broadcast([P, ET, 3]), ALU.mult))
            v.link(nc.vector.tensor_scalar(l.yv[:], l.yv[:], Y1_SCALE, None, ALU.mult))
            rc = l.pay[:, :, 2:3].to_broadcast([P, ET, 3])
            v.link(nc.vector.tensor_tensor(l.c_v[:], l.yv[:], rc, ALU.mult))
            v.link(nc.vector.tensor_scalar(l.c_s[:], l.c_v[:], 1.0 / float(np.sqrt(3.0)), None, ALU.mult))
            v.link(nc.vector.tensor_scalar(l.c_0[:], l.pay[:, :, 2], Y0, None, ALU.mult))
            dve.wait_ge(loaded, m.net_loads)
            root_c, root_2f = 1.0 / float(np.sqrt(C)), 1.0 / float(np.sqrt(2 * P))
            for t, c in ((l.Ws, root_c), (l.Wv, root_c), (l.W2s, root_c), (l.W2v, root_c), (l.W1s, root_2f), (l.W1v, root_2f)):
                nc.vector.tensor_scalar(t[:], t[:], c, None, ALU.mult).then_inc(wt, 1)
            dve.wait_ge(wps, 1)
            nc.vector.tensor_copy(l.W1vT[:], l.ps[0][:, 0:2 * P].rearrange("p (a b) -> p a b", a=2)).then_inc(wout, 1)
            dve.wait_ge(wprod, 1)
            v.link(nc.vector.tensor_copy(l.Wvv[:], l.ps[1][:, 0:2 * P].rearrange("p (a b) -> p a b", a=2)))

            def group(g, q):
                nc.vector.tensor_copy(l.fst[q][:, :, 0:nbr], l.pay[:, bass.ds(4 * g, 4), f_in:f_in + nbr]).then_inc(staged, 1)
                dve.wait_ge(turned, g + 1)
                nc.vector.tensor_copy(l.fT[q][:], l.ps[2 + q][:, 0:P]).then_inc(tout, 1)
                dve.wait_ge(absd, g + 1)
                nc.vector.tensor_scalar(l.hT[:, bass.ds(4 * P * g, 4 * P)], l.ps[4 + q][:], l.bf1[:, 0:1], 0.0,
                                        ALU.add, ALU.max).then_inc(relu, 1)
            with dve.Fori(0, groups // 2) as g:
                group(2 * g, 0)
                group(2 * g + 1, 1)
            dve.wait_ge(sc, 2)
            dve.wait_ge(relu, groups)
            v.link(nc.vector.scalar_tensor_tensor(l.hT[:], l.big[:], -LOG2, l.hT[:], ALU.add, ALU.add))

        @block.tensor
        def _(pe):
            pe.wait_ge(wt, 6)
            for a in range(2):
                t = nc.tensor.transpose(l.ps[0][:, a * P:(a + 1) * P], l.W1v[:, a, :], k.ident[:])
            t.then_inc(wps, 1)
            pe.wait_ge(wout, 1)
            for a in range(2):
                t = nc.tensor.matmul(l.ps[1][:, a * P:(a + 1) * P], l.W1vT[:, a, :], l.W2v[:], start=True, stop=True)
            t.then_inc(wprod, 1)

            def group(g, q, first):
                pe.wait_ge(staged, g + 1)
                if not first:
                    pe.wait_ge(tout, g - 1)
                nc.tensor.transpose(l.ps[2 + q][:, 0:P], l.fst[q][:].rearrange("p a b -> p (a b)"), k.ident[:]).then_inc(turned, 1)
                pe.wait_ge(tout, g + 1)
                if not first:
                    pe.wait_ge(relu, g - 1)
                for a in range(4):
                    t = nc.tensor.matmul(l.ps[4 + q][:, a * P:(a + 1) * P], l.Wf1[:, a, :],
                                         l.fT[q][:], start=True, stop=True)
                t.then_inc(hps, 1)
            group(0, 0, True)
            group(1, 1, True)
            with pe.Fori(1, groups // 2) as g:
                group(2 * g, 0, False)
                group(2 * g + 1, 1, False)

        @block.scalar
        def _(act):
            act.wait_ge(sq, 1)
            nc.scalar.activation(l.norm[:], l.n2[:], ACT.Sqrt).then_inc(root, 1)
            act.wait_ge(loaded, m.net_loads)

            def group(g, q):
                act.wait_ge(hps, g + 1)
                nc.scalar.activation(l.big[:, bass.ds(4 * P * g, 4 * P)], l.ps[4 + q][:], ACT.Abs, bias=l.bf1[:, 0:1]).then_inc(absd, 1)
            with act.Fori(0, groups // 2) as g:
                group(2 * g, 0)
                group(2 * g + 1, 1)
            act.wait_ge(absd, groups)
            nc.scalar.activation(l.big[:], l.big[:], ACT.Exp, scale=-1.0).then_inc(sc, 1)
            act.wait_ge(sc, 1)
            nc.scalar.activation(l.big[:], l.big[:], ACT.Ln, bias=k.ones[:, 0:1]).then_inc(sc, 1)


@stage
def messages(m, k, l, x2_dram):
    nc, ET, D = m.nc, m.ET, m.D
    names = ("staged", "turned", "xT", "hcopy", "filt", "maps", "wb", "same", "cont", "u", "vec", "side",
             "msg", "sums", "agg", "outs", "kept")
    s = {n: m.sem(f"msg_{n}") for n in names}
    got = [m.sem(f"msg_got{r}") for r in range(4)]
    G = [l.G[r][:] for r in range(4)]
    DV = 7

    def run(engine, body, first=-1, last=ET):
        turns(engine, body, first, last, 4, ET // 4 - 2, ET)

    with nc.Block() as block:
        @block.gpsimd
        def _(pool):
            def body(t):
                if t.runs(1):
                    b, r = t.block(1), t.slot(1, 4)
                    ge(pool, s["staged"], b + 1)
                    ge(pool, s["turned"], b - 2)
                    if t.runs(2):
                        nc.gpsimd.tensor_copy(l.idx[t.slot(2, 4)][:], l.dst[:, bass.ds(b + 1, 1)]).then_inc(s["staged"], 1)
                    pool.indirect_dma_start(G[r], None, x2_dram,
                                            bass.IndirectOffsetOnAxis(ap=l.idx[r][:, 0:1], axis=0)).then_inc(got[r], 16)
            nc.gpsimd.tensor_copy(l.idx[0][:], l.dst[:, 0:1]).then_inc(s["staged"], 1)
            run(pool, body)

        @block.tensor
        def _(pe):
            def body(t):
                if t.runs(0):
                    b, q = t.block(), t.slot(0, 2)
                    pe.wait_ge(s["msg"], b + 1)
                    pe.wait_ge(s["side"], 3 * (b + 1))
                    pe.wait_ge(s["same"], b + 1)
                    ge(pe, s["agg"], 8 * b)
                    for c in range(8):
                        i = nc.tensor.matmul(l.ps[4 + c // 4][:, (c % 4) * P:(c % 4 + 1) * P], l.msg[q][:, c, :],
                                             l.same[q][:], start=True, stop=True)
                    i.then_inc(s["sums"], 1)
                if t.runs(1):
                    b, q, r = t.block(1), t.slot(1, 2), t.slot(1, 4)
                    pe.wait_ge(got[r], 16 * (t.round(1, 4) + 1))
                    ge(pe, s["xT"], b)
                    for c in range(4):
                        src = G[r][:, 0:P] if c == 0 else G[r][:, P:D].rearrange("p (c i) -> p i c", i=3)[:, c - 1, :]
                        i = nc.tensor.transpose(l.ps[0][:, c * P:(c + 1) * P], src, k.ident[:])
                    i.then_inc(s["turned"], 1)
                    pe.wait_ge(s["hcopy"], b + 1)
                    ge(pe, s["wb"], b)
                    nc.tensor.matmul(l.ps[1][:], l.hb[q][:], l.Wf2[:], start=True, stop=True).then_inc(s["filt"], 1)
                    pe.wait_ge(s["xT"], b + 1)
                    ge(pe, s["msg"], b - 1)
                    for c in range(4):
                        i = nc.tensor.matmul(l.ps[2 + q][:, c * P:(c + 1) * P], l.xT[q][:, c, :],
                                             (l.Ws if c == 0 else l.Wv)[:], start=True, stop=True)
                    i.then_inc(s["maps"], 1)
                if t.runs(-1):
                    b, q = t.block(-1), t.slot(-1, 2)
                    pe.wait_ge(s["agg"], 8 * (b + 1))
                    ge(pe, s["kept"], 2 * b)
                    o = l.ps[6]
                    for c in range(2):
                        nc.tensor.matmul(o[:, 0:P], l.W1s[:, c, :], l.agg[q][:, c, :], start=(c == 0), stop=(c == 1))
                    for i in range(3):
                        for c in range(2):
                            x = nc.tensor.matmul(o[:, (i + 1) * P:(i + 2) * P], l.agg[q][:, 2 + 3 * c + i, :], l.Wvv[:, c, :],
                                                 start=(c == 0), stop=(c == 1))
                    x.then_inc(s["outs"], 1)
            run(pe, body)

        @block.scalar
        def _(act):
            def body(t):
                if t.runs(1):
                    b, q = t.block(1), t.slot(1, 2)
                    ge(act, s["filt"], b - 1)
                    nc.scalar.copy(l.hb[q][:], l.hT[:, bass.ds(P * b, P)]).then_inc(s["hcopy"], 1)
                    act.wait_ge(s["turned"], b + 1)
                    ge(act, s["maps"], b - 1)
                    nc.scalar.copy(l.xT[q][:], l.ps[0][:].rearrange("p (c n) -> p c n", c=4)).then_inc(s["xT"], 1)
                    act.wait_ge(s["u"], b + 1)
                    ge(act, s["sums"], b - 1)
                    for i in range(3):
                        nc.scalar.activation(l.msg[q][:, 2 + i, :], l.u[q][:], ACT.Copy,
                                             scale=l.c_v[:, bass.ds(b, 1), i]).then_inc(s["side"], 1)
                if t.runs(-1):
                    b = t.block(-1)
                    act.wait_ge(s["outs"], b + 1)
                    nc.scalar.copy(l.sT[:, bass.ds(P * b, P)], l.ps[6][:, 0:P]).then_inc(s["kept"], 1)
                    nc.scalar.copy(l.V[:, bass.ds(b, 1), :].rearrange("p a (d i) -> p (a d) i", i=3),
                                   l.ps[6][:, P:4 * P].rearrange("p (i d) -> p d i", i=3)).then_inc(s["kept"], 1)
            run(act, body)
            act.wait_ge(s["kept"], 2 * ET)

        @block.vector
        def _(dve):
            def body(t):
                if t.runs(1):
                    b, q = t.block(1), t.slot(1, 2)
                    n0 = DV * b

                    def link(i, step):
                        i.then_inc(s["vec"], 1)
                        dve.wait_ge(s["vec"], n0 + step)
                    dve.wait_ge(s["filt"], b + 1)
                    ge(dve, s["same"], b)
                    nc.vector.tensor_tensor(l.Wb[q][:], l.ps[1][:], l.bf2[:], ALU.add).then_inc(s["wb"], 1)
                    ge(dve, s["sums"], b - 1)
                    nc.vector.tensor_scalar(l.same[q][:], l.rows[:, bass.ds(P * b + 4, P)], l.skey[:, bass.ds(b, 1)],
                                            None, ALU.is_equal).then_inc(s["same"], 1)
                    nc.vector.tensor_scalar(l.cont[q][:], l.rows[:, bass.ds(P * b + 4, P)], l.rows[:, bass.ds(P * b + 3, 1)],
                                            None, ALU.is_equal).then_inc(s["cont"], 1)
                    dve.wait_ge(s["wb"], b + 1)
                    dve.wait_ge(s["maps"], b + 1)
                    sj = l.ps[2 + q][:, 0:P]
                    v = [l.ps[2 + q][:, (i + 1) * P:(i + 2) * P] for i in range(3)]
                    fs = l.Wb[q][:, 0:2 * P].rearrange("p (f c) -> p c f", c=2)
                    fv = l.Wb[q][:, 2 * P:4 * P].rearrange("p (f c) -> p c f", c=2)
                    c0 = l.c_0[:, bass.ds(b, 1)]
                    ge(dve, s["side"], 3 * (b - 1))
                    nc.vector.tensor_tensor(l.u[q][:], sj, fv[:, 0, :], ALU.mult).then_inc(s["u"], 1)
                    link(nc.vector.scalar_tensor_tensor(l.msg[q][:, 0, :], sj, c0, fs[:, 0, :], ALU.mult, ALU.mult), 1)
                    link(nc.vector.tensor_scalar(l.dot[:], v[0], l.c_s[:, bass.ds(b, 1), 0], None, ALU.mult), 2)
                    link(nc.vector.scalar_tensor_tensor(l.dot[:], v[1], l.c_s[:, bass.ds(b, 1), 1], l.dot[:], ALU.mult, ALU.add), 3)
                    link(nc.vector.scalar_tensor_tensor(l.dot[:], v[2], l.c_s[:, bass.ds(b, 1), 2], l.dot[:], ALU.mult, ALU.add), 4)
                    link(nc.vector.tensor_tensor(l.msg[q][:, 1, :], l.dot[:], fs[:, 1, :], ALU.mult), 5)
                    for i in range(2):
                        link(nc.vector.scalar_tensor_tensor(l.msg[q][:, 5 + i, :], v[i], c0, fv[:, 1, :], ALU.mult, ALU.mult), 6 + i)
                    nc.vector.scalar_tensor_tensor(l.msg[q][:, 7, :], v[2], c0, fv[:, 1, :], ALU.mult, ALU.mult).then_inc(s["msg"], 1)
                if t.runs(0):
                    b, q = t.block(), t.slot(0, 2)
                    dve.wait_ge(s["sums"], b + 1)
                    dve.wait_ge(s["cont"], b + 1)
                    ge(dve, s["outs"], b - 1)
                    ge(dve, s["agg"], 8 * b)
                    for c in range(8):
                        nc.vector.scalar_tensor_tensor(l.agg[q][:, c, :], l.cont[q][:], l.agg[1 - q][:, c, P - 1:P],
                                                       l.ps[4 + c // 4][:, (c % 4) * P:(c % 4 + 1) * P],
                                                       ALU.mult, ALU.add).then_inc(s["agg"], 1)
            run(dve, body)


@stage
def touched(m, k, l, x2_dram, out_dram):
    nc, ET, D = m.nc, m.ET, m.D
    names = ("sc", "vec", "staged", "hcopy", "prod", "ysum", "meas", "aggr", "root", "rec", "nmr", "done", "idx2")
    s = {n: m.sem(f"tch_{n}") for n in names}
    got = [m.sem(f"tch_got{r}") for r in range(4)]
    put = [m.sem(f"tch_put{r}") for r in range(2)]
    G = [l.G[r][:] for r in range(4)]

    def run(engine, body, first=-2, last=ET - 1):
        turns(engine, body, first, last, 4, ET // 4 - 2, ET)

    with nc.Block() as block:
        @block.scalar
        def _(act):
            nc.scalar.activation(l.big[:], l.sT[:], ACT.Abs).then_inc(s["sc"], 1)
            act.wait_ge(s["sc"], 1)
            nc.scalar.activation(l.big[:], l.big[:], ACT.Exp, scale=-1.0).then_inc(s["sc"], 1)
            act.wait_ge(s["sc"], 2)
            nc.scalar.activation(l.big[:], l.big[:], ACT.Ln, bias=k.ones[:, 0:1]).then_inc(s["sc"], 1)
            act.wait_ge(s["vec"], 2)

            def body(t):
                if t.runs(1):
                    b, q = t.block(1), t.slot(1, 2)
                    ge(act, s["prod"], b - 1)
                    nc.scalar.copy(l.hb[q][:], l.sT[:, bass.ds(P * b, P)]).then_inc(s["hcopy"], 1)
                if t.runs(0):
                    b, q, r = t.block(), t.slot(0, 2), t.slot(0, 4)
                    act.wait_ge(s["aggr"], b + 1)
                    nc.scalar.activation(l.std[q][:], l.mv[q][:, 1:2], ACT.Sqrt, bias=k.eps[:, 0:1]).then_inc(s["root"], 1)
                    act.wait_ge(s["nmr"], b + 1)
                    ge(act, put[q], 16 * t.round(0, 2))
                    nc.scalar.activation(l.Y[q][:], G[r], ACT.Identity, scale=l.rstd[q][:], bias=l.nmr[q][:]).then_inc(s["done"], 1)
            run(act, body)

        @block.gpsimd
        def _(pool):
            ge(pool, s["vec"], 2)

            def body(t):
                if t.runs(2):
                    b = t.block(2)
                    ge(pool, s["staged"], b + 1)
                    ge(pool, s["done"], b - 2)
                    if t.runs(3):
                        nc.gpsimd.tensor_copy(l.idx[t.slot(3, 4)][:], l.src[:, bass.ds(b + 1, 1)]).then_inc(s["staged"], 1)
                    pool.indirect_dma_start(G[t.slot(2, 4)], None, x2_dram,
                                            bass.IndirectOffsetOnAxis(ap=l.idx[t.slot(2, 4)][:, 0:1], axis=0)
                                            ).then_inc(got[t.slot(2, 4)], 16)
                if t.runs(0):
                    b, q = t.block(), t.slot(0, 2)
                    ge(pool, s["idx2"], b + 1)
                    ge(pool, s["done"], b + 1)
                    ge(pool, put[1 - q], 16 * t.round(1, 2))
                    if t.runs(1):
                        nc.gpsimd.tensor_copy(l.idx2[1 - q][:], l.row[:, bass.ds(b + 1, 1)]).then_inc(s["idx2"], 1)
                    pool.indirect_dma_start(out_dram, bass.IndirectOffsetOnAxis(ap=l.idx2[q][:, 0:1], axis=0), l.Y[q][:], None,
                                            bounds_check=m.N - 1, oob_is_err=False).then_inc(put[q], 16)
            nc.gpsimd.tensor_copy(l.idx[0][:], l.src[:, 0:1]).then_inc(s["staged"], 1)
            nc.gpsimd.tensor_copy(l.idx2[0][:], l.row[:, 0:1]).then_inc(s["idx2"], 1)
            run(pool, body)
            for q in range(2):
                ge(pool, put[q], 16 * (ET // 2))

        @block.tensor
        def _(pe):
            def body(t):
                if t.runs(1):
                    b, q = t.block(1), t.slot(1, 2)
                    pe.wait_ge(s["hcopy"], b + 1)
                    ge(pe, s["ysum"], 2 * (b - 1))
                    nc.tensor.matmul(l.ps[q][:, 0:P], l.hb[q][:], l.W2s[:], start=True, stop=True).then_inc(s["prod"], 1)
            run(pe, body)

        @block.vector
        def _(dve):
            nc.vector.tensor_tensor(l.more[:], l.skey[:], l.next[:], ALU.is_equal).then_inc(s["vec"], 1)
            dve.wait_ge(s["vec"], 1)
            steps = Steps(dve, m.sem("tch_own"))
            steps.link(nc.vector.scalar_tensor_tensor(l.rowf[:], l.more[:], float(SKIP), l.skey[:], ALU.mult, ALU.add))
            steps.link(nc.vector.tensor_copy(l.row[:], l.rowf[:]))
            dve.wait_ge(s["sc"], 1)
            steps.link(nc.vector.tensor_scalar(l.sT[:], l.sT[:], 0.0, None, ALU.max))
            dve.wait_ge(s["sc"], 3)
            nc.vector.scalar_tensor_tensor(l.sT[:], l.big[:], -LOG2, l.sT[:], ALU.add, ALU.add).then_inc(s["vec"], 1)

            def body(t):
                if t.runs(0):
                    b, q, r = t.block(), t.slot(0, 2), t.slot(0, 4)
                    dve.wait_ge(got[r], 16 * (t.round(0, 4) + 1))
                    dve.wait_ge(s["prod"], b + 1)
                    nc.vector.tensor_tensor(G[r][:, 0:P], G[r][:, 0:P], l.ps[q][:, 0:P], ALU.add).then_inc(s["ysum"], 1)
                    nc.vector.tensor_tensor(G[r][:, P:D], G[r][:, P:D], l.V[:, bass.ds(b, 1), :].rearrange("p a f -> p (a f)"),
                                            ALU.add).then_inc(s["ysum"], 1)
                    dve.wait_ge(s["ysum"], 2 * b + 2)
                    ge(dve, s["done"], b - 1)
                    nc.vector.bn_stats(l.st[:], G[r])
                    dve.drain()
                    nc.vector.bn_aggr(l.mv[q][:], l.st[:]).then_inc(s["aggr"], 1)
                    dve.wait_ge(s["root"], b + 1)
                    nc.vector.reciprocal(l.rstd[q][:], l.std[q][:]).then_inc(s["rec"], 1)
                    dve.wait_ge(s["rec"], b + 1)
                    nc.vector.scalar_tensor_tensor(l.nmr[q][:], l.mv[q][:, 0:1], -1.0, l.rstd[q][:], ALU.mult, ALU.mult).then_inc(s["nmr"], 1)
            run(dve, body)


class Bag:
    pass


def build(nc, x, src, dst, attr20, attr3, weight, W, b, gamma, beta, net, out):
    n_nodes, d = x.shape
    n_edges, = src.shape
    n_layers = W.shape[0]
    n_rbf = attr20.shape[1]
    with ExitStack() as whole:
        m = Machine(nc, whole, n_nodes, n_edges, d)
        ET, NC, EPAD = m.ET, m.NCOL, m.EPAD
        width = 6 + n_rbf
        agg = [m.dram(f"agg{i}", [m.NPAD, d]) for i in range(2)]
        merged_dram = m.dram("merged", [EPAD, d])
        x2_dram = m.dram("x2", [m.NPAD, d])
        dinv_dram = m.dram("dinv_rows", [m.NPAD, 1])
        by_dst = m.dram("by_dst", [EPAD, 2], I32)
        by_src = m.dram("by_src", [EPAD + 1, width], I32)

        k = Bag()
        k.ident, k.ones, k.before, k.after, k.count = (m.sb(n, [P, P]) for n in ("ident", "ones", "before", "after", "count"))
        k.part, k.eps = m.sb("part", [P, 1]), m.sb("eps", [P, 1])
        constants(m, k)
        k.node = n = Bag()
        n.dinv, n.self_w, n.edge_w = (m.sb(f"node_{s}", [P, NC]) for s in ("dinv", "self_w", "edge_w"))
        n.row = m.sb("node_row", [P, NC], I32)
        n.idx = [m.sb(f"node_idx{q}", [P, 4], I32) for q in range(4)]
        bn = k.bn = Bag()
        bn.mv = m.sb("bn_mv", [P, m.C, 2])
        bn.std, bn.mean, bn.scale, bn.shift = (m.sb(f"bn_{s}", [P, m.C]) for s in ("std", "mean", "scale", "shift"))
        k.param = m.sb("param", [P, 3, n_layers * m.C])

        with ExitStack() as part:
            m.ctx = part
            w = k.sort = Bag()
            w.key, w.tmp, w.tmp2, w.place = (m.sb(f"sort_{s}", [P, ET], I32) for s in ("key", "tmp", "tmp2", "place"))
            w.keyf, w.lof, w.colf, w.rank, w.pos = (m.sb(f"sort_{s}", [P, ET]) for s in ("keyf", "lof", "colf", "rank", "pos"))
            w.hot_col, w.hot_lo = m.sb("hot_col", [P, ET, NC], BF16), m.sb("hot_lo", [P, ET, P], BF16)
            w.keyrow, w.hot_loT = m.sb("keyrow", [P, EPAD]), m.sb("hot_loT", [P, EPAD])
            w.diag = [m.sb(f"diag{q}", [P, 4, P]) for q in range(2)]
            w.cnt, w.end, w.has, w.tmpn, w.tmpn2 = (m.sb(f"sort_{s}", [P, NC]) for s in ("cnt", "end", "has", "tmpn", "tmpn2"))
            w.rowsum, w.rowsum2, w.scan = (m.sb(f"sort_{s}", [P, m.NB]) for s in ("rowsum", "rowsum2", "scan"))
            w.pre = m.sb("sort_pre", [P, 2 * m.NB])
            w.base = [m.sb(f"sort_base{q}", [P, NC]) for q in range(2)]
            w.lt = [m.sb(f"sort_lt{q}", [P, P]) for q in range(2)]
            w.junk, w.junk2 = m.sb("sort_junk", [P, P]), m.sb("sort_junk2", [P, NC])
            w.idx = [m.sb(f"sort_idx{q}", [P, 1], I32) for q in range(2)]
            w.pay = [m.sb(f"sort_pay{q}", [P, width], I32) for q in range(2)]
            payload = m.sb("payload", [P, ET, width], I32)
            w.ps_row = [m.ps(f"ps_row{q}", [P, 512]) for q in range(2)]
            w.ps_cnt = m.ps("ps_cnt", [P, 512])
            w.ps_new = [m.ps(f"ps_new{q}", [P, 512]) for q in range(2)]
            w.ps_look = [m.ps(f"ps_look{q}", [P, 512]) for q in range(2)]
            w.ps_pre = m.ps("ps_pre", [P, 512])
            load_edges(m, k, payload, (src, dst, weight, attr3, attr20), (b, gamma, beta), by_src, n_layers)
            sort_by(m, k, "dst", dst, payload, 2, by_dst, n)
            sort_by(m, k, "src", src, payload, width, by_src, None)

        with ExitStack() as part:
            m.ctx = part
            w = k.sort = Bag()
            e = k.edge = Bag()
            e.pair = m.sb("edge_pair", [P, ET, 2], I32)
            e.src = m.sb("edge_src", [P, ET], I32)
            e.skey, e.dsrc = m.sb("edge_key", [P, ET]), m.sb("edge_dsrc", [P, ET])
            e.rows = m.sb("edge_rows", [P, EPAD])
            e.tiles = m.sb("edge_tiles", [ET, 2 * P], I32)
            e.tkey, e.tjunk = m.sb("edge_tkey", [ET, P]), m.sb("edge_tjunk", [ET, P])
            e.run, e.run2 = m.sb("edge_run", [ET, 1]), m.sb("edge_run2", [ET, 1])
            e.fix_row = m.sb("edge_fix_row", [ET, 1], I32)
            e.lacks = m.sb("edge_lacks", [ET, ET])
            e.idx = [m.sb(f"edge_idx{q}", [P, 1], I32) for q in range(4)]
            e.val = [m.sb(f"edge_val{q}", [P, 1]) for q in range(2)]
            e.same = [m.sb(f"edge_same{q}", [P, P]) for q in range(2)]
            k.R = [m.sb(f"R{r}", [P, 4 * d]) for r in range(4)]
            k.Cb = [m.sb(f"Cb{r}", [P, 4 * d]) for r in range(2)]
            k.rows_out = [m.sb(f"rows_out{r}", [P, 4 * d]) for r in range(2)]
            k.scale, k.shift = m.sb("scale", [P, d]), m.sb("shift", [P, d])
            k.stat = m.sb("stat", [P, m.C, 6 * m.NB])
            k.ps_a, k.ps_b, k.ps_c = ([m.ps(f"ps_{s}{q}", [P, 512]) for q in range(2)] for s in "abc")
            w.diag = [k.rows_out[q][:, 0:4 * P].rearrange("p (a b) -> p a b", a=4) for q in range(2)]
            w.ps_row = k.ps_a
            sorted_edges(m, k, "dst", by_dst, 2, 1, e.rows, e.skey, e.pair)
            edge_tables(m, k, dinv_dram, by_dst)
            clear_gathered(m, k)
            with ExitStack() as inner:
                m.ctx = inner
                k.whi, k.wlo = m.sb("whi", [P, m.C, d], F32R), m.sb("wlo", [P, m.C, d], F32R)
                k.yhi = [m.sb(f"yhi{q}", [P, m.C, 4 * P], F32R) for q in range(2)]
                k.ylo = [m.sb(f"ylo{q}", [P, m.C, 4 * P], F32R) for q in range(2)]
                k.aggT = [m.sb(f"aggT{q}", [P, m.C, 4 * P]) for q in range(2)]
                table = x
                for layer in range(n_layers):
                    prepare(m, k, layer, W)
                    merge(m, k, layer, table, merged_dram)
                    dense(m, k, layer, table, agg[layer % 2], merged_dram)
                    table = agg[layer % 2]
                prepare(m, k, n_layers, None)
            m.ctx = part
            f = k.fin = Bag()
            f.out = [m.sb(f"fin_out{q}", [P, 4 * d]) for q in range(2)]
            f.st = m.sb("fin_st", [P, 4, 6])
            f.mv = [m.sb(f"fin_mv{q}", [P, 4, 2]) for q in range(2)]
            f.std, f.rstd, f.nmr, f.v2, f.std2, f.rstd2 = ([m.sb(f"fin_{s}{q}", [P, 4]) for q in range(2)]
                                                           for s in ("std", "rstd", "nmr", "v2", "std2", "rstd2"))
            finish_gcn(m, k, table, x, x2_dram, out)

        with ExitStack() as part:
            m.ctx = part
            l = Bag()
            w = k.sort = Bag()
            edges = m.sb("l_edges", [P, ET, width], I32)
            l.pay = edges[:].bitcast(F32)
            rows = m.sb("l_rows", [P, EPAD + 4])
            l.rows = rows
            l.skey, l.next, l.more, l.rowf = (m.sb(f"l_{s}", [P, ET]) for s in ("skey", "next", "more", "rowf"))
            l.src, l.dst, l.row, nexti = (m.sb(f"l_{s}", [P, ET], I32) for s in ("src", "dst", "row", "nexti"))
            l.Ws, l.Wv, l.W2s, l.W2v = (m.sb(f"l_{s}", [P, P]) for s in ("Ws", "Wv", "W2s", "W2v"))
            l.W1s, l.W1v, l.W1vT, l.Wvv = (m.sb(f"l_{s}", [P, 2, P]) for s in ("W1s", "W1v", "W1vT", "Wvv"))
            l.Wf1, l.Wf2 = m.sb("l_Wf1", [P, 4, P]), m.sb("l_Wf2", [P, 4 * P])
            l.bf1, l.bf2 = m.sb("l_bf1", [P, 1]), m.sb("l_bf2", [P, 4 * P])
            l.yv, l.c_v, l.c_s = (m.sb(f"l_{s}", [P, ET, 3]) for s in ("yv", "c_v", "c_s"))
            l.n2, l.norm, l.c_0 = (m.sb(f"l_{s}", [P, ET]) for s in ("n2", "norm", "c_0"))
            l.fst = [m.sb(f"l_fst{q}", [P, 4, 32]) for q in range(2)]
            l.fT = [m.sb(f"l_fT{q}", [P, P]) for q in range(2)]
            l.hT, l.big, l.sT = (m.sb(f"l_{s}", [P, EPAD]) for s in ("hT", "big", "sT"))
            l.V = m.sb("l_V", [P, ET, 3 * P])
            l.G = [m.sb(f"l_G{r}", [P, d]) for r in range(4)]
            l.idx = [m.sb(f"l_idx{r}", [P, 1], I32) for r in range(4)]
            l.idx2 = [m.sb(f"l_idx2{r}", [P, 1], I32) for r in range(2)]
            two = lambda s, shape: [m.sb(f"l_{s}{q}", shape) for q in range(2)]
            l.same, l.cont, l.u, l.hb = (two(s, [P, P]) for s in ("same", "cont", "u", "hb"))
            l.xT, l.Wb = two("xT", [P, 4, P]), two("Wb", [P, 4 * P])
            l.msg, l.agg = two("msg", [P, 8, P]), two("agg", [P, 8, P])
            l.dot = m.sb("l_dot", [P, P])
            l.st = m.sb("l_st", [P, 6])
            l.mv = two("mv", [P, 2])
            l.std, l.rstd, l.nmr = (two(s, [P, 1]) for s in ("std", "rstd", "nmr"))
            l.Y = [a[:, 0:4, :].rearrange("p a b -> p (a b)") for a in (l.msg[0], l.msg[1])]
            l.ps = [m.ps(f"l_ps{i}", [P, 512]) for i in range(7)]
            w.diag = l.xT
            w.ps_row = l.ps[0:2]
            sorted_edges(m, k, "src", by_src[0:EPAD, :], width, 0, rows[:, 4:EPAD + 4], l.skey, edges)
            edge_ends(m, l, edges, nexti, by_src)
            edge_net(m, k, l, net)
            messages(m, k, l, x2_dram)
            touched(m, k, l, x2_dram, out)


@stage
def load_edges(m, k, payload, arrays, params, by_src, n_layers):
    nc, ET = m.nc, m.ET
    filled, loaded = m.sem("pay_filled"), m.sem("pay_loaded")
    with ExitStack() as stack, nc.Block() as block:
        @block.vector
        def _(dve):
            nc.vector.memset(payload[:].bitcast(F32), 1.0).then_inc(filled, 1)
            nc.vector.memset(k.eps[:], LN_EPS).then_inc(filled, 1)
            dve.wait_ge(filled, 2)
            nc.vector.memset(payload[:, :, 0:2], m.NPAD - 1).then_inc(filled, 1)
            nc.vector.memset(k.sort.key[:], -1).then_inc(filled, 1)

        @block.sync
        def _(sp):
            stack.enter_context(nc.allow_non_contiguous_dma(reason="edge payloads and parameters, once"))
            n, at_word = 0, 0
            sp.wait_ge(filled, 4)
            for a in arrays:
                if len(a.shape) == 1:
                    a = a.rearrange("(e o) -> e o", o=1)
                wide = a.shape[1]
                to = payload[0:m.EP, :, at_word:at_word + wide]
                if a.dtype == F32:
                    to = to.bitcast(F32)
                sp.dma_start(to, a.rearrange("(p t) w -> p t w", t=ET)).then_inc(loaded, 16)
                at_word += wide
                n += 16
            for i, a in enumerate(params):
                for layer in range(n_layers):
                    sp.dma_start(k.param[:, i, layer * m.C:(layer + 1) * m.C],
                                 a[layer].rearrange("(c p) -> p c", p=P)).then_inc(loaded, 16)
                    n += 16
            sp.dma_start(by_src[m.EPAD:m.EPAD + 1, 0:2], k.sort.key[0:1, 0:2]).then_inc(loaded, 16)
            sp.wait_ge(loaded, n + 16)


@stage
def clear_gathered(m, k):
    nc, cleared = m.nc, m.sem("cleared")
    with nc.Block() as block:
        @block.vector
        def _(dve):
            for q in range(2):
                nc.vector.memset(k.Cb[q][:], 0.0).then_inc(cleared, 1)
            dve.wait_ge(cleared, 2)


@stage
def edge_ends(m, l, edges, nexti, by_src):
    nc, loaded, made = m.nc, m.sem("ends_loaded"), m.sem("ends_made")
    with nc.Block() as block:
        @block.sync
        def _(sp):
            with nc.allow_non_contiguous_dma(reason="one word of each sorted row"):
                sp.dma_start(nexti[:], by_src[1:m.EPAD + 1, :].rearrange("(t p) w -> p t w", p=P)[:, :, 0]).then_inc(loaded, 16)

        @block.vector
        def _(dve):
            nc.vector.tensor_copy(l.src[:], edges[:, :, 0]).then_inc(made, 1)
            nc.vector.tensor_copy(l.dst[:], edges[:, :, 1]).then_inc(made, 1)
            nc.vector.memset(l.rows[:, 0:4], -1.0).then_inc(made, 1)
            nc.vector.memset(l.agg[1][:], 0.0).then_inc(made, 1)
            dve.wait_ge(loaded, 16)
            nc.vector.tensor_copy(l.next[:], nexti[:]).then_inc(made, 1)
            dve.wait_ge(made, 5)


NET = ["W_in2f_s", "W_in2f_v", "Wf1", "bf1", "Wf2", "bf2", "W1_s", "W1_v", "W2_s", "W2_v"]
_INS = ["x", "src", "dst", "edge_attr_20", "edge_attr_3", "edge_weight", "L0_gnn_W", "L0_gnn_b",
        "L0_gnn_gamma", "L0_gnn_beta"] + ["L1_gnn_" + n for n in NET]


def program(nc, a, out):
    build(nc, a["x"], a["src"], a["dst"], a["edge_attr_20"], a["edge_attr_3"], a["edge_weight"],
          a["L0_gnn_W"], a["L0_gnn_b"], a["L0_gnn_gamma"], a["L0_gnn_beta"],
          {n: a["L1_gnn_" + n] for n in NET}, out)


def kernel(**inputs):
    import concourse.bacc as _bacc
    from concourse import mybir as _mybir
    from concourse.bass_utils import run_bass_kernel_spmd as _run

    nc = _bacc.Bacc("TRN2", target_bir_lowering=False, num_devices=1)
    arrays, args = {}, {}
    for name in _INS:
        a = np.ascontiguousarray(inputs[name])
        arrays[f"in_{name}"] = a
        args[name] = nc.dram_tensor(f"in_{name}", a.shape, _mybir.dt.from_np(a.dtype), kind="ExternalInput").ap()
    out = nc.dram_tensor("out_0", inputs["x"].shape, F32, kind="ExternalOutput").ap()
    program(nc, args, out)
    r = _run(nc, [arrays], core_ids=[0])
    return r.results[0]["out_0"]
```

```python
from contextlib import ExitStack

import numpy as np
import concourse.bass as bass
from concourse import mybir

F32, F32R = mybir.dt.float32, mybir.dt.float32r
BF16, I32 = mybir.dt.bfloat16, mybir.dt.int32
ALU, ACT, AX = mybir.AluOpType, mybir.ActivationFunctionType, mybir.AxisListType

P = 128
BN_EPS = LN_EPS = 1e-5
LOG2 = float(np.log(2.0))
Y0 = float(1.0 / np.sqrt(4.0 * np.pi))
Y1_SCALE = float(np.sqrt(3.0 / (4.0 * np.pi)))
SKIP = 1 << 20


class Steps:

    def __init__(self, engine, sem, base=0):
        self.engine, self.sem, self.base, self.n = engine, sem, base, 0

    def link(self, instruction):
        instruction.then_inc(self.sem, 1)
        self.n += 1
        self.engine.wait_ge(self.sem, self.base + self.n)


class Machine:

    def __init__(self, nc, ctx, n_nodes, n_edges, d):
        self.nc, self.ctx = nc, ctx
        self.N, self.E, self.D = n_nodes, n_edges, d
        self.C = d // P
        self.BLK = 4 * P
        self.NB = -(-n_nodes // self.BLK)
        self.NPAD = self.NB * self.BLK
        self.NCOL = self.NB * 4
        self.TP = (n_nodes - (self.NB - 1) * self.BLK) // 4
        self.ET = -(-n_edges // P)
        self.EPAD = self.ET * P
        self.EP = n_edges // self.ET
        assert self.EP * self.ET == n_edges and self.TP * 4 + (self.NB - 1) * self.BLK == n_nodes
        assert self.ET % 4 == 0 and self.NB % 4 == 0

    def sb(self, name, shape, dt=F32):
        return self.ctx.enter_context(self.nc.sbuf_tensor(name, shape, dt))

    def ps(self, name, shape, dt=F32):
        return self.ctx.enter_context(self.nc.psum_tensor(name, shape, dt))

    def sem(self, name):
        self.counters.append(self.nc.alloc_semaphore(name=name))
        return self.counters[-1]

    def dram(self, name, shape, dt=F32):
        return self.nc.dram_tensor(name, shape, dt).ap()


def stage(function):
    def run(m, *args):
        m.counters = []
        function(m, *args)
        m.nc.clear_and_free_semaphores(m.counters)
        m.nc.all_engine_barrier()
    return run


def block_rows(table, m):
    return table.rearrange("(b p j) f -> b p (j f)", p=P, j=4)


def at(view, i):
    if isinstance(i, int):
        return view[i]
    return view[bass.ds(i, 1)].rearrange("a p f -> (a p) f")


@stage
def constants(m, k):
    nc = m.nc
    filled, made = m.sem("const_filled"), m.sem("const_made")
    with nc.Block() as block:
        @block.gpsimd
        def _(pool):
            nc.gpsimd.memset(k.ident[:], 0.0).then_inc(filled, 1)
            nc.gpsimd.memset(k.ones[:], 1.0).then_inc(filled, 1)
            nc.gpsimd.iota(k.count[:], [[1, P]], base=0, channel_multiplier=0,
                           allow_small_or_imprecise_dtypes=True).then_inc(made, 1)
            nc.gpsimd.iota(k.part[:], [[0, 1]], base=0, channel_multiplier=1,
                           allow_small_or_imprecise_dtypes=True).then_inc(made, 1)
            ge(pool, filled, 2)
            nc.gpsimd.affine_select(out=k.ident[:], in_=k.ident[:], compare_op=ALU.not_equal, fill=1.0,
                                    base=0, pattern=[[-1, P]], channel_multiplier=1).then_inc(made, 1)
            nc.gpsimd.affine_select(out=k.before[:], in_=k.ones[:], compare_op=ALU.is_gt, fill=0.0,
                                    base=0, pattern=[[1, P]], channel_multiplier=-1).then_inc(made, 1)
            nc.gpsimd.affine_select(out=k.after[:], in_=k.ones[:], compare_op=ALU.is_gt, fill=0.0,
                                    base=0, pattern=[[-1, P]], channel_multiplier=1).then_inc(made, 1)
            ge(pool, made, 5)


@stage
def sort_by(m, k, tag, key_dram, places, table, earlier):
    nc, ET, NC = m.nc, m.ET, m.NCOL
    w = k.sort
    loaded, filled, cols, hot = (m.sem(f"{tag}_{s}") for s in ("loaded", "filled", "cols", "hot"))
    diag, row_ps, row_out = (m.sem(f"{tag}_{s}") for s in ("diag", "row_ps", "row_out"))
    counted, pre_in, pre_ps, base0 = (m.sem(f"{tag}_{s}") for s in ("counted", "pre_in", "pre_ps", "base0"))
    lt, cnt_ps, base, look_ps = (m.sem(f"{tag}_{s}") for s in ("lt", "cnt_ps", "base", "look_ps"))
    ranked, looked = m.sem(f"{tag}_ranked"), m.sem(f"{tag}_looked")
    vec, place = m.sem(f"{tag}_vec"), m.sem(f"{tag}_place")
    root_in, root = m.sem(f"{tag}_root_in"), m.sem(f"{tag}_root")
    rows4 = ET // 4
    ident4 = k.ident[:].unsqueeze(1).to_broadcast([P, 4, P])

    def spread_out(dve, n):
        q, which = divmod(n, 2)
        dve.wait_ge(row_ps, n + 1)
        span = slice(q * 4 * P, (q + 1) * 4 * P)
        if which == 0:
            nc.vector.tensor_copy(w.keyrow[:, span], w.ps_row[0][:]).then_inc(row_out, 1)
        else:
            nc.vector.tensor_scalar(w.hot_loT[:, span], w.ps_row[1][:], k.part[:, 0:1], None,
                                    ALU.is_equal).then_inc(row_out, 1)

    with nc.Block() as block:
        @block.sync
        def _(sp):
            sp.wait_ge(filled, 1)
            sp.dma_start(w.key[0:m.EP, :], key_dram.rearrange("(p t) -> p t", t=ET)).then_inc(loaded, 16)

        @block.vector
        def _(dve):
            v = Steps(dve, vec)
            nc.vector.memset(w.key[:], m.NPAD - 1).then_inc(filled, 1)
            dve.wait_ge(loaded, 16)
            v.link(nc.vector.tensor_scalar(w.tmp[:], w.key[:], 9, 2, ALU.logical_shift_right, ALU.logical_shift_left))
            v.link(nc.vector.tensor_scalar(w.tmp2[:], w.key[:], 3, None, ALU.bitwise_and))
            v.link(nc.vector.tensor_tensor(w.tmp[:], w.tmp[:], w.tmp2[:], ALU.bitwise_or))
            v.link(nc.vector.tensor_copy(w.colf[:], w.tmp[:]))
            v.link(nc.vector.tensor_scalar(w.tmp[:], w.key[:], 2, P - 1, ALU.logical_shift_right, ALU.bitwise_and))
            v.link(nc.vector.tensor_copy(w.lof[:], w.tmp[:]))
            v.link(nc.vector.tensor_copy(w.keyf[:], w.key[:]))
            nc.vector.tensor_tensor(w.hot_col[:], k.count[:, 0:NC].unsqueeze(1).to_broadcast([P, ET, NC]),
                                    w.colf[:].unsqueeze(2).to_broadcast([P, ET, NC]), ALU.is_equal).then_inc(hot, 1)
            nc.vector.tensor_tensor(w.hot_lo[:], k.count[:].unsqueeze(1).to_broadcast([P, ET, P]),
                                    w.lof[:].unsqueeze(2).to_broadcast([P, ET, P]), ALU.is_equal).then_inc(hot, 1)
            for q in range(rows4):
                for which, src in enumerate((w.keyf, w.lof)):
                    n = 2 * q + which
                    if n >= 2:
                        dve.wait_ge(row_ps, n - 1)
                    nc.vector.tensor_tensor(w.diag[n % 2][:], ident4,
                                            src[:, 4 * q:4 * q + 4].unsqueeze(2).to_broadcast([P, 4, P]),
                                            ALU.mult).then_inc(diag, 1)
                    if n >= 1:
                        spread_out(dve, n - 1)
            spread_out(dve, 2 * rows4 - 1)
            dve.wait_ge(counted, 1)
            cnt4 = w.cnt[:].rearrange("p (b j) -> p b j", j=4)
            v.link(nc.vector.tensor_copy(w.cnt[:], w.ps_cnt[:, 0:NC]))
            v.link(nc.vector.tensor_reduce(w.rowsum[:], cnt4, axis=AX.X, op=ALU.add))
            nc.vector.tensor_copy(w.rowsum2[:], w.rowsum[:]).then_inc(pre_in, 1)
            dve.wait_ge(pre_ps, 1)
            v.link(nc.vector.tensor_copy(w.pre[:], w.ps_pre[:, 0:2 * m.NB]))
            total = w.pre[:, m.NB:2 * m.NB]
            v.link(nc.vector.tensor_tensor_scan(w.scan[:], k.ones[:, 0:m.NB], total, 0.0, ALU.mult, ALU.add))
            v.link(nc.vector.tensor_tensor(w.scan[:], w.scan[:], total, ALU.subtract))
            start4 = w.base[0][:].rearrange("p (b j) -> p b j", j=4)
            v.link(nc.vector.tensor_tensor(start4[:, :, 0], w.pre[:, 0:m.NB], w.scan[:], ALU.add))
            for j in range(1, 4):
                v.link(nc.vector.tensor_tensor(start4[:, :, j], start4[:, :, j - 1], cnt4[:, :, j - 1], ALU.add))
            v.link(nc.vector.tensor_tensor(w.end[:], w.base[0][:], w.cnt[:], ALU.add))
            v.link(nc.vector.tensor_scalar(w.has[:], w.cnt[:], 0.0, None, ALU.is_gt))
            if table is not None:
                v.link(nc.vector.tensor_scalar(w.tmpn[:], w.has[:], -float(SKIP), float(SKIP) - 1.0, ALU.mult, ALU.add))
                v.link(nc.vector.tensor_tensor(w.tmpn[:], w.tmpn[:], w.end[:], ALU.add))
                nc.vector.tensor_copy(table.row[:], w.tmpn[:]).then_inc(root_in, 1)
                dve.wait_ge(root, 1)
                v.link(nc.vector.reciprocal(table.dinv[:], w.tmpn2[:]))
                for dst, a in ((table.self_w, table.dinv), (table.edge_w, w.has)):
                    v.link(nc.vector.tensor_tensor(dst[:], a[:], table.dinv[:], ALU.mult))
            nc.vector.memset(w.rank[:], 0.0).then_inc(base0, 1)
            dve.wait_ge(base0, 1)
            dve.wait_ge(hot, 2)
            dve.wait_ge(row_out, 2 * rows4)

            def body(t):
                if t.runs(0):
                    b, r = t.block(), t.slot(0, 4)
                    dve.wait_ge(cnt_ps, b + 1)
                    ge(dve, base, b)
                    ge(dve, look_ps, b - 2)
                    nc.vector.tensor_tensor(w.base[t.slot(1, 4)][:], w.base[r][:], w.ps_new[r % 2][:, 0:NC],
                                            ALU.add).then_inc(base, 1)
                    ge(dve, ranked, b)
                    nc.vector.scalar_tensor_tensor(w.junk[:], w.keyrow[:, bass.ds(b * P, P)], w.keyf[:, bass.ds(b, 1)],
                                                   k.after[:], ALU.is_equal, ALU.mult,
                                                   accum_out=w.rank[:, bass.ds(b, 1)]).then_inc(ranked, 1)
                if t.runs(-1):
                    b, r = t.block(-1), t.slot(-1, 4)
                    dve.wait_ge(look_ps, b + 1)
                    ge(dve, looked, b)
                    nc.vector.scalar_tensor_tensor(w.junk2[:], w.ps_look[r % 2][:, 0:NC], 1.0,
                                                   w.hot_col[:, bass.ds(b, 1), :].rearrange("p a c -> p (a c)"),
                                                   ALU.mult, ALU.mult, accum_out=w.pos[:, bass.ds(b, 1)]).then_inc(looked, 1)
            turns(dve, body, 0, ET, 4, ET // 4 - 2, ET)
            dve.wait_ge(looked, ET)
            dve.wait_ge(ranked, ET)
            v.link(nc.vector.tensor_tensor(w.pos[:], w.pos[:], w.rank[:], ALU.add))
            nc.vector.tensor_copy(places[:], w.pos[:]).then_inc(place, 1)
            dve.wait_ge(place, 1)

        @block.tensor
        def _(pe):
            def count(out, t, start, stop):
                return nc.tensor.matmul(out, w.hot_lo[:, bass.ds(t, 1), :].rearrange("p a c -> p (a c)"),
                                        w.hot_col[:, bass.ds(t, 1), :].rearrange("p a c -> p (a c)"),
                                        start=start, stop=stop)
            pe.wait_ge(hot, 2)
            for n in range(2 * rows4):
                pe.wait_ge(diag, n + 1)
                if n >= 2:
                    pe.wait_ge(row_out, n - 1)
                nc.tensor.matmul(w.ps_row[n % 2][:], k.ones[:], w.diag[n % 2][:].rearrange("p a b -> p (a b)"),
                                 start=True, stop=True).then_inc(row_ps, 1)
                for t in (2 * n, 2 * n + 1):
                    c = count(w.ps_cnt[:, 0:NC], t, t == 0, t == ET - 1)
            c.then_inc(counted, 1)
            pe.wait_ge(pre_in, 1)
            nc.tensor.matmul(w.ps_pre[:, 0:m.NB], k.before[:], w.rowsum2[:], start=True, stop=True)
            nc.tensor.matmul(w.ps_pre[:, m.NB:2 * m.NB], k.ones[:], w.rowsum2[:], start=True, stop=True).then_inc(pre_ps, 1)

            def body(t):
                if t.runs(1):
                    b, q = t.block(1), t.slot(1, 2)
                    ge(pe, base, b - 1)
                    count(w.ps_new[q][:, 0:NC], b, True, True).then_inc(cnt_ps, 1)
                if t.runs(0):
                    b, r = t.block(), t.slot(0, 4)
                    pe.wait_ge(lt, b + 1)
                    ge(pe, base, b)
                    ge(pe, looked, b - 1)
                    nc.tensor.matmul(w.ps_look[r % 2][:, 0:NC], w.lt[r][:], w.base[r][:], start=True, stop=True).then_inc(look_ps, 1)
            pe.wait_ge(base0, 1)
            turns(pe, body, -1, ET - 1, 4, ET // 4 - 2, ET)

        @block.scalar
        def _(act):
            if table is not None:
                act.wait_ge(root_in, 1)
                nc.scalar.activation(w.tmpn2[:], w.cnt[:], ACT.Sqrt, bias=k.ones[:, 0:1]).then_inc(root, 1)
            act.wait_ge(row_out, 2 * rows4)

            def body(t):
                b, r = t.block(), t.slot(0, 4)
                ge(act, look_ps, b - 3)
                nc.scalar.copy(w.lt[r][:], w.hot_loT[:, bass.ds(b * P, P)]).then_inc(lt, 1)
            turns(act, body, 0, ET - 1, 4, ET // 4 - 2, ET)

        @block.gpsimd
        def _(pool):
            if earlier is not None:
                def body(t):
                    earlier.step(pool, t.block(), t.slot(0, 4), t.slot(1, 4), t.round(1, 4), t.runs(1))
                earlier.begin(m, pool)
                turns(pool, body, 0, ET - 1, 4, ET // 4 - 2, ET)
                earlier.finish(pool)


class Scatter:

    def __init__(self, m, tag, payload, width, place, bufs, sorted_dram):
        self.m, self.tag, self.payload, self.width, self.place, self.dram = m, tag, payload, width, place, sorted_dram
        self.idx, self.rows = bufs

    def begin(self, m, pool):
        self.staged = m.sem(f"{self.tag}_staged")
        self.sent = [m.sem(f"{self.tag}_sent{r}") for r in range(4)]
        self.fill(0, 0)

    def fill(self, t, r):
        nc = self.m.nc
        nc.gpsimd.tensor_copy(self.idx[r][:], self.place[:, bass.ds(t, 1)]).then_inc(self.staged, 1)
        nc.gpsimd.tensor_copy(self.rows[r][:, 0:self.width],
                              self.payload[:, bass.ds(t, 1), 0:self.width].rearrange("p a w -> p (a w)")).then_inc(self.staged, 1)

    def step(self, pool, t, r, r_next, uses, more):
        ge(pool, self.staged, 2 * (t + 1))
        if more:
            ge(pool, self.sent[r_next], 16 * uses)
            self.fill(t + 1, r_next)
        pool.indirect_dma_start(self.dram, bass.IndirectOffsetOnAxis(ap=self.idx[r][:, 0:1], axis=0),
                                self.rows[r][:, 0:self.width], None).then_inc(self.sent[r], 16)

    def finish(self, pool):
        for r in range(4):
            ge(pool, self.sent[r], 16 * (self.m.ET // 4))


class Turn:

    def __init__(self, group, s, last):
        self.group, self.s, self.last = group, s, last

    def block(self, off=0):
        return self.group * 4 + (self.s + off)

    def slot(self, off, ring):
        return (self.s + off) % ring

    def round(self, off, ring):
        return self.group * (4 // ring) + (self.s + off) // ring

    def runs(self, off):
        return not isinstance(self.group, int) or 0 <= self.block(off) <= self.last


def turns(engine, body, first, last, loop_from, loop_groups, blocks):
    for b in range(first, loop_from):
        body(Turn(0, b, blocks - 1))
    with engine.Fori(0, loop_groups) as g:
        for u in range(4):
            body(Turn(g, loop_from + u, blocks - 1))
    for b in range(loop_from + 4 * loop_groups, last + 1):
        body(Turn(0, b, blocks - 1))


def ge(engine, sem, value):
    if not isinstance(value, int) or value > 0:
        engine.wait_ge(sem, value)


@stage
def sorted_edges(m, k, tag, sorted_dram, width, key_word, rows, skey, sbuf):
    nc, ET = m.nc, m.ET
    loaded, vec, diag, out_ps, out = (m.sem(f"{tag}_{s}") for s in ("re_loaded", "re_vec", "re_diag", "re_ps", "re_out"))
    ident4 = k.ident[:].unsqueeze(1).to_broadcast([P, 4, P])
    w = k.sort
    with nc.Block() as block:
        @block.sync
        def _(sp):
            sp.dma_start(sbuf[:, :, 0:width], sorted_dram.rearrange("(t p) w -> p t w", p=P)).then_inc(loaded, 16)

        @block.vector
        def _(dve):
            v = Steps(dve, vec)
            dve.wait_ge(loaded, 16)
            v.link(nc.vector.tensor_copy(skey[:], sbuf[:, :, key_word]))
            for q in range(ET // 4):
                ge(dve, out_ps, q - 1)
                nc.vector.tensor_tensor(w.diag[q % 2][:], ident4,
                                        skey[:, 4 * q:4 * q + 4].unsqueeze(2).to_broadcast([P, 4, P]),
                                        ALU.mult).then_inc(diag, 1)

        @block.tensor
        def _(pe):
            for q in range(ET // 4):
                pe.wait_ge(diag, q + 1)
                ge(pe, out, q - 1)
                nc.tensor.matmul(w.ps_row[q % 2][:], k.ones[:], w.diag[q % 2][:].rearrange("p a b -> p (a b)"),
                                 start=True, stop=True).then_inc(out_ps, 1)

        @block.scalar
        def _(act):
            for q in range(ET // 4):
                act.wait_ge(out_ps, q + 1)
                nc.scalar.copy(rows[:, q * 4 * P:(q + 1) * 4 * P], w.ps_row[q % 2][:]).then_inc(out, 1)
            act.wait_ge(out, ET // 4)


@stage
def edge_tables(m, k, dinv_dram, sorted_dram):
    nc, ET = m.nc, m.ET
    e = k.edge
    stored, loaded, staged, vec = (m.sem(f"edge_{s}") for s in ("stored", "loaded", "staged", "vec"))
    got = [m.sem(f"edge_got{q}") for q in range(4)]
    kept, srcs = m.sem("edge_kept"), m.sem("edge_srcs")
    with nc.Block() as block:
        @block.sync
        def _(sp):
            sp.dma_start(dinv_dram.rearrange("(b p j) o -> p b (j o)", p=P, j=4),
                         k.node.dinv[:].rearrange("p (b j) -> p b j", j=4)).then_inc(stored, 16)
            sp.dma_start(e.tiles[:], sorted_dram.rearrange("(t p) w -> t (p w)", p=P)).then_inc(loaded, 16)
            sp.wait_ge(stored, 16)

        @block.gpsimd
        def _(pool):
            nc.gpsimd.tensor_scalar(e.src[:], e.pair[:, :, 0], m.N - 1, None, ALU.min).then_inc(srcs, 1)
            ge(pool, srcs, 1)
            ge(pool, stored, 16)

            def body(t):
                b, r = t.block(), t.slot(0, 4)
                ge(pool, staged, b + 1)
                ge(pool, kept, b - 2)
                if t.runs(1):
                    nc.gpsimd.tensor_copy(e.idx[t.slot(1, 4)][:], e.src[:, bass.ds(b + 1, 1)]).then_inc(staged, 1)
                pool.indirect_dma_start(e.val[r][:], None, dinv_dram,
                                        bass.IndirectOffsetOnAxis(ap=e.idx[r][:, 0:1], axis=0)).then_inc(got[r], 16)
            nc.gpsimd.tensor_copy(e.idx[0][:], e.src[:, 0:1]).then_inc(staged, 1)
            turns(pool, body, 0, ET - 1, 4, ET // 4 - 2, ET)

        @block.vector
        def _(dve):
            v = Steps(dve, vec)
            dve.wait_ge(loaded, 16)
            keys = e.tiles[:].rearrange("t (p w) -> t p w", w=2)[:, :, 1]
            v.link(nc.vector.tensor_copy(e.tkey[:], keys))
            v.link(nc.vector.tensor_scalar(e.tjunk[:], e.tkey[:], e.tkey[:, 0:1], 0.0, ALU.is_equal, ALU.add,
                                           accum_out=e.run[:]))
            v.link(nc.vector.tensor_scalar(e.run2[:], k.part[0:ET, 0:1], float(P), -1.0, ALU.mult, ALU.add))
            v.link(nc.vector.tensor_tensor(e.run2[:], e.run2[:], e.run[:], ALU.add))
            v.link(nc.vector.tensor_copy(e.fix_row[:], e.run2[:]))
            firsts = e.rows[0:ET, :].rearrange("q (t p) -> q t p", p=P)[:, :, 0]
            v.link(nc.vector.tensor_scalar(e.lacks[:], firsts, e.tkey[:, P - 1:P], None, ALU.is_equal))
            v.link(nc.vector.tensor_tensor(e.lacks[:], e.lacks[:], k.before[0:ET, 0:ET], ALU.mult))

            def keep(t):
                dve.wait_ge(got[t.slot(0, 4)], 16 * (t.round(0, 4) + 1))
                nc.vector.tensor_copy(e.dsrc[:, bass.ds(t.block(), 1)], e.val[t.slot(0, 4)][:]).then_inc(kept, 1)
            turns(dve, keep, 0, ET - 1, 4, ET // 4 - 2, ET)
            dve.wait_ge(kept, ET)


@stage
def prepare(m, k, layer, w_dram):
    nc, C, tag = m.nc, m.C, f"prep{layer}"
    loaded, tps, hi, lo = (m.sem(f"{tag}_{s}") for s in ("loaded", "tps", "hi", "lo"))
    vec, var, root, diag, spread, out = (m.sem(f"{tag}_{s}") for s in ("vec", "var", "root", "diag", "spread", "out"))
    raw = k.R[0][:].rearrange("p (c f) -> p c f", c=C)
    stats, weights = layer > 0, w_dram is not None
    s = k.bn
    with nc.Block() as block:
        @block.sync
        def _(sp):
            if weights:
                sp.dma_start(raw, w_dram[layer].rearrange("(c p) f -> p c f", p=P)).then_inc(loaded, 16)

        @block.tensor
        def _(pe):
            if weights:
                pe.wait_ge(loaded, 16)
                for q in range(C):
                    ge(pe, lo, q - 1)
                    for c in range(C):
                        t = nc.tensor.transpose(k.ps_a[q % 2][:, c * P:(c + 1) * P], raw[:, c, q * P:(q + 1) * P], k.ident[:])
                    t.then_inc(tps, 1)
            if stats:
                for i in range(2):
                    pe.wait_ge(diag, i + 1)
                    nc.tensor.matmul(k.ps_b[i][:], k.ones[:], k.R[1 + i][:, 0:m.D], start=True, stop=True).then_inc(spread, 1)

        @block.scalar
        def _(act):
            if stats:
                act.wait_ge(var, 1)
                nc.scalar.activation(s.std[:], s.mv[:, :, 1], ACT.Sqrt, bias=k.eps[:, 0:1]).then_inc(root, 1)
            if weights:
                for q in range(C):
                    act.wait_ge(tps, q + 1)
                    nc.scalar.copy(k.whi[:, q, :], k.ps_a[q % 2][:]).then_inc(hi, 1)
            if stats:
                for i, dst in enumerate((k.scale, k.shift)):
                    act.wait_ge(spread, i + 1)
                    nc.scalar.copy(dst[:], k.ps_b[i][:]).then_inc(out, 1)
                act.wait_ge(out, 2)

        @block.vector
        def _(dve):
            v = Steps(dve, vec)
            if stats:
                prm = k.param[:, :, (layer - 1) * C:layer * C]
                for c in range(C):
                    last = nc.vector.bn_aggr(s.mv[:, c, :], k.stat[:, c, :])
                    last.then_inc(var if c == C - 1 else vec, 1)
                v.n = C - 1
                dve.wait_ge(vec, C - 1)
                dve.wait_ge(var, 1)
                v.link(nc.vector.tensor_tensor(s.mean[:], s.mv[:, :, 0], prm[:, 0, :], ALU.add))
                v.link(nc.vector.tensor_tensor(s.mean[:], prm[:, 0, :], s.mean[:], ALU.subtract))
                dve.wait_ge(root, 1)
                v.link(nc.vector.reciprocal(s.scale[:], s.std[:]))
                v.link(nc.vector.tensor_tensor(s.scale[:], s.scale[:], prm[:, 1, :], ALU.mult))
                v.link(nc.vector.tensor_tensor(s.shift[:], s.scale[:], s.mean[:], ALU.mult))
                v.link(nc.vector.tensor_tensor(s.shift[:], s.shift[:], prm[:, 2, :], ALU.add))
                for i, col in enumerate((s.scale, s.shift)):
                    nc.vector.tensor_tensor(k.R[1 + i][:, 0:m.D].rearrange("p (c f) -> p c f", c=C),
                                            k.ident[:].unsqueeze(1).to_broadcast([P, C, P]),
                                            col[:].unsqueeze(2).to_broadcast([P, C, P]), ALU.mult).then_inc(diag, 1)
            if weights:
                for q in range(C):
                    dve.wait_ge(hi, q + 1)
                    nc.vector.tensor_tensor(k.wlo[:, q, :], k.ps_a[q % 2][:], k.whi[:, q, :].bitcast(F32),
                                            ALU.subtract).then_inc(lo, 1)
                dve.wait_ge(lo, C)


@stage
def merge(m, k, layer, table, merged_dram):
    nc, ET, D, tag = m.nc, m.ET, m.D, f"merge{layer}"
    e, norm = k.edge, layer > 0
    staged, scaled, shifted, weighted, sel = (m.sem(f"{tag}_{s}") for s in ("staged", "scaled", "shifted", "weighted", "sel"))
    merged, copied = m.sem(f"{tag}_merged"), m.sem(f"{tag}_copied")
    got = [m.sem(f"{tag}_got{r}") for r in range(4)]
    put = [m.sem(f"{tag}_put{r}") for r in range(4)]
    lasts, lacking, fix_ps, fixed, sent = (m.sem(f"{tag}_{s}") for s in ("lasts", "lacking", "fix_ps", "fixed", "sent"))
    m_rows = merged_dram.rearrange("(t p) f -> t p f", p=P)
    G = [k.R[r][:, 0:D] for r in range(4)]
    O = [k.rows_out[r // 2][:, (r % 2) * D:(r % 2 + 1) * D] for r in range(4)]
    last_rows, fix = k.Cb[0][0:ET, 0:D], k.Cb[1][0:ET, 0:D]
    group = ET // 4

    def run(engine, body, extra=0):
        turns(engine, body, 0, ET - 1 + extra, 4, group - 2, ET)

    with nc.Block() as block:
        @block.gpsimd
        def _(pool):
            def body(t):
                b, r = t.block(), t.slot(0, 4)
                ge(pool, staged, b + 1)
                ge(pool, merged, b - 2)
                if t.runs(1):
                    nc.gpsimd.tensor_copy(e.idx[t.slot(1, 4)][:], e.src[:, bass.ds(t.block(1), 1)]).then_inc(staged, 1)
                pool.indirect_dma_start(G[r], None, table,
                                        bass.IndirectOffsetOnAxis(ap=e.idx[r][:, 0:1], axis=0)).then_inc(got[r], 16)
            nc.gpsimd.tensor_copy(e.idx[0][:], e.src[:, 0:1]).then_inc(staged, 1)
            run(pool, body)
            ge(pool, lacking, 16)
            pool.indirect_dma_start(fix, None, merged_dram,
                                    bass.IndirectOffsetOnAxis(ap=e.fix_row[:, 0:1], axis=0)).then_inc(lasts, 16)
            ge(pool, fixed, 1)
            pool.indirect_dma_start(merged_dram, bass.IndirectOffsetOnAxis(ap=e.fix_row[:, 0:1], axis=0),
                                    fix, None).then_inc(sent, 16)
            ge(pool, sent, 16)

        @block.vector
        def _(dve):
            def body(t):
                b, r = t.block(), t.slot(0, 4)
                if norm:
                    dve.wait_ge(got[r], 16 * (t.round(0, 4) + 1))
                    nc.vector.tensor_tensor(G[r], G[r], k.scale[:], ALU.mult).then_inc(scaled, 1)
                ge(dve, merged, b - 1)
                nc.vector.tensor_scalar(e.same[r % 2][:], e.rows[:, bass.ds(b * P, P)], e.skey[:, bass.ds(b, 1)],
                                        None, ALU.is_equal).then_inc(sel, 1)
                if norm:
                    dve.wait_ge(scaled, b + 1)
                    nc.vector.tensor_tensor(G[r], G[r], k.shift[:], ALU.add).then_inc(shifted, 1)
            run(dve, body)
            dve.wait_ge(fix_ps, 1)
            dve.wait_ge(lasts, 16)
            nc.vector.tensor_tensor(fix, fix, k.ps_b[0][0:ET, :], ALU.add).then_inc(fixed, 1)

        @block.scalar
        def _(act):
            def body(t):
                if t.runs(0):
                    b, r = t.block(), t.slot(0, 4)
                    if norm:
                        act.wait_ge(shifted, b + 1)
                    else:
                        act.wait_ge(got[r], 16 * (t.round(0, 4) + 1))
                    nc.scalar.activation(G[r], G[r], ACT.Relu if norm else ACT.Copy,
                                         scale=e.dsrc[:, bass.ds(b, 1)]).then_inc(weighted, 1)
                if t.runs(-1):
                    b, r = t.block(-1), t.slot(-1, 4)
                    act.wait_ge(merged, b + 1)
                    ge(act, put[r], 16 * t.round(-1, 4))
                    nc.scalar.copy(O[r], k.ps_a[r % 2][:]).then_inc(copied, 1)
            run(act, body, 1)

        @block.tensor
        def _(pe):
            def body(t):
                b, r = t.block(), t.slot(0, 4)
                pe.wait_ge(weighted, b + 1)
                pe.wait_ge(sel, b + 1)
                ge(pe, copied, b - 1)
                nc.tensor.matmul(k.ps_a[r % 2][:], e.same[r % 2][:], G[r], start=True, stop=True).then_inc(merged, 1)
            run(pe, body)
            pe.wait_ge(lacking, 16)
            nc.tensor.matmul(k.ps_b[0][0:ET, :], e.lacks[:], last_rows, start=True, stop=True).then_inc(fix_ps, 1)

        @block.sync
        def _(sp):
            def body(t):
                b, r = t.block(), t.slot(0, 4)
                sp.wait_ge(copied, b + 1)
                sp.dma_start(at(m_rows, b), O[r]).then_inc(put[r], 16)
            run(sp, body)
            for r in range(4):
                sp.wait_ge(put[r], 16 * group)
            sp.dma_start(last_rows, m_rows[:, P - 1, :]).then_inc(lacking, 16)
            sp.wait_ge(lacking, 16)


@stage
def dense(m, k, layer, table, out_table, merged_dram):
    nc, C, D, NB, tag = m.nc, m.C, m.D, m.NB, f"dense{layer}"
    norm = layer > 0
    n = k.node
    scaled, shifted, weighted, joined = (m.sem(f"{tag}_{s}") for s in ("scaled", "shifted", "weighted", "joined"))
    turned, hi, lo, product = (m.sem(f"{tag}_{s}") for s in ("turned", "hi", "lo", "product"))
    copied, counted, back, rows = (m.sem(f"{tag}_{s}") for s in ("copied", "counted", "back", "rows"))
    staged = m.sem(f"{tag}_staged")
    read = [m.sem(f"{tag}_read{r}") for r in range(4)]
    got = [m.sem(f"{tag}_got{r}") for r in range(2)]
    put = [m.sem(f"{tag}_put{r}") for r in range(2)]
    src = block_rows(table[0:(NB - 1) * m.BLK, :], m) if layer == 0 else block_rows(table, m)
    dst = block_rows(out_table, m)
    quarter = [slice(j * D, (j + 1) * D) for j in range(4)]

    def run(engine, body):
        turns(engine, body, -4, NB, 4, (NB - 8) // 4, NB)

    with nc.Block() as block:
        @block.sync
        def _(sp):
            def body(t):
                if t.runs(4):
                    r = t.slot(4, 4)
                    ge(sp, turned, 4 * (t.block() + 1))
                    if layer == 0 and isinstance(t.group, int) and t.block(4) == NB - 1:
                        sp.dma_start(k.R[r][0:m.TP, :], table[(NB - 1) * m.BLK:m.N, :]
                                     .rearrange("(p j) f -> p (j f)", j=4)).then_inc(read[r], 16)
                    else:
                        sp.dma_start(k.R[r][:], at(src, t.block(4))).then_inc(read[r], 16)
                if t.runs(-1):
                    q = t.slot(-1, 2)
                    sp.wait_ge(rows, 4 * (t.block(-1) + 1))
                    sp.dma_start(at(dst, t.block(-1)), k.rows_out[q][:]).then_inc(put[q], 16)
            turns(sp, body, -4, NB, 4, (NB - 12) // 4, NB)
            for q in range(2):
                sp.wait_ge(put[q], 16 * (NB // 2))

        @block.gpsimd
        def _(pool):
            def body(t):
                if not t.runs(3):
                    return
                b, q = t.block(3), t.slot(3, 2)
                ge(pool, staged, b + 1)
                ge(pool, joined, 4 * (b - 1))
                if t.runs(4):
                    nc.gpsimd.tensor_copy(n.idx[t.slot(4, 4)][:], n.row[:, bass.ds(4 * (b + 1), 4)]).then_inc(staged, 1)
                for j in range(4):
                    pool.indirect_dma_start(k.Cb[q][:, quarter[j]], None, merged_dram,
                                            bass.IndirectOffsetOnAxis(ap=n.idx[t.slot(3, 4)][:, j:j + 1], axis=0),
                                            bounds_check=m.EPAD - 1, oob_is_err=False).then_inc(got[q], 16)
                if norm:
                    r = t.slot(3, 4)
                    for j in range(4):
                        ge(pool, scaled, 4 * b + j + 1)
                        nc.gpsimd.tensor_tensor(k.R[r][:, quarter[j]], k.R[r][:, quarter[j]], k.shift[:],
                                                ALU.add).then_inc(shifted, 1)
            nc.gpsimd.tensor_copy(n.idx[0][:], n.row[:, 0:4]).then_inc(staged, 1)
            run(pool, body)

        @block.vector
        def _(dve):
            def body(t):
                for j in range(4):
                    if t.runs(1):
                        b, q = t.block(1), t.slot(1, 2)
                        dve.wait_ge(hi, 4 * b + j + 1)
                        nc.vector.tensor_tensor(k.ylo[q][:, :, j * P:(j + 1) * P],
                                                k.ps_a[j % 2][:].rearrange("p (c n) -> p c n", c=C),
                                                k.yhi[q][:, :, j * P:(j + 1) * P].bitcast(F32),
                                                ALU.subtract).then_inc(lo, 1)
                    if norm and t.runs(3):
                        r = t.slot(3, 4)
                        if j == 0:
                            dve.wait_ge(read[r], 16 * (t.round(3, 4) + 1))
                        nc.vector.tensor_tensor(k.R[r][:, quarter[j]], k.R[r][:, quarter[j]], k.scale[:],
                                                ALU.mult).then_inc(scaled, 1)
                    if t.runs(2):
                        b, r, q = t.block(2), t.slot(2, 4), t.slot(2, 2)
                        if j == 0:
                            dve.wait_ge(got[q], 64 * (t.round(2, 2) + 1))
                        dve.wait_ge(weighted, 4 * b + j + 1)
                        nc.vector.scalar_tensor_tensor(k.R[r][:, quarter[j]], k.Cb[q][:, quarter[j]],
                                                       n.edge_w[:, bass.ds(4 * b + j, 1)], k.R[r][:, quarter[j]],
                                                       ALU.mult, ALU.add).then_inc(joined, 1)
                    if t.runs(0):
                        b = t.block()
                        dve.wait_ge(copied, 4 * b + j + 1)
                        view = k.aggT[t.slot(0, 2)][:, j, :]
                        if isinstance(t.group, int) and b == NB - 1:
                            view = view.rearrange("p (j n) -> p j n", j=4)[:, :, 0:m.TP]
                        nc.vector.bn_stats(k.stat[:, j, bass.ds(6 * b, 6)], view).then_inc(counted, 1)
            run(dve, body)
            dve.wait_ge(counted, 4 * NB)

        @block.scalar
        def _(act):
            def body(t):
                for j in range(4):
                    if t.runs(1):
                        b, q = t.block(1), t.slot(1, 2)
                        act.wait_ge(turned, 4 * b + j + 1)
                        ge(act, product, 4 * (b - 1))
                        nc.scalar.copy(k.yhi[q][:, :, j * P:(j + 1) * P],
                                       k.ps_a[j % 2][:].rearrange("p (c n) -> p c n", c=C)).then_inc(hi, 1)
                    if t.runs(2):
                        b, r = t.block(2), t.slot(2, 4)
                        if norm:
                            act.wait_ge(shifted, 4 * b + j + 1)
                        else:
                            act.wait_ge(read[r], 16 * (t.round(2, 4) + 1))
                        nc.scalar.activation(k.R[r][:, quarter[j]], k.R[r][:, quarter[j]],
                                             ACT.Relu if norm else ACT.Copy,
                                             scale=n.self_w[:, bass.ds(4 * b + j, 1)]).then_inc(weighted, 1)
                    if t.runs(0):
                        b, q = t.block(), t.slot(0, 2)
                        act.wait_ge(product, 4 * b + j + 1)
                        ge(act, back, 4 * (b - 1))
                        ge(act, counted, 4 * (b - 1))
                        nc.scalar.copy(k.aggT[q][:, j, :], k.ps_b[j % 2][:]).then_inc(copied, 1)
                    if t.runs(-1):
                        b, q = t.block(-1), t.slot(-1, 2)
                        act.wait_ge(back, 4 * b + j + 1)
                        ge(act, put[q], 16 * t.round(-1, 2))
                        nc.scalar.copy(k.rows_out[q][:, quarter[j]], k.ps_c[j % 2][:]).then_inc(rows, 1)
            run(act, body)

        @block.tensor
        def _(pe):
            def body(t):
                for j in range(4):
                    if t.runs(1):
                        b, r = t.block(1), t.slot(1, 4)
                        pe.wait_ge(joined, 4 * b + j + 1)
                        ge(pe, lo, 4 * b + j - 1)
                        for c in range(C):
                            i = nc.tensor.transpose(k.ps_a[j % 2][:, c * P:(c + 1) * P],
                                                    k.R[r][:, j * D + c * P:j * D + (c + 1) * P], k.ident[:])
                        i.then_inc(turned, 1)
                    if t.runs(0):
                        b, q = t.block(), t.slot(0, 2)
                        if j == 0:
                            pe.wait_ge(lo, 4 * (b + 1))
                        ge(pe, copied, 4 * b + j - 1)
                        parts = [(k.whi, k.yhi[q]), (k.whi, k.ylo[q]), (k.wlo, k.yhi[q])]
                        for c in range(C):
                            for i, (wt, y) in enumerate(parts):
                                mm = nc.tensor.matmul(k.ps_b[j % 2][:], wt[:, c, j * P:(j + 1) * P], y[:, c, :],
                                                      start=(c == 0 and i == 0), stop=(c == C - 1 and i == 2))
                        mm.then_inc(product, 1)
                    if t.runs(-1):
                        b, q = t.block(-1), t.slot(-1, 2)
                        if j == 0:
                            pe.wait_ge(copied, 4 * (b + 1))
                        ge(pe, rows, 4 * b + max(j - 1, 0))
                        for c in range(C):
                            i = nc.tensor.transpose(k.ps_c[j % 2][:, c * P:(c + 1) * P],
                                                    k.aggT[q][:, c, j * P:(j + 1) * P], k.ident[:])
                        i.then_inc(back, 1)
            run(pe, body)


@stage
def finish_gcn(m, k, table, x_dram, x2_dram, out_dram, rows_by_src):
    nc, D, NB, ET = m.nc, m.D, m.NB, m.ET
    f = k.fin
    tag = "fin"
    scaled, shifted, relued, summed = (m.sem(f"{tag}_{s}") for s in ("scaled", "shifted", "relued", "summed"))
    moments, root1, small, var2, root2, ready = (m.sem(f"{tag}_{s}") for s in ("moments", "root1", "small", "var2", "root2", "ready"))
    normed, outed = m.sem(f"{tag}_normed"), m.sem(f"{tag}_outed")
    read = [m.sem(f"{tag}_read{r}") for r in range(4)]
    xread = [m.sem(f"{tag}_xread{r}") for r in range(2)]
    put = [m.sem(f"{tag}_put{r}") for r in range(2)]
    src, x2 = block_rows(table, m), block_rows(x2_dram, m)
    full = (NB - 1) * m.BLK
    x_full, out_full = block_rows(x_dram[0:full, :], m), block_rows(out_dram[0:full, :], m)
    x_tail, out_tail = (a[full:m.N, :].rearrange("(p j) f -> p (j f)", j=4) for a in (x_dram, out_dram))
    quarter = [slice(j * D, (j + 1) * D) for j in range(4)]

    def tail(t, off):
        return isinstance(t.group, int) and t.block(off) == NB - 1

    def run(engine, body):
        turns(engine, body, -4, NB - 1, 4, (NB - 8) // 4, NB)

    assert ET == 2 * NB

    with nc.Block() as block:
        @block.sync
        def _(sp):
            def body(t):
                if t.runs(2):
                    q = t.slot(2, 2)
                    ge(sp, summed, 4 * (t.block(2) - 1))
                    if tail(t, 2):
                        sp.dma_start(k.Cb[q][0:m.TP, :], x_tail).then_inc(xread[q], 16)
                    else:
                        sp.dma_start(k.Cb[q][:], at(x_full, t.block(2))).then_inc(xread[q], 16)
                if t.runs(0):
                    q = t.slot(0, 2)
                    sp.wait_ge(normed, 4 * (t.block() + 1))
                    sp.dma_start(at(x2, t.block()), k.rows_out[q][:]).then_inc(put[q], 16)
                if t.runs(4):
                    sp.dma_start(k.R[t.slot(4, 4)][:], at(src, t.block(4))).then_inc(read[t.slot(4, 4)], 16)
                if t.runs(0):
                    sp.wait_ge(outed, 4 * (t.block() + 1))
                    if tail(t, 0):
                        sp.dma_start(out_tail, f.out[q][0:m.TP, :]).then_inc(put[q], 16)
                    else:
                        sp.dma_start(at(out_full, t.block()), f.out[q][:]).then_inc(put[q], 16)
            run(sp, body)
            for q in range(2):
                sp.wait_ge(put[q], 32 * (NB // 2))

        @block.gpsimd
        def _(pool):
            def body(t):
                if t.runs(3):
                    r = t.slot(3, 4)
                    for j in range(4):
                        ge(pool, scaled, 4 * t.block(3) + j + 1)
                        nc.gpsimd.tensor_tensor(k.R[r][:, quarter[j]], k.R[r][:, quarter[j]], k.shift[:],
                                                ALU.add).then_inc(shifted, 1)
                if t.runs(0):
                    for h in range(2):
                        last = isinstance(t.group, int) and t.block() == NB - 1 and h == 1
                        rows_by_src.step(pool, 2 * t.block() + h, (2 * t.s + h) % 4, (2 * t.s + h + 1) % 4,
                                         2 * t.group + (2 * t.s + h + 1) // 4, not last)
            rows_by_src.begin(m, pool)
            run(pool, body)
            rows_by_src.finish(pool)

        @block.vector
        def _(dve):
            def body(t):
                if t.runs(1):
                    b, q = t.block(1), t.slot(1, 2)
                    dve.wait_ge(root1, b + 1)
                    ge(dve, normed, 4 * (b - 1))
                    ge(dve, outed, 4 * (b - 1))
                    nc.vector.reciprocal(f.rstd[q][:], f.std[q][:]).then_inc(small, 1)
                    dve.wait_ge(small, 3 * b + 1)
                    nc.vector.scalar_tensor_tensor(f.nmr[q][:], f.mv[q][:, :, 0], -1.0, f.rstd[q][:],
                                                   ALU.mult, ALU.mult).then_inc(small, 1)
                    nc.vector.tensor_tensor(f.v2[q][:], f.mv[q][:, :, 1], f.rstd[q][:], ALU.mult).then_inc(small, 1)
                    dve.wait_ge(small, 3 * b + 3)
                    nc.vector.tensor_tensor(f.v2[q][:], f.v2[q][:], f.rstd[q][:], ALU.mult).then_inc(var2, 1)
                if t.runs(2):
                    b, r, q = t.block(2), t.slot(2, 4), t.slot(2, 2)
                    dve.wait_ge(xread[q], 16 * (t.round(2, 2) + 1))
                    for j in range(4):
                        dve.wait_ge(relued, 4 * b + j + 1)
                        nc.vector.tensor_tensor(k.R[r][:, quarter[j]], k.R[r][:, quarter[j]], k.Cb[q][:, quarter[j]],
                                                ALU.add).then_inc(summed, 1)
                    for j in range(4):
                        dve.wait_ge(summed, 4 * b + j + 1)
                        nc.vector.bn_stats(f.st[:, j, :], k.R[r][:, quarter[j]])
                    dve.drain()
                    for j in range(4):
                        nc.vector.bn_aggr(f.mv[q][:, j, :], f.st[:, j, :]).then_inc(moments, 1)
                if t.runs(1):
                    b, q = t.block(1), t.slot(1, 2)
                    dve.wait_ge(root2, b + 1)
                    nc.vector.reciprocal(f.rstd2[q][:], f.std2[q][:]).then_inc(ready, 1)
                if t.runs(3):
                    r = t.slot(3, 4)
                    dve.wait_ge(read[r], 16 * (t.round(3, 4) + 1))
                    for j in range(4):
                        nc.vector.tensor_tensor(k.R[r][:, quarter[j]], k.R[r][:, quarter[j]], k.scale[:],
                                                ALU.mult).then_inc(scaled, 1)
            run(dve, body)

        @block.scalar
        def _(act):
            def body(t):
                if t.runs(1):
                    b, q = t.block(1), t.slot(1, 2)
                    act.wait_ge(moments, 4 * b + 4)
                    nc.scalar.activation(f.std[q][:], f.mv[q][:, :, 1], ACT.Sqrt, bias=k.eps[:, 0:1]).then_inc(root1, 1)
                if t.runs(2):
                    b, r = t.block(2), t.slot(2, 4)
                    for j in range(4):
                        act.wait_ge(shifted, 4 * b + j + 1)
                        nc.scalar.activation(k.R[r][:, quarter[j]], k.R[r][:, quarter[j]], ACT.Relu).then_inc(relued, 1)
                if t.runs(1):
                    b, q = t.block(1), t.slot(1, 2)
                    act.wait_ge(var2, b + 1)
                    nc.scalar.activation(f.std2[q][:], f.v2[q][:], ACT.Sqrt, bias=k.eps[:, 0:1]).then_inc(root2, 1)
                if t.runs(0):
                    b, r, q = t.block(), t.slot(0, 4), t.slot(0, 2)
                    act.wait_ge(ready, b + 1)
                    ge(act, put[q], 32 * t.round(0, 2))
                    for j in range(4):
                        nc.scalar.activation(k.rows_out[q][:, quarter[j]], k.R[r][:, quarter[j]], ACT.Identity,
                                             scale=f.rstd[q][:, j:j + 1], bias=f.nmr[q][:, j:j + 1]).then_inc(normed, 1)
                    for j in range(4):
                        act.wait_ge(normed, 4 * b + j + 1)
                        nc.scalar.activation(f.out[q][:, quarter[j]], k.rows_out[q][:, quarter[j]], ACT.Copy,
                                             scale=f.rstd2[q][:, j:j + 1]).then_inc(outed, 1)
            run(act, body)


@stage
def edge_net(m, k, l, w):
    nc, ET, C = m.nc, m.ET, P
    nbr, f_in = w["Wf1"].shape[0], 6
    loaded, zeroed, vec, sc = (m.sem(f"net_{s}") for s in ("loaded", "zeroed", "vec", "sc"))
    sq, root, wt, wps, wout, wprod = (m.sem(f"net_{s}") for s in ("sq", "root", "wt", "wps", "wout", "wprod"))
    staged, turned, tout, hps, absd, relu = (m.sem(f"net_{s}") for s in ("staged", "turned", "tout", "hps", "absd", "relu"))
    groups = ET // 4
    with nc.Block() as block:
        @block.sync
        def _(sp):
            n = 0
            sp.wait_ge(zeroed, 1)
            loads = [(l.Ws[:], w["W_in2f_s"]), (l.Wv[:], w["W_in2f_v"]), (l.W2s[:], w["W2_s"]), (l.W2v[:], w["W2_v"]),
                     (l.W1s[:], w["W1_s"].rearrange("(f c) o -> f c o", c=2)),
                     (l.W1v[:], w["W1_v"].rearrange("(f c) o -> f c o", c=2)),
                     (l.Wf2[:], w["Wf2"][:, 0:4 * P]), (l.bf1[:], w["bf1"].rearrange("(f o) -> f o", o=1)),
                     (l.bf2[:], w["bf2"][0:4 * P].rearrange("(o f) -> o f", o=1).to_broadcast([P, 4 * P]))]
            loads += [(l.Wf1[32 * g:32 * g + nbr, g, :], w["Wf1"]) for g in range(4)]
            for dst, src in loads:
                sp.dma_start(dst, src).then_inc(loaded, 16)
                n += 16
            m.net_loads = n

        @block.vector
        def _(dve):
            v = Steps(dve, vec)
            nc.vector.memset(l.Wf1[:], 0.0).then_inc(zeroed, 1)
            v.link(nc.vector.memset(l.fst[0][:], 0.0))
            v.link(nc.vector.memset(l.fst[1][:], 0.0))
            r = l.pay[:, :, 3:6]
            v.link(nc.vector.tensor_tensor(l.yv[:], r, r, ALU.mult))
            nc.vector.tensor_reduce(l.n2[:], l.yv[:], axis=AX.X, op=ALU.add).then_inc(sq, 1)
            dve.wait_ge(root, 1)
            v.link(nc.vector.reciprocal(l.n2[:], l.norm[:]))
            v.link(nc.vector.tensor_tensor(l.yv[:], r, l.n2[:].unsqueeze(2).to_broadcast([P, ET, 3]), ALU.mult))
            v.link(nc.vector.tensor_scalar(l.yv[:], l.yv[:], Y1_SCALE, None, ALU.mult))
            rc = l.pay[:, :, 2:3].to_broadcast([P, ET, 3])
            v.link(nc.vector.tensor_tensor(l.c_v[:], l.yv[:], rc, ALU.mult))
            v.link(nc.vector.tensor_scalar(l.c_s[:], l.c_v[:], 1.0 / float(np.sqrt(3.0)), None, ALU.mult))
            v.link(nc.vector.tensor_scalar(l.c_0[:], l.pay[:, :, 2], Y0, None, ALU.mult))
            dve.wait_ge(loaded, m.net_loads)
            root_c, root_2f = 1.0 / float(np.sqrt(C)), 1.0 / float(np.sqrt(2 * P))
            for t, c in ((l.Ws, root_c), (l.Wv, root_c), (l.W2s, root_c), (l.W2v, root_c), (l.W1s, root_2f), (l.W1v, root_2f)):
                nc.vector.tensor_scalar(t[:], t[:], c, None, ALU.mult).then_inc(wt, 1)
            dve.wait_ge(wps, 1)
            nc.vector.tensor_copy(l.W1vT[:], l.ps[0][:, 0:2 * P].rearrange("p (a b) -> p a b", a=2)).then_inc(wout, 1)
            dve.wait_ge(wprod, 1)
            v.link(nc.vector.tensor_copy(l.Wvv[:], l.ps[1][:, 0:2 * P].rearrange("p (a b) -> p a b", a=2)))

            def group(g, q):
                nc.vector.tensor_copy(l.fst[q][:, :, 0:nbr], l.pay[:, bass.ds(4 * g, 4), f_in:f_in + nbr]).then_inc(staged, 1)
                dve.wait_ge(turned, g + 1)
                nc.vector.tensor_copy(l.fT[q][:], l.ps[2 + q][:, 0:P]).then_inc(tout, 1)
                dve.wait_ge(absd, g + 1)
                nc.vector.tensor_scalar(l.hT[:, bass.ds(4 * P * g, 4 * P)], l.ps[4 + q][:], l.bf1[:, 0:1], 0.0,
                                        ALU.add, ALU.max).then_inc(relu, 1)
            with dve.Fori(0, groups // 2) as g:
                group(2 * g, 0)
                group(2 * g + 1, 1)
            dve.wait_ge(sc, 2)
            dve.wait_ge(relu, groups)
            v.link(nc.vector.scalar_tensor_tensor(l.hT[:], l.big[:], -LOG2, l.hT[:], ALU.add, ALU.add))

        @block.tensor
        def _(pe):
            pe.wait_ge(wt, 6)
            for a in range(2):
                t = nc.tensor.transpose(l.ps[0][:, a * P:(a + 1) * P], l.W1v[:, a, :], k.ident[:])
            t.then_inc(wps, 1)
            pe.wait_ge(wout, 1)
            for a in range(2):
                t = nc.tensor.matmul(l.ps[1][:, a * P:(a + 1) * P], l.W1vT[:, a, :], l.W2v[:], start=True, stop=True)
            t.then_inc(wprod, 1)

            def group(g, q, first):
                pe.wait_ge(staged, g + 1)
                if not first:
                    pe.wait_ge(tout, g - 1)
                nc.tensor.transpose(l.ps[2 + q][:, 0:P], l.fst[q][:].rearrange("p a b -> p (a b)"), k.ident[:]).then_inc(turned, 1)
                pe.wait_ge(tout, g + 1)
                if not first:
                    pe.wait_ge(relu, g - 1)
                for a in range(4):
                    t = nc.tensor.matmul(l.ps[4 + q][:, a * P:(a + 1) * P], l.Wf1[:, a, :],
                                         l.fT[q][:], start=True, stop=True)
                t.then_inc(hps, 1)
            group(0, 0, True)
            group(1, 1, True)
            with pe.Fori(1, groups // 2) as g:
                group(2 * g, 0, False)
                group(2 * g + 1, 1, False)

        @block.scalar
        def _(act):
            act.wait_ge(sq, 1)
            nc.scalar.activation(l.norm[:], l.n2[:], ACT.Sqrt).then_inc(root, 1)
            act.wait_ge(loaded, m.net_loads)

            def group(g, q):
                act.wait_ge(hps, g + 1)
                nc.scalar.activation(l.big[:, bass.ds(4 * P * g, 4 * P)], l.ps[4 + q][:], ACT.Abs, bias=l.bf1[:, 0:1]).then_inc(absd, 1)
            with act.Fori(0, groups // 2) as g:
                group(2 * g, 0)
                group(2 * g + 1, 1)
            act.wait_ge(absd, groups)
            nc.scalar.activation(l.big[:], l.big[:], ACT.Exp, scale=-1.0).then_inc(sc, 1)
            act.wait_ge(sc, 1)
            nc.scalar.activation(l.big[:], l.big[:], ACT.Ln, bias=k.ones[:, 0:1]).then_inc(sc, 1)


@stage
def messages(m, k, l, x2_dram):
    nc, ET, D = m.nc, m.ET, m.D
    names = ("staged", "turned", "xT", "hcopy", "filt", "maps", "wb", "same", "cont", "u", "vec", "side",
             "msg", "sums", "agg", "outs", "scalars", "kept", "own_staged")
    s = {n: m.sem(f"msg_{n}") for n in names}
    got, own_got = ([m.sem(f"msg_{n}{r}") for r in range(4)] for n in ("got", "own_got"))
    G, own = ([a[r][:] for r in range(4)] for a in (l.G, l.own))
    DV = 7

    def run(engine, body, first=-3, last=ET):
        turns(engine, body, first, last, 4, ET // 4 - 2, ET)

    with nc.Block() as block:
        @block.gpsimd
        def _(pool):
            def body(t):
                if t.runs(3):
                    b, r = t.block(3), t.slot(3, 4)
                    ge(pool, s["staged"], b + 1)
                    ge(pool, s["turned"], b - 2)
                    if t.runs(4):
                        nc.gpsimd.tensor_copy(l.idx[t.slot(4, 4)][:], l.dst[:, bass.ds(b + 1, 1)]).then_inc(s["staged"], 1)
                    pool.indirect_dma_start(G[r], None, x2_dram,
                                            bass.IndirectOffsetOnAxis(ap=l.idx[r][:, 0:1], axis=0)).then_inc(got[r], 16)
                if t.runs(1):
                    b, r = t.block(1), t.slot(1, 4)
                    ge(pool, s["own_staged"], b + 1)
                    ge(pool, s["scalars"], 2 * (b - 2))
                    ge(pool, s["kept"], b - 2)
                    if t.runs(2):
                        nc.gpsimd.tensor_copy(l.idx2[t.slot(2, 4)][:], l.src[:, bass.ds(b + 1, 1)]).then_inc(s["own_staged"], 1)
                    pool.indirect_dma_start(own[r], None, x2_dram,
                                            bass.IndirectOffsetOnAxis(ap=l.idx2[r][:, 0:1], axis=0)).then_inc(own_got[r], 16)
            nc.gpsimd.tensor_copy(l.idx[0][:], l.dst[:, 0:1]).then_inc(s["staged"], 1)
            nc.gpsimd.tensor_copy(l.idx2[0][:], l.src[:, 0:1]).then_inc(s["own_staged"], 1)
            run(pool, body)

        @block.tensor
        def _(pe):
            def body(t):
                if t.runs(0):
                    b, q = t.block(), t.slot(0, 2)
                    pe.wait_ge(s["msg"], b + 1)
                    pe.wait_ge(s["side"], 3 * (b + 1))
                    pe.wait_ge(s["same"], b + 1)
                    ge(pe, s["agg"], 8 * b)
                    for c in range(8):
                        i = nc.tensor.matmul(l.ps[4 + c // 4][:, (c % 4) * P:(c % 4 + 1) * P], l.msg[q][:, c, :],
                                             l.same[q][:], start=True, stop=True)
                    i.then_inc(s["sums"], 1)
                if t.runs(-1):
                    b, q = t.block(-1), t.slot(-1, 2)
                    pe.wait_ge(s["agg"], 8 * (b + 1))
                    ge(pe, s["scalars"], 2 * b)
                    ge(pe, s["kept"], b)
                    o = l.ps[6]
                    for c in range(2):
                        nc.tensor.matmul(l.ps[7][:, 0:P], l.W1s[:, c, :], l.agg[q][:, c, :], start=(c == 0), stop=(c == 1))
                    for i in range(3):
                        for c in range(2):
                            x = nc.tensor.matmul(o[:, i * P:(i + 1) * P], l.agg[q][:, 2 + 3 * c + i, :], l.Wvv[:, c, :],
                                                 start=(c == 0), stop=(c == 1))
                    x.then_inc(s["outs"], 1)
                if t.runs(2):
                    b, q, r = t.block(2), t.slot(2, 2), t.slot(2, 4)
                    pe.wait_ge(got[r], 16 * (t.round(2, 4) + 1))
                    ge(pe, s["xT"], b)
                    for c in range(4):
                        src = G[r][:, 0:P] if c == 0 else G[r][:, P:D].rearrange("p (c i) -> p i c", i=3)[:, c - 1, :]
                        i = nc.tensor.transpose(l.ps[0][:, c * P:(c + 1) * P], src, k.ident[:])
                    i.then_inc(s["turned"], 1)
                    pe.wait_ge(s["hcopy"], b + 1)
                    ge(pe, s["wb"], b)
                    nc.tensor.matmul(l.ps[1][:], l.hb[q][:], l.Wf2[:], start=True, stop=True).then_inc(s["filt"], 1)
                    pe.wait_ge(s["xT"], b + 1)
                    ge(pe, s["msg"], b - 1)
                    for c in range(4):
                        i = nc.tensor.matmul(l.ps[2 + q][:, c * P:(c + 1) * P], l.xT[q][:, c, :],
                                             (l.Ws if c == 0 else l.Wv)[:], start=True, stop=True)
                    i.then_inc(s["maps"], 1)
            run(pe, body)

        @block.scalar
        def _(act):
            def body(t):
                if t.runs(2):
                    b, q = t.block(2), t.slot(2, 2)
                    ge(act, s["filt"], b - 1)
                    nc.scalar.copy(l.hb[q][:], l.hT[:, bass.ds(P * b, P)]).then_inc(s["hcopy"], 1)
                if t.runs(1):
                    b, q = t.block(1), t.slot(1, 2)
                    act.wait_ge(s["u"], b + 1)
                    ge(act, s["sums"], b - 1)
                    for i in range(3):
                        nc.scalar.activation(l.msg[q][:, 2 + i, :], l.u[q][:], ACT.Copy,
                                             scale=l.c_v[:, bass.ds(b, 1), i]).then_inc(s["side"], 1)
                if t.runs(-1):
                    b, r = t.block(-1), t.slot(-1, 4)
                    act.wait_ge(s["outs"], b + 1)
                    nc.scalar.copy(l.sT[:, bass.ds(P * b, P)], l.ps[7][:, 0:P]).then_inc(s["scalars"], 1)
                    act.wait_ge(own_got[r], 16 * (t.round(-1, 4) + 1))
                    nc.scalar.copy(l.X[:, bass.ds(b, 1), 0:P].rearrange("p a f -> p (a f)"), own[r][:, 0:P]).then_inc(s["scalars"], 1)
                if t.runs(2):
                    b, q = t.block(2), t.slot(2, 2)
                    act.wait_ge(s["turned"], b + 1)
                    ge(act, s["maps"], b - 1)
                    nc.scalar.copy(l.xT[q][:], l.ps[0][:].rearrange("p (c n) -> p c n", c=4)).then_inc(s["xT"], 1)
            run(act, body)
            act.wait_ge(s["scalars"], 2 * ET)

        @block.vector
        def _(dve):
            def body(t):
                if t.runs(1):
                    b, q = t.block(1), t.slot(1, 2)
                    n0 = DV * b

                    def link(i, step):
                        i.then_inc(s["vec"], 1)
                        dve.wait_ge(s["vec"], n0 + step)
                    ge(dve, s["sums"], b - 1)
                    nc.vector.tensor_scalar(l.same[q][:], l.rows[:, bass.ds(P * b + 4, P)], l.skey[:, bass.ds(b, 1)],
                                            None, ALU.is_equal).then_inc(s["same"], 1)
                    ge(dve, s["agg"], 8 * (b - 1))
                    nc.vector.tensor_scalar(l.cont[q][:], l.rows[:, bass.ds(P * b + 4, P)], l.rows[:, bass.ds(P * b + 3, 1)],
                                            None, ALU.is_equal).then_inc(s["cont"], 1)
                    dve.wait_ge(s["wb"], b + 1)
                    dve.wait_ge(s["maps"], b + 1)
                    sj = l.ps[2 + q][:, 0:P]
                    v = [l.ps[2 + q][:, (i + 1) * P:(i + 2) * P] for i in range(3)]
                    fs = l.Wb[q][:, 0:2 * P].rearrange("p (f c) -> p c f", c=2)
                    fv = l.Wb[q][:, 2 * P:4 * P].rearrange("p (f c) -> p c f", c=2)
                    c0 = l.c_0[:, bass.ds(b, 1)]
                    ge(dve, s["side"], 3 * (b - 1))
                    nc.vector.tensor_tensor(l.u[q][:], sj, fv[:, 0, :], ALU.mult).then_inc(s["u"], 1)
                    link(nc.vector.scalar_tensor_tensor(l.msg[q][:, 0, :], sj, c0, fs[:, 0, :], ALU.mult, ALU.mult), 1)
                    link(nc.vector.tensor_scalar(l.dot[:], v[0], l.c_s[:, bass.ds(b, 1), 0], None, ALU.mult), 2)
                    link(nc.vector.scalar_tensor_tensor(l.dot[:], v[1], l.c_s[:, bass.ds(b, 1), 1], l.dot[:], ALU.mult, ALU.add), 3)
                    link(nc.vector.scalar_tensor_tensor(l.dot[:], v[2], l.c_s[:, bass.ds(b, 1), 2], l.dot[:], ALU.mult, ALU.add), 4)
                    link(nc.vector.tensor_tensor(l.msg[q][:, 1, :], l.dot[:], fs[:, 1, :], ALU.mult), 5)
                    for i in range(2):
                        link(nc.vector.scalar_tensor_tensor(l.msg[q][:, 5 + i, :], v[i], c0, fv[:, 1, :], ALU.mult, ALU.mult), 6 + i)
                    nc.vector.scalar_tensor_tensor(l.msg[q][:, 7, :], v[2], c0, fv[:, 1, :], ALU.mult, ALU.mult).then_inc(s["msg"], 1)
                if t.runs(0):
                    b, q = t.block(), t.slot(0, 2)
                    dve.wait_ge(s["sums"], b + 1)
                    dve.wait_ge(s["cont"], b + 1)
                    ge(dve, s["outs"], b - 1)
                    ge(dve, s["agg"], 8 * b)
                    for c in range(8):
                        nc.vector.scalar_tensor_tensor(l.agg[q][:, c, :], l.cont[q][:], l.agg[1 - q][:, c, P - 1:P],
                                                       l.ps[4 + c // 4][:, (c % 4) * P:(c % 4 + 1) * P],
                                                       ALU.mult, ALU.add).then_inc(s["agg"], 1)
                if t.runs(-1):
                    b, r = t.block(-1), t.slot(-1, 4)
                    dve.wait_ge(s["outs"], b + 1)
                    dve.wait_ge(own_got[r], 16 * (t.round(-1, 4) + 1))
                    nc.vector.tensor_tensor(l.X[:, bass.ds(b, 1), P:D].rearrange("p a (d i) -> p (a d) i", i=3),
                                            own[r][:, P:D].rearrange("p (d i) -> p d i", i=3),
                                            l.ps[6][:, 0:3 * P].rearrange("p (i d) -> p d i", i=3), ALU.add).then_inc(s["kept"], 1)
                if t.runs(2):
                    b, q = t.block(2), t.slot(2, 2)
                    dve.wait_ge(s["filt"], b + 1)
                    nc.vector.tensor_tensor(l.Wb[q][:], l.ps[1][:], l.bf2[:], ALU.add).then_inc(s["wb"], 1)
            run(dve, body)
            dve.wait_ge(s["kept"], ET)


@stage
def touched(m, k, l, out_dram):
    nc, ET, D = m.nc, m.ET, m.D
    mag = l.rows[:, 0:m.EPAD]
    names = ("mag", "exp", "log", "pos", "plus", "vec", "hcopy", "prod", "ysum", "aggr", "root", "rec", "nmr", "done", "idx2")
    s = {n: m.sem(f"tch_{n}") for n in names}
    put = [m.sem(f"tch_put{r}") for r in range(4)]
    parts = 4
    part = [slice(i * m.EPAD // parts, (i + 1) * m.EPAD // parts) for i in range(parts)]

    def x_row(b):
        return l.X[:, bass.ds(b, 1), :].rearrange("p a f -> p (a f)")

    def run(engine, body, first=-2, last=ET - 1):
        turns(engine, body, first, last, 4, ET // 4 - 2, ET)

    with nc.Block() as block:
        @block.scalar
        def _(act):
            for i in range(parts):
                nc.scalar.activation(mag[:, part[i]], l.sT[:, part[i]], ACT.Abs).then_inc(s["mag"], 1)
            for i in range(parts):
                act.wait_ge(s["mag"], i + 1)
                nc.scalar.activation(mag[:, part[i]], mag[:, part[i]], ACT.Exp, scale=-1.0).then_inc(s["exp"], 1)
            for i in range(parts):
                act.wait_ge(s["exp"], i + 1)
                nc.scalar.activation(mag[:, part[i]], mag[:, part[i]], ACT.Ln, bias=k.ones[:, 0:1]).then_inc(s["log"], 1)
            act.wait_ge(s["plus"], parts)

            def body(t):
                if t.runs(2):
                    b, q = t.block(2), t.slot(2, 2)
                    ge(act, s["prod"], b - 1)
                    nc.scalar.copy(l.hb[q][:], l.sT[:, bass.ds(P * b, P)]).then_inc(s["hcopy"], 1)
                if t.runs(0):
                    b, q, r = t.block(), t.slot(0, 2), t.slot(0, 4)
                    act.wait_ge(s["nmr"], b + 1)
                    ge(act, put[r], 16 * t.round(0, 4))
                    nc.scalar.activation(l.Y[r], x_row(b), ACT.Identity, scale=l.rstd[q][:], bias=l.nmr[q][:]).then_inc(s["done"], 1)
                if t.runs(1):
                    b, q = t.block(1), t.slot(1, 2)
                    act.wait_ge(s["aggr"], b + 1)
                    nc.scalar.activation(l.std[q][:], l.mv[q][:, 1:2], ACT.Sqrt, bias=k.eps[:, 0:1]).then_inc(s["root"], 1)
            run(act, body)

        @block.gpsimd
        def _(pool):
            ge(pool, s["vec"], 3)

            def body(t):
                if t.runs(0):
                    b, r, r_next = t.block(), t.slot(0, 4), t.slot(1, 4)
                    ge(pool, s["idx2"], b + 1)
                    ge(pool, s["done"], b + 1)
                    ge(pool, put[r_next], 16 * t.round(1, 4))
                    if t.runs(1):
                        nc.gpsimd.tensor_copy(l.idx2[r_next][:], l.row[:, bass.ds(b + 1, 1)]).then_inc(s["idx2"], 1)
                    pool.indirect_dma_start(out_dram, bass.IndirectOffsetOnAxis(ap=l.idx2[r][:, 0:1], axis=0), l.Y[r], None,
                                            bounds_check=m.N - 1, oob_is_err=False).then_inc(put[r], 16)
            nc.gpsimd.tensor_copy(l.idx2[0][:], l.row[:, 0:1]).then_inc(s["idx2"], 1)
            run(pool, body)
            for r in range(4):
                ge(pool, put[r], 16 * (ET // 4))

        @block.tensor
        def _(pe):
            def body(t):
                if t.runs(2):
                    b, q = t.block(2), t.slot(2, 2)
                    pe.wait_ge(s["hcopy"], b + 1)
                    ge(pe, s["ysum"], b - 1)
                    nc.tensor.matmul(l.ps[q][:, 0:P], l.hb[q][:], l.W2s[:], start=True, stop=True).then_inc(s["prod"], 1)
            run(pe, body)

        @block.vector
        def _(dve):
            v = Steps(dve, s["vec"])
            v.link(nc.vector.tensor_tensor(l.more[:], l.skey[:], l.next[:], ALU.is_equal))
            v.link(nc.vector.scalar_tensor_tensor(l.rowf[:], l.more[:], float(SKIP), l.skey[:], ALU.mult, ALU.add))
            v.link(nc.vector.tensor_copy(l.row[:], l.rowf[:]))
            for i in range(parts):
                dve.wait_ge(s["mag"], i + 1)
                nc.vector.tensor_scalar(l.sT[:, part[i]], l.sT[:, part[i]], 0.0, None, ALU.max).then_inc(s["pos"], 1)
            dve.wait_ge(s["pos"], parts)
            for i in range(parts):
                dve.wait_ge(s["log"], i + 1)
                nc.vector.scalar_tensor_tensor(l.sT[:, part[i]], mag[:, part[i]], -LOG2, l.sT[:, part[i]],
                                               ALU.add, ALU.add).then_inc(s["plus"], 1)

            def body(t):
                if t.runs(0):
                    b, q = t.block(), t.slot(0, 2)
                    dve.wait_ge(s["root"], b + 1)
                    ge(dve, s["done"], b - 1)
                    nc.vector.reciprocal(l.rstd[q][:], l.std[q][:]).then_inc(s["rec"], 1)
                if t.runs(1):
                    b = t.block(1)
                    dve.wait_ge(s["prod"], b + 1)
                    ge(dve, s["nmr"], b - 1)
                    nc.vector.tensor_tensor(l.X[:, bass.ds(b, 1), 0:P].rearrange("p a f -> p (a f)"),
                                            l.X[:, bass.ds(b, 1), 0:P].rearrange("p a f -> p (a f)"),
                                            l.ps[t.slot(1, 2)][:, 0:P], ALU.add).then_inc(s["ysum"], 1)
                if t.runs(0):
                    b, q = t.block(), t.slot(0, 2)
                    dve.wait_ge(s["rec"], b + 1)
                    nc.vector.scalar_tensor_tensor(l.nmr[q][:], l.mv[q][:, 0:1], -1.0, l.rstd[q][:], ALU.mult, ALU.mult).then_inc(s["nmr"], 1)
                if t.runs(1):
                    b, q = t.block(1), t.slot(1, 2)
                    dve.drain()
                    nc.vector.bn_stats(l.st[:], x_row(b))
                    dve.drain()
                    nc.vector.bn_aggr(l.mv[q][:], l.st[:]).then_inc(s["aggr"], 1)
            run(dve, body)


class Bag:
    pass


def build(nc, x, src, dst, attr20, attr3, weight, W, b, gamma, beta, net, out):
    n_nodes, d = x.shape
    n_edges, = src.shape
    n_layers = W.shape[0]
    n_rbf = attr20.shape[1]
    with ExitStack() as whole:
        m = Machine(nc, whole, n_nodes, n_edges, d)
        ET, NC, EPAD = m.ET, m.NCOL, m.EPAD
        width = 6 + n_rbf
        agg = [m.dram(f"agg{i}", [m.NPAD, d]) for i in range(2)]
        merged_dram = m.dram("merged", [EPAD, d])
        x2_dram = m.dram("x2", [m.NPAD, d])
        dinv_dram = m.dram("dinv_rows", [m.NPAD, 1])
        by_dst = m.dram("by_dst", [EPAD, 2], I32)
        by_src = m.dram("by_src", [EPAD + 1, width], I32)

        k = Bag()
        k.ident, k.ones, k.before, k.after, k.count = (m.sb(n, [P, P]) for n in ("ident", "ones", "before", "after", "count"))
        k.part, k.eps = m.sb("part", [P, 1]), m.sb("eps", [P, 1])
        constants(m, k)
        k.node = n = Bag()
        n.dinv, n.self_w, n.edge_w = (m.sb(f"node_{s}", [P, NC]) for s in ("dinv", "self_w", "edge_w"))
        n.row = m.sb("node_row", [P, NC], I32)
        n.idx = [m.sb(f"node_idx{q}", [P, 4], I32) for q in range(4)]
        bn = k.bn = Bag()
        bn.mv = m.sb("bn_mv", [P, m.C, 2])
        bn.std, bn.mean, bn.scale, bn.shift = (m.sb(f"bn_{s}", [P, m.C]) for s in ("std", "mean", "scale", "shift"))
        k.param = m.sb("param", [P, 3, n_layers * m.C])

        edge_sort = ExitStack()
        m.ctx = edge_sort
        payload = m.sb("payload", [P, ET, width], I32)
        place_dst, place_src = (m.sb(f"place_{s}", [P, ET], I32) for s in ("dst", "src"))
        bufs = [m.sb(f"scatter_idx{r}", [P, 1], I32) for r in range(4)], [m.sb(f"scatter_row{r}", [P, width], I32) for r in range(4)]
        rows_by_dst = Scatter(m, "by_dst", payload, 2, place_dst, bufs, by_dst)
        rows_by_src = Scatter(m, "by_src", payload, width, place_src, bufs, by_src)

        with ExitStack() as part:
            m.ctx = part
            w = k.sort = Bag()
            w.key, w.tmp, w.tmp2 = (m.sb(f"sort_{s}", [P, ET], I32) for s in ("key", "tmp", "tmp2"))
            w.keyf, w.lof, w.colf, w.rank, w.pos = (m.sb(f"sort_{s}", [P, ET]) for s in ("keyf", "lof", "colf", "rank", "pos"))
            w.hot_col, w.hot_lo = m.sb("hot_col", [P, ET, NC], BF16), m.sb("hot_lo", [P, ET, P], BF16)
            w.keyrow, w.hot_loT = m.sb("keyrow", [P, EPAD]), m.sb("hot_loT", [P, EPAD])
            w.diag = [m.sb(f"diag{q}", [P, 4, P]) for q in range(2)]
            w.cnt, w.end, w.has, w.tmpn, w.tmpn2 = (m.sb(f"sort_{s}", [P, NC]) for s in ("cnt", "end", "has", "tmpn", "tmpn2"))
            w.rowsum, w.rowsum2, w.scan = (m.sb(f"sort_{s}", [P, m.NB]) for s in ("rowsum", "rowsum2", "scan"))
            w.pre = m.sb("sort_pre", [P, 2 * m.NB])
            w.base = [m.sb(f"sort_base{r}", [P, NC]) for r in range(4)]
            w.lt = [m.sb(f"sort_lt{r}", [P, P]) for r in range(4)]
            w.junk, w.junk2 = m.sb("sort_junk", [P, P]), m.sb("sort_junk2", [P, NC])
            w.ps_row = [m.ps(f"ps_row{q}", [P, 512]) for q in range(2)]
            w.ps_cnt = m.ps("ps_cnt", [P, 512])
            w.ps_new = [m.ps(f"ps_new{q}", [P, 512]) for q in range(2)]
            w.ps_look = [m.ps(f"ps_look{q}", [P, 512]) for q in range(2)]
            w.ps_pre = m.ps("ps_pre", [P, 512])
            load_edges(m, k, payload, (src, dst, weight, attr3, attr20), (b, gamma, beta), by_src, n_layers)
            sort_by(m, k, "dst", dst, place_dst, n, None)
            sort_by(m, k, "src", src, place_src, None, rows_by_dst)

        with ExitStack() as part:
            m.ctx = part
            w = k.sort = Bag()
            e = k.edge = Bag()
            e.pair = m.sb("edge_pair", [P, ET, 2], I32)
            e.src = m.sb("edge_src", [P, ET], I32)
            e.skey, e.dsrc = m.sb("edge_key", [P, ET]), m.sb("edge_dsrc", [P, ET])
            e.rows = m.sb("edge_rows", [P, EPAD])
            e.tiles = m.sb("edge_tiles", [ET, 2 * P], I32)
            e.tkey, e.tjunk = m.sb("edge_tkey", [ET, P]), m.sb("edge_tjunk", [ET, P])
            e.run, e.run2 = m.sb("edge_run", [ET, 1]), m.sb("edge_run2", [ET, 1])
            e.fix_row = m.sb("edge_fix_row", [ET, 1], I32)
            e.lacks = m.sb("edge_lacks", [ET, ET])
            e.idx = [m.sb(f"edge_idx{q}", [P, 1], I32) for q in range(4)]
            e.val = [m.sb(f"edge_val{q}", [P, 1]) for q in range(4)]
            e.same = [m.sb(f"edge_same{q}", [P, P]) for q in range(2)]
            k.R = [m.sb(f"R{r}", [P, 4 * d]) for r in range(4)]
            k.Cb = [m.sb(f"Cb{r}", [P, 4 * d]) for r in range(2)]
            k.rows_out = [m.sb(f"rows_out{r}", [P, 4 * d]) for r in range(2)]
            k.scale, k.shift = m.sb("scale", [P, d]), m.sb("shift", [P, d])
            k.stat = m.sb("stat", [P, m.C, 6 * m.NB])
            k.ps_a, k.ps_b, k.ps_c = ([m.ps(f"ps_{s}{q}", [P, 512]) for q in range(2)] for s in "abc")
            w.diag = [k.rows_out[q][:, 0:4 * P].rearrange("p (a b) -> p a b", a=4) for q in range(2)]
            w.ps_row = k.ps_a
            sorted_edges(m, k, "dst", by_dst, 2, 1, e.rows, e.skey, e.pair)
            edge_tables(m, k, dinv_dram, by_dst)
            clear_gathered(m, k)
            with ExitStack() as inner:
                m.ctx = inner
                k.whi, k.wlo = m.sb("whi", [P, m.C, d], F32R), m.sb("wlo", [P, m.C, d], F32R)
                k.yhi = [m.sb(f"yhi{q}", [P, m.C, 4 * P], F32R) for q in range(2)]
                k.ylo = [m.sb(f"ylo{q}", [P, m.C, 4 * P], F32R) for q in range(2)]
                k.aggT = [m.sb(f"aggT{q}", [P, m.C, 4 * P]) for q in range(2)]
                table = x
                for layer in range(n_layers):
                    prepare(m, k, layer, W)
                    merge(m, k, layer, table, merged_dram)
                    dense(m, k, layer, table, agg[layer % 2], merged_dram)
                    table = agg[layer % 2]
                prepare(m, k, n_layers, None)
            m.ctx = part
            f = k.fin = Bag()
            f.out = [m.sb(f"fin_out{q}", [P, 4 * d]) for q in range(2)]
            f.st = m.sb("fin_st", [P, 4, 6])
            f.mv = [m.sb(f"fin_mv{q}", [P, 4, 2]) for q in range(2)]
            f.std, f.rstd, f.nmr, f.v2, f.std2, f.rstd2 = ([m.sb(f"fin_{s}{q}", [P, 4]) for q in range(2)]
                                                           for s in ("std", "rstd", "nmr", "v2", "std2", "rstd2"))
            finish_gcn(m, k, table, x, x2_dram, out, rows_by_src)

        edge_sort.close()

        with ExitStack() as part:
            m.ctx = part
            l = Bag()
            w = k.sort = Bag()
            edges = m.sb("l_edges", [P, ET, width], I32)
            l.pay = edges[:].bitcast(F32)
            rows = m.sb("l_rows", [P, EPAD + 4])
            l.rows = rows
            l.skey, l.next, l.more, l.rowf = (m.sb(f"l_{s}", [P, ET]) for s in ("skey", "next", "more", "rowf"))
            l.src, l.dst, l.row, nexti = (m.sb(f"l_{s}", [P, ET], I32) for s in ("src", "dst", "row", "nexti"))
            l.Ws, l.Wv, l.W2s = (m.sb(f"l_{s}", [P, P]) for s in ("Ws", "Wv", "W2s"))
            l.W1s, l.Wvv = (m.sb(f"l_{s}", [P, 2, P]) for s in ("W1s", "Wvv"))
            l.Wf2 = m.sb("l_Wf2", [P, 4 * P])
            l.bf1, l.bf2 = m.sb("l_bf1", [P, 1]), m.sb("l_bf2", [P, 4 * P])
            l.yv, l.c_v, l.c_s = (m.sb(f"l_{s}", [P, ET, 3]) for s in ("yv", "c_v", "c_s"))
            l.n2, l.norm, l.c_0 = (m.sb(f"l_{s}", [P, ET]) for s in ("n2", "norm", "c_0"))
            l.hT, l.sT = (m.sb(f"l_{s}", [P, EPAD]) for s in ("hT", "sT"))
            l.X = m.sb("l_X", [P, ET, d])
            scratch, used = l.X[:].rearrange("p a f -> p (a f)"), EPAD
            l.big = scratch[:, 0:EPAD]
            views = []
            for a, b_ in ((1, P), (2, P), (2, P), (4, P), (4, 32), (4, 32), (1, P), (1, P)):
                views.append(scratch[:, used:used + a * b_])
                if a > 1:
                    views[-1] = views[-1].rearrange("p (a b) -> p a b", a=a)
                used += a * b_
            l.W2v, l.W1v, l.W1vT, l.Wf1 = views[:4]
            l.fst, l.fT = views[4:6], views[6:8]
            l.G = [m.sb(f"l_G{r}", [P, d]) for r in range(4)]
            l.idx = [m.sb(f"l_idx{r}", [P, 1], I32) for r in range(4)]
            l.idx2 = [m.sb(f"l_idx2{r}", [P, 1], I32) for r in range(4)]
            l.own = [m.sb(f"l_own{r}", [P, d]) for r in range(4)]
            two = lambda s, shape: [m.sb(f"l_{s}{q}", shape) for q in range(2)]
            l.same, l.cont, l.u, l.hb = (two(s, [P, P]) for s in ("same", "cont", "u", "hb"))
            l.xT, l.Wb = two("xT", [P, 4, P]), two("Wb", [P, 4 * P])
            l.msg, l.agg = two("msg", [P, 8, P]), two("agg", [P, 8, P])
            l.dot = m.sb("l_dot", [P, P])
            l.st = m.sb("l_st", [P, 6])
            l.mv = two("mv", [P, 2])
            l.std, l.rstd, l.nmr = (two(s, [P, 1]) for s in ("std", "rstd", "nmr"))
            l.Y = [a[:, 0:4, :].rearrange("p a b -> p (a b)") for a in l.msg + l.agg]
            l.ps = [m.ps(f"l_ps{i}", [P, 512]) for i in range(8)]
            w.diag = l.xT
            w.ps_row = l.ps[0:2]
            sorted_edges(m, k, "src", by_src[0:EPAD, :], width, 0, rows[:, 4:EPAD + 4], l.skey, edges)
            edge_ends(m, l, edges, nexti, by_src)
            edge_net(m, k, l, net)
            messages(m, k, l, x2_dram)
            touched(m, k, l, out)


@stage
def load_edges(m, k, payload, arrays, params, by_src, n_layers):
    nc, ET = m.nc, m.ET
    filled, loaded = m.sem("pay_filled"), m.sem("pay_loaded")
    with ExitStack() as stack, nc.Block() as block:
        @block.vector
        def _(dve):
            nc.vector.memset(payload[:].bitcast(F32), 1.0).then_inc(filled, 1)
            nc.vector.memset(k.eps[:], LN_EPS).then_inc(filled, 1)
            dve.wait_ge(filled, 2)
            nc.vector.memset(payload[:, :, 0:2], m.NPAD - 1).then_inc(filled, 1)
            nc.vector.memset(k.sort.key[:], -1).then_inc(filled, 1)

        @block.sync
        def _(sp):
            stack.enter_context(nc.allow_non_contiguous_dma(reason="edge payloads and parameters, once"))
            n, at_word = 0, 0
            sp.wait_ge(filled, 4)
            for a in arrays:
                if len(a.shape) == 1:
                    a = a.rearrange("(e o) -> e o", o=1)
                wide = a.shape[1]
                to = payload[0:m.EP, :, at_word:at_word + wide]
                if a.dtype == F32:
                    to = to.bitcast(F32)
                sp.dma_start(to, a.rearrange("(p t) w -> p t w", t=ET)).then_inc(loaded, 16)
                at_word += wide
                n += 16
            for i, a in enumerate(params):
                for layer in range(n_layers):
                    sp.dma_start(k.param[:, i, layer * m.C:(layer + 1) * m.C],
                                 a[layer].rearrange("(c p) -> p c", p=P)).then_inc(loaded, 16)
                    n += 16
            sp.dma_start(by_src[m.EPAD:m.EPAD + 1, 0:2], k.sort.key[0:1, 0:2]).then_inc(loaded, 16)
            sp.wait_ge(loaded, n + 16)


@stage
def clear_gathered(m, k):
    nc, cleared = m.nc, m.sem("cleared")
    with nc.Block() as block:
        @block.vector
        def _(dve):
            for q in range(2):
                nc.vector.memset(k.Cb[q][:], 0.0).then_inc(cleared, 1)
            dve.wait_ge(cleared, 2)


@stage
def edge_ends(m, l, edges, nexti, by_src):
    nc, loaded, made = m.nc, m.sem("ends_loaded"), m.sem("ends_made")
    with nc.Block() as block:
        @block.sync
        def _(sp):
            with nc.allow_non_contiguous_dma(reason="one word of each sorted row"):
                sp.dma_start(nexti[:], by_src[1:m.EPAD + 1, :].rearrange("(t p) w -> p t w", p=P)[:, :, 0]).then_inc(loaded, 16)

        @block.vector
        def _(dve):
            nc.vector.tensor_copy(l.src[:], edges[:, :, 0]).then_inc(made, 1)
            nc.vector.tensor_copy(l.dst[:], edges[:, :, 1]).then_inc(made, 1)
            nc.vector.memset(l.rows[:, 0:4], -1.0).then_inc(made, 1)
            nc.vector.memset(l.agg[1][:], 0.0).then_inc(made, 1)
            dve.wait_ge(loaded, 16)
            nc.vector.tensor_copy(l.next[:], nexti[:]).then_inc(made, 1)
            dve.wait_ge(made, 5)


NET = ["W_in2f_s", "W_in2f_v", "Wf1", "bf1", "Wf2", "bf2", "W1_s", "W1_v", "W2_s", "W2_v"]
_INS = ["x", "src", "dst", "edge_attr_20", "edge_attr_3", "edge_weight", "L0_gnn_W", "L0_gnn_b",
        "L0_gnn_gamma", "L0_gnn_beta"] + ["L1_gnn_" + n for n in NET]


def program(nc, a, out):
    build(nc, a["x"], a["src"], a["dst"], a["edge_attr_20"], a["edge_attr_3"], a["edge_weight"],
          a["L0_gnn_W"], a["L0_gnn_b"], a["L0_gnn_gamma"], a["L0_gnn_beta"],
          {n: a["L1_gnn_" + n] for n in NET}, out)


def kernel(**inputs):
    import concourse.bacc as _bacc
    from concourse import mybir as _mybir
    from concourse.bass_utils import run_bass_kernel_spmd as _run

    nc = _bacc.Bacc("TRN2", target_bir_lowering=False, num_devices=1)
    arrays, args = {}, {}
    for name in _INS:
        a = np.ascontiguousarray(inputs[name])
        arrays[f"in_{name}"] = a
        args[name] = nc.dram_tensor(f"in_{name}", a.shape, _mybir.dt.from_np(a.dtype), kind="ExternalInput").ap()
    out = nc.dram_tensor("out_0", inputs["x"].shape, F32, kind="ExternalOutput").ap()
    program(nc, args, out)
    r = _run(nc, [arrays], core_ids=[0])
    return r.results[0]["out_0"]
```

```python
from contextlib import ExitStack

import numpy as np
import concourse.bass as bass
from concourse import mybir

F32, F32R = mybir.dt.float32, mybir.dt.float32r
BF16, I32 = mybir.dt.bfloat16, mybir.dt.int32
ALU, ACT, AX = mybir.AluOpType, mybir.ActivationFunctionType, mybir.AxisListType

P = 128
BN_EPS = LN_EPS = 1e-5
LOG2 = float(np.log(2.0))
Y0 = float(1.0 / np.sqrt(4.0 * np.pi))
Y1_SCALE = float(np.sqrt(3.0 / (4.0 * np.pi)))
SKIP = 1 << 20


class Steps:

    def __init__(self, engine, sem, base=0):
        self.engine, self.sem, self.base, self.n = engine, sem, base, 0

    def link(self, instruction):
        instruction.then_inc(self.sem, 1)
        self.n += 1
        self.engine.wait_ge(self.sem, self.base + self.n)


class Machine:

    def __init__(self, nc, ctx, n_nodes, n_edges, d):
        self.nc, self.ctx = nc, ctx
        self.N, self.E, self.D = n_nodes, n_edges, d
        self.C = d // P
        self.BLK = 4 * P
        self.NB = -(-n_nodes // self.BLK)
        self.NPAD = self.NB * self.BLK
        self.NCOL = self.NB * 4
        self.TP = (n_nodes - (self.NB - 1) * self.BLK) // 4
        self.ET = -(-n_edges // P)
        assert self.ET == 2 * self.NB
        self.EPAD = self.ET * P
        self.EP = n_edges // self.ET
        assert self.EP * self.ET == n_edges and self.TP * 4 + (self.NB - 1) * self.BLK == n_nodes
        assert self.ET % 4 == 0 and self.NB % 4 == 0

    def sb(self, name, shape, dt=F32):
        return self.ctx.enter_context(self.nc.sbuf_tensor(name, shape, dt))

    def ps(self, name, shape, dt=F32):
        return self.ctx.enter_context(self.nc.psum_tensor(name, shape, dt))

    def sem(self, name):
        self.counters.append(self.nc.alloc_semaphore(name=name))
        return self.counters[-1]

    def dram(self, name, shape, dt=F32):
        return self.nc.dram_tensor(name, shape, dt).ap()


def stage(function):
    def run(m, *args):
        m.counters = []
        function(m, *args)
        m.nc.clear_and_free_semaphores(m.counters)
        m.nc.all_engine_barrier()
    return run


def block_rows(table, m):
    return table.rearrange("(b p j) f -> b p (j f)", p=P, j=4)


def at(view, i):
    if isinstance(i, int):
        return view[i]
    return view[bass.ds(i, 1)].rearrange("a p f -> (a p) f")


@stage
def constants(m, k):
    nc = m.nc
    filled, made = m.sem("const_filled"), m.sem("const_made")
    with nc.Block() as block:
        @block.gpsimd
        def _(pool):
            nc.gpsimd.memset(k.ident[:], 0.0).then_inc(filled, 1)
            nc.gpsimd.memset(k.ones[:], 1.0).then_inc(filled, 1)
            nc.gpsimd.iota(k.count[:], [[1, P]], base=0, channel_multiplier=0,
                           allow_small_or_imprecise_dtypes=True).then_inc(made, 1)
            nc.gpsimd.iota(k.part[:], [[0, 1]], base=0, channel_multiplier=1,
                           allow_small_or_imprecise_dtypes=True).then_inc(made, 1)
            ge(pool, filled, 2)
            nc.gpsimd.affine_select(out=k.ident[:], in_=k.ident[:], compare_op=ALU.not_equal, fill=1.0,
                                    base=0, pattern=[[-1, P]], channel_multiplier=1).then_inc(made, 1)
            nc.gpsimd.affine_select(out=k.before[:], in_=k.ones[:], compare_op=ALU.is_gt, fill=0.0,
                                    base=0, pattern=[[1, P]], channel_multiplier=-1).then_inc(made, 1)
            nc.gpsimd.affine_select(out=k.after[:], in_=k.ones[:], compare_op=ALU.is_gt, fill=0.0,
                                    base=0, pattern=[[-1, P]], channel_multiplier=1).then_inc(made, 1)
            ge(pool, made, 5)


@stage
def sort_by(m, k, tag, key_dram, places, table, earlier):
    nc, ET, NC = m.nc, m.ET, m.NCOL
    w = k.sort
    loaded, filled, hot = (m.sem(f"{tag}_{s}") for s in ("loaded", "filled", "hot"))
    diag, row_ps, row_out = (m.sem(f"{tag}_{s}") for s in ("diag", "row_ps", "row_out"))
    counted, pre_in, pre_ps, base0 = (m.sem(f"{tag}_{s}") for s in ("counted", "pre_in", "pre_ps", "base0"))
    lt, cnt_ps, base, look_ps = (m.sem(f"{tag}_{s}") for s in ("lt", "cnt_ps", "base", "look_ps"))
    ranked, looked = m.sem(f"{tag}_ranked"), m.sem(f"{tag}_looked")
    vec, place = m.sem(f"{tag}_vec"), m.sem(f"{tag}_place")
    root_in, root = m.sem(f"{tag}_root_in"), m.sem(f"{tag}_root")
    rows4 = ET // 4
    ident4 = k.ident[:].unsqueeze(1).to_broadcast([P, 4, P])

    def spread_out(dve, n):
        q, which = divmod(n, 2)
        dve.wait_ge(row_ps, n + 1)
        span = slice(q * 4 * P, (q + 1) * 4 * P)
        if which == 0:
            nc.vector.tensor_copy(w.keyrow[:, span], w.ps_row[0][:]).then_inc(row_out, 1)
        else:
            nc.vector.tensor_scalar(w.hot_loT[:, span], w.ps_row[1][:], k.part[:, 0:1], None,
                                    ALU.is_equal).then_inc(row_out, 1)

    with nc.Block() as block:
        @block.sync
        def _(sp):
            sp.wait_ge(filled, 1)
            sp.dma_start(w.key[0:m.EP, :], key_dram.rearrange("(p t) -> p t", t=ET)).then_inc(loaded, 16)

        @block.vector
        def _(dve):
            v = Steps(dve, vec)
            nc.vector.memset(w.key[:], m.NPAD - 1).then_inc(filled, 1)
            dve.wait_ge(loaded, 16)
            v.link(nc.vector.tensor_scalar(w.tmp[:], w.key[:], 9, 2, ALU.logical_shift_right, ALU.logical_shift_left))
            v.link(nc.vector.tensor_scalar(w.tmp2[:], w.key[:], 3, None, ALU.bitwise_and))
            v.link(nc.vector.tensor_tensor(w.tmp[:], w.tmp[:], w.tmp2[:], ALU.bitwise_or))
            v.link(nc.vector.tensor_copy(w.colf[:], w.tmp[:]))
            v.link(nc.vector.tensor_scalar(w.tmp[:], w.key[:], 2, P - 1, ALU.logical_shift_right, ALU.bitwise_and))
            v.link(nc.vector.tensor_copy(w.lof[:], w.tmp[:]))
            v.link(nc.vector.tensor_copy(w.keyf[:], w.key[:]))
            nc.vector.tensor_tensor(w.hot_col[:], k.count[:, 0:NC].unsqueeze(1).to_broadcast([P, ET, NC]),
                                    w.colf[:].unsqueeze(2).to_broadcast([P, ET, NC]), ALU.is_equal).then_inc(hot, 1)
            nc.vector.tensor_tensor(w.hot_lo[:], k.count[:].unsqueeze(1).to_broadcast([P, ET, P]),
                                    w.lof[:].unsqueeze(2).to_broadcast([P, ET, P]), ALU.is_equal).then_inc(hot, 1)
            for q in range(rows4):
                for which, src in enumerate((w.keyf, w.lof)):
                    n = 2 * q + which
                    if n >= 2:
                        dve.wait_ge(row_ps, n - 1)
                    nc.vector.tensor_tensor(w.diag[n % 2][:], ident4,
                                            src[:, 4 * q:4 * q + 4].unsqueeze(2).to_broadcast([P, 4, P]),
                                            ALU.mult).then_inc(diag, 1)
                    if n >= 1:
                        spread_out(dve, n - 1)
            spread_out(dve, 2 * rows4 - 1)
            dve.wait_ge(counted, 1)
            cnt4 = w.cnt[:].rearrange("p (b j) -> p b j", j=4)
            v.link(nc.vector.tensor_copy(w.cnt[:], w.ps_cnt[:, 0:NC]))
            v.link(nc.vector.tensor_reduce(w.rowsum[:], cnt4, axis=AX.X, op=ALU.add))
            nc.vector.tensor_copy(w.rowsum2[:], w.rowsum[:]).then_inc(pre_in, 1)
            dve.wait_ge(pre_ps, 1)
            v.link(nc.vector.tensor_copy(w.pre[:], w.ps_pre[:, 0:2 * m.NB]))
            total = w.pre[:, m.NB:2 * m.NB]
            v.link(nc.vector.tensor_tensor_scan(w.scan[:], k.ones[:, 0:m.NB], total, 0.0, ALU.mult, ALU.add))
            v.link(nc.vector.tensor_tensor(w.scan[:], w.scan[:], total, ALU.subtract))
            start4 = w.base[0][:].rearrange("p (b j) -> p b j", j=4)
            v.link(nc.vector.tensor_tensor(start4[:, :, 0], w.pre[:, 0:m.NB], w.scan[:], ALU.add))
            for j in range(1, 4):
                v.link(nc.vector.tensor_tensor(start4[:, :, j], start4[:, :, j - 1], cnt4[:, :, j - 1], ALU.add))
            v.link(nc.vector.tensor_tensor(w.end[:], w.base[0][:], w.cnt[:], ALU.add))
            v.link(nc.vector.tensor_scalar(w.has[:], w.cnt[:], 0.0, None, ALU.is_gt))
            if table is not None:
                v.link(nc.vector.tensor_scalar(w.tmpn[:], w.has[:], -float(SKIP), float(SKIP) - 1.0, ALU.mult, ALU.add))
                v.link(nc.vector.tensor_tensor(w.tmpn[:], w.tmpn[:], w.end[:], ALU.add))
                nc.vector.tensor_copy(table.row[:], w.tmpn[:]).then_inc(root_in, 1)
                dve.wait_ge(root, 1)
                v.link(nc.vector.reciprocal(table.dinv[:], w.tmpn2[:]))
                for dst, a in ((table.self_w, table.dinv), (table.edge_w, w.has)):
                    v.link(nc.vector.tensor_tensor(dst[:], a[:], table.dinv[:], ALU.mult))
            nc.vector.memset(w.rank[:], 0.0).then_inc(base0, 1)
            dve.wait_ge(base0, 1)
            dve.wait_ge(hot, 2)
            dve.wait_ge(row_out, 2 * rows4)

            def body(t):
                if t.runs(0):
                    b, r = t.block(), t.slot(0, 4)
                    dve.wait_ge(cnt_ps, b + 1)
                    ge(dve, base, b)
                    ge(dve, look_ps, b - 2)
                    nc.vector.tensor_tensor(w.base[t.slot(1, 4)][:], w.base[r][:], w.ps_new[r % 2][:, 0:NC],
                                            ALU.add).then_inc(base, 1)
                    ge(dve, ranked, b)
                    nc.vector.scalar_tensor_tensor(w.junk[:], w.keyrow[:, bass.ds(b * P, P)], w.keyf[:, bass.ds(b, 1)],
                                                   k.after[:], ALU.is_equal, ALU.mult,
                                                   accum_out=w.rank[:, bass.ds(b, 1)]).then_inc(ranked, 1)
                if t.runs(-1):
                    b, r = t.block(-1), t.slot(-1, 4)
                    dve.wait_ge(look_ps, b + 1)
                    ge(dve, looked, b)
                    nc.vector.scalar_tensor_tensor(w.junk2[:], w.ps_look[r % 2][:, 0:NC], 1.0,
                                                   w.hot_col[:, bass.ds(b, 1), :].rearrange("p a c -> p (a c)"),
                                                   ALU.mult, ALU.mult, accum_out=w.pos[:, bass.ds(b, 1)]).then_inc(looked, 1)
            turns(dve, body, 0, ET, 4, ET // 4 - 2, ET)
            dve.wait_ge(looked, ET)
            dve.wait_ge(ranked, ET)
            v.link(nc.vector.tensor_tensor(w.pos[:], w.pos[:], w.rank[:], ALU.add))
            nc.vector.tensor_copy(places[:], w.pos[:]).then_inc(place, 1)
            dve.wait_ge(place, 1)

        @block.tensor
        def _(pe):
            def count(out, t, start, stop):
                return nc.tensor.matmul(out, w.hot_lo[:, bass.ds(t, 1), :].rearrange("p a c -> p (a c)"),
                                        w.hot_col[:, bass.ds(t, 1), :].rearrange("p a c -> p (a c)"),
                                        start=start, stop=stop)
            pe.wait_ge(hot, 2)
            for n in range(2 * rows4):
                pe.wait_ge(diag, n + 1)
                if n >= 2:
                    pe.wait_ge(row_out, n - 1)
                nc.tensor.matmul(w.ps_row[n % 2][:], k.ones[:], w.diag[n % 2][:].rearrange("p a b -> p (a b)"),
                                 start=True, stop=True).then_inc(row_ps, 1)
                for t in (2 * n, 2 * n + 1):
                    c = count(w.ps_cnt[:, 0:NC], t, t == 0, t == ET - 1)
            c.then_inc(counted, 1)
            pe.wait_ge(pre_in, 1)
            nc.tensor.matmul(w.ps_pre[:, 0:m.NB], k.before[:], w.rowsum2[:], start=True, stop=True)
            nc.tensor.matmul(w.ps_pre[:, m.NB:2 * m.NB], k.ones[:], w.rowsum2[:], start=True, stop=True).then_inc(pre_ps, 1)

            def body(t):
                if t.runs(1):
                    b, q = t.block(1), t.slot(1, 2)
                    ge(pe, base, b - 1)
                    count(w.ps_new[q][:, 0:NC], b, True, True).then_inc(cnt_ps, 1)
                if t.runs(0):
                    b, r = t.block(), t.slot(0, 4)
                    pe.wait_ge(lt, b + 1)
                    ge(pe, base, b)
                    ge(pe, looked, b - 1)
                    nc.tensor.matmul(w.ps_look[r % 2][:, 0:NC], w.lt[r][:], w.base[r][:], start=True, stop=True).then_inc(look_ps, 1)
            pe.wait_ge(base0, 1)
            turns(pe, body, -1, ET - 1, 4, ET // 4 - 2, ET)

        @block.scalar
        def _(act):
            if table is not None:
                act.wait_ge(root_in, 1)
                nc.scalar.activation(w.tmpn2[:], w.cnt[:], ACT.Sqrt, bias=k.ones[:, 0:1]).then_inc(root, 1)
            act.wait_ge(row_out, 2 * rows4)

            def body(t):
                b, r = t.block(), t.slot(0, 4)
                ge(act, look_ps, b - 3)
                nc.scalar.copy(w.lt[r][:], w.hot_loT[:, bass.ds(b * P, P)]).then_inc(lt, 1)
            turns(act, body, 0, ET - 1, 4, ET // 4 - 2, ET)

        @block.gpsimd
        def _(pool):
            if earlier is not None:
                def body(t):
                    earlier.step(pool, t.block(), t.slot(0, 4), t.slot(1, 4), t.round(1, 4), t.runs(1))
                earlier.begin(m, pool)
                turns(pool, body, 0, ET - 1, 4, ET // 4 - 2, ET)
                earlier.finish(pool)


class Scatter:

    def __init__(self, m, tag, payload, width, place, bufs, sorted_dram):
        self.m, self.tag, self.payload, self.width, self.place, self.dram = m, tag, payload, width, place, sorted_dram
        self.idx, self.rows = bufs

    def begin(self, m, pool):
        self.staged = m.sem(f"{self.tag}_staged")
        self.sent = [m.sem(f"{self.tag}_sent{r}") for r in range(4)]
        self.fill(0, 0)

    def fill(self, t, r):
        nc = self.m.nc
        nc.gpsimd.tensor_copy(self.idx[r][:], self.place[:, bass.ds(t, 1)]).then_inc(self.staged, 1)
        nc.gpsimd.tensor_copy(self.rows[r][:, 0:self.width],
                              self.payload[:, bass.ds(t, 1), 0:self.width].rearrange("p a w -> p (a w)")).then_inc(self.staged, 1)

    def step(self, pool, t, r, r_next, uses, more):
        ge(pool, self.staged, 2 * (t + 1))
        if more:
            ge(pool, self.sent[r_next], 16 * uses)
            self.fill(t + 1, r_next)
        pool.indirect_dma_start(self.dram, bass.IndirectOffsetOnAxis(ap=self.idx[r][:, 0:1], axis=0),
                                self.rows[r][:, 0:self.width], None).then_inc(self.sent[r], 16)

    def pair(self, pool, t, off):
        for h in range(2):
            n = 2 * (t.s + off) + h
            last = isinstance(t.group, int) and n == self.m.ET - 1
            self.step(pool, 2 * t.block(off) + h, n % 4, (n + 1) % 4, 2 * t.group + (n + 1) // 4, not last)

    def finish(self, pool):
        for r in range(4):
            ge(pool, self.sent[r], 16 * (self.m.ET // 4))


class Turn:

    def __init__(self, group, s, last, size):
        self.group, self.s, self.last, self.size = group, s, last, size

    def block(self, off=0):
        return self.group * self.size + (self.s + off)

    def slot(self, off, ring):
        return (self.s + off) % ring

    def round(self, off, ring):
        return self.group * (self.size // ring) + (self.s + off) // ring

    def runs(self, off):
        return not isinstance(self.group, int) or 0 <= self.block(off) <= self.last


def turns(engine, body, first, last, loop_from, loop_groups, blocks, size=4):
    for b in range(first, loop_from):
        body(Turn(0, b, blocks - 1, size))
    with engine.Fori(0, loop_groups) as g:
        for u in range(size):
            body(Turn(g, loop_from + u, blocks - 1, size))
    for b in range(loop_from + size * loop_groups, last + 1):
        body(Turn(0, b, blocks - 1, size))


def ge(engine, sem, value):
    if not isinstance(value, int) or value > 0:
        engine.wait_ge(sem, value)


@stage
def sorted_edges(m, k, tag, sorted_dram, width, key_word, rows, skey, sbuf):
    nc, ET = m.nc, m.ET
    loaded, vec, diag, out_ps, out = (m.sem(f"{tag}_{s}") for s in ("re_loaded", "re_vec", "re_diag", "re_ps", "re_out"))
    ident4 = k.ident[:].unsqueeze(1).to_broadcast([P, 4, P])
    w = k.sort
    with nc.Block() as block:
        @block.sync
        def _(sp):
            sp.dma_start(sbuf[:, :, 0:width], sorted_dram.rearrange("(t p) w -> p t w", p=P)).then_inc(loaded, 16)

        @block.vector
        def _(dve):
            v = Steps(dve, vec)
            dve.wait_ge(loaded, 16)
            v.link(nc.vector.tensor_copy(skey[:], sbuf[:, :, key_word]))
            for q in range(ET // 4):
                ge(dve, out_ps, q - 1)
                nc.vector.tensor_tensor(w.diag[q % 2][:], ident4,
                                        skey[:, 4 * q:4 * q + 4].unsqueeze(2).to_broadcast([P, 4, P]),
                                        ALU.mult).then_inc(diag, 1)

        @block.tensor
        def _(pe):
            for q in range(ET // 4):
                pe.wait_ge(diag, q + 1)
                ge(pe, out, q - 1)
                nc.tensor.matmul(w.ps_row[q % 2][:], k.ones[:], w.diag[q % 2][:].rearrange("p a b -> p (a b)"),
                                 start=True, stop=True).then_inc(out_ps, 1)

        @block.scalar
        def _(act):
            for q in range(ET // 4):
                act.wait_ge(out_ps, q + 1)
                nc.scalar.copy(rows[:, q * 4 * P:(q + 1) * 4 * P], w.ps_row[q % 2][:]).then_inc(out, 1)
            act.wait_ge(out, ET // 4)


def edge_tables(m, k, dinv_dram, sorted_dram):
    nc, ET = m.nc, m.ET
    e = k.edge
    stored, loaded, staged, vec = (m.sem(f"edge_{s}") for s in ("stored", "loaded", "staged", "vec"))
    got = [m.sem(f"edge_got{q}") for q in range(4)]
    kept, srcs = m.sem("edge_kept"), m.sem("edge_srcs")

    def sync(sp):
        sp.dma_start(dinv_dram.rearrange("(b p j) o -> p b (j o)", p=P, j=4),
                     k.node.dinv[:].rearrange("p (b j) -> p b j", j=4)).then_inc(stored, 16)
        sp.dma_start(e.tiles[:], sorted_dram.rearrange("(t p) w -> t (p w)", p=P)).then_inc(loaded, 16)
        sp.wait_ge(stored, 16)

    def gpsimd(pool):
        nc.gpsimd.tensor_scalar(e.src[:], e.pair[:, :, 0], m.N - 1, None, ALU.min).then_inc(srcs, 1)
        ge(pool, srcs, 1)
        ge(pool, stored, 16)

        def body(t):
            b, r = t.block(), t.slot(0, 4)
            ge(pool, staged, b + 1)
            ge(pool, kept, b - 2)
            if t.runs(1):
                nc.gpsimd.tensor_copy(e.idx[t.slot(1, 4)][:], e.src[:, bass.ds(b + 1, 1)]).then_inc(staged, 1)
            pool.indirect_dma_start(e.val[r][:], None, dinv_dram,
                                    bass.IndirectOffsetOnAxis(ap=e.idx[r][:, 0:1], axis=0)).then_inc(got[r], 16)
        nc.gpsimd.tensor_copy(e.idx[0][:], e.src[:, 0:1]).then_inc(staged, 1)
        turns(pool, body, 0, ET - 1, 4, ET // 4 - 2, ET)
        ge(pool, kept, ET)

    def vector(dve):
        v = Steps(dve, vec)
        for q in range(2):
            v.link(nc.vector.memset(k.Cb[q][:], 0.0))
        dve.wait_ge(loaded, 16)
        keys = e.tiles[:].rearrange("t (p w) -> t p w", w=2)[:, :, 1]
        v.link(nc.vector.tensor_copy(e.tkey[:], keys))
        v.link(nc.vector.tensor_scalar(e.tjunk[:], e.tkey[:], e.tkey[:, 0:1], 0.0, ALU.is_equal, ALU.add,
                                       accum_out=e.run[:]))
        v.link(nc.vector.tensor_scalar(e.run2[:], k.part[0:ET, 0:1], float(P), -1.0, ALU.mult, ALU.add))
        v.link(nc.vector.tensor_tensor(e.run2[:], e.run2[:], e.run[:], ALU.add))
        v.link(nc.vector.tensor_copy(e.fix_row[:], e.run2[:]))
        firsts = e.rows[0:ET, :].rearrange("q (t p) -> q t p", p=P)[:, :, 0]
        v.link(nc.vector.tensor_scalar(e.lacks[:], firsts, e.tkey[:, P - 1:P], None, ALU.is_equal))
        v.link(nc.vector.tensor_tensor(e.lacks[:], e.lacks[:], k.before[0:ET, 0:ET], ALU.mult))

        def keep(t):
            dve.wait_ge(got[t.slot(0, 4)], 16 * (t.round(0, 4) + 1))
            nc.vector.tensor_copy(e.dsrc[:, bass.ds(t.block(), 1)], e.val[t.slot(0, 4)][:]).then_inc(kept, 1)
        turns(dve, keep, 0, ET - 1, 4, ET // 4 - 2, ET)
        dve.wait_ge(kept, ET)

    def scalar(act):
        act.wait_ge(kept, ET)

    def tensor(pe):
        pass

    return Part(sync, gpsimd, vector, scalar, tensor)


def prepare(m, k, layer, w_dram):
    nc, C, tag = m.nc, m.C, f"prep{layer}"
    loaded, tps, hi, lo = (m.sem(f"{tag}_{s}") for s in ("loaded", "tps", "hi", "lo"))
    vec, var, root, diag, spread, out = (m.sem(f"{tag}_{s}") for s in ("vec", "var", "root", "diag", "spread", "out"))
    raw = k.R[0][:].rearrange("p (c f) -> p c f", c=C)
    stats, weights = layer > 0, w_dram is not None
    s = k.bn

    def gpsimd(pool):
        pass

    def sync(sp):
        if weights:
            sp.dma_start(raw, w_dram[layer].rearrange("(c p) f -> p c f", p=P)).then_inc(loaded, 16)

    def tensor(pe):
        if weights:
            pe.wait_ge(loaded, 16)
            for q in range(C):
                ge(pe, lo, q - 1)
                for c in range(C):
                    t = nc.tensor.transpose(k.ps_a[q % 2][:, c * P:(c + 1) * P], raw[:, c, q * P:(q + 1) * P], k.ident[:])
                t.then_inc(tps, 1)
        if stats:
            for i in range(2):
                pe.wait_ge(diag, i + 1)
                nc.tensor.matmul(k.ps_b[i][:], k.ones[:], k.R[1 + i][:, 0:m.D], start=True, stop=True).then_inc(spread, 1)

    def scalar(act):
        if stats:
            act.wait_ge(var, 1)
            nc.scalar.activation(s.std[:], s.mv[:, :, 1], ACT.Sqrt, bias=k.eps[:, 0:1]).then_inc(root, 1)
        if weights:
            for q in range(C):
                act.wait_ge(tps, q + 1)
                nc.scalar.copy(k.whi[:, q, :], k.ps_a[q % 2][:]).then_inc(hi, 1)
        if stats:
            for i, dst in enumerate((k.scale, k.shift)):
                act.wait_ge(spread, i + 1)
                nc.scalar.copy(dst[:], k.ps_b[i][:]).then_inc(out, 1)
            act.wait_ge(out, 2)

    def vector(dve):
        v = Steps(dve, vec)
        if stats:
            prm = k.param[:, :, (layer - 1) * C:layer * C]
            for c in range(C):
                last = nc.vector.bn_aggr(s.mv[:, c, :], k.stat[:, c, :])
                last.then_inc(var if c == C - 1 else vec, 1)
            v.n = C - 1
            dve.wait_ge(vec, C - 1)
            dve.wait_ge(var, 1)
            v.link(nc.vector.tensor_tensor(s.mean[:], s.mv[:, :, 0], prm[:, 0, :], ALU.add))
            v.link(nc.vector.tensor_tensor(s.mean[:], prm[:, 0, :], s.mean[:], ALU.subtract))
            dve.wait_ge(root, 1)
            v.link(nc.vector.reciprocal(s.scale[:], s.std[:]))
            v.link(nc.vector.tensor_tensor(s.scale[:], s.scale[:], prm[:, 1, :], ALU.mult))
            v.link(nc.vector.tensor_tensor(s.shift[:], s.scale[:], s.mean[:], ALU.mult))
            v.link(nc.vector.tensor_tensor(s.shift[:], s.shift[:], prm[:, 2, :], ALU.add))
            for i, col in enumerate((s.scale, s.shift)):
                nc.vector.tensor_tensor(k.R[1 + i][:, 0:m.D].rearrange("p (c f) -> p c f", c=C),
                                        k.ident[:].unsqueeze(1).to_broadcast([P, C, P]),
                                        col[:].unsqueeze(2).to_broadcast([P, C, P]), ALU.mult).then_inc(diag, 1)
        if weights:
            for q in range(C):
                dve.wait_ge(hi, q + 1)
                nc.vector.tensor_tensor(k.wlo[:, q, :], k.ps_a[q % 2][:], k.whi[:, q, :].bitcast(F32),
                                        ALU.subtract).then_inc(lo, 1)
            dve.wait_ge(lo, C)

    part = Part(sync, gpsimd, vector, scalar, tensor)
    part.read, part.spread, part.out, part.lo = tps, spread, out, lo
    return part


def merge(m, k, layer, table, merged_dram, ready):
    nc, ET, D, tag = m.nc, m.ET, m.D, f"merge{layer}"
    e, norm, RING = k.edge, layer > 0, 8
    staged, scaled, shifted, weighted, sel = (m.sem(f"{tag}_{s}") for s in ("staged", "scaled", "shifted", "weighted", "sel"))
    merged, copied = m.sem(f"{tag}_merged"), m.sem(f"{tag}_copied")
    got = [m.sem(f"{tag}_got{r}") for r in range(RING)]
    put = [m.sem(f"{tag}_put{r}") for r in range(4)]
    lasts, lacking, fix_ps, fixed, sent = (m.sem(f"{tag}_{s}") for s in ("lasts", "lacking", "fix_ps", "fixed", "sent"))
    m_rows = merged_dram.rearrange("(t p) f -> t p f", p=P)
    G = [a[:, c, :] for a in k.aggT for c in range(m.C)]
    O = [k.rows_out[r // 2][:, (r % 2) * D:(r % 2 + 1) * D] for r in range(4)]
    last_rows, fix = k.Cb[0][0:ET, 0:D], k.Cb[1][0:ET, 0:D]
    group = ET // 4

    def run(engine, body, extra=0):
        turns(engine, body, 0, ET - 1 + extra, 8, ET // 8 - 2, ET, 8)

    def gpsimd(pool):
        def body(t):
            b, r = t.block(), t.slot(0, RING)
            ge(pool, staged, b + 1)
            ge(pool, merged, b - RING + 2)
            if t.runs(1):
                nc.gpsimd.tensor_copy(e.idx[t.slot(1, RING)][:], e.src[:, bass.ds(t.block(1), 1)]).then_inc(staged, 1)
            pool.indirect_dma_start(G[r], None, table,
                                    bass.IndirectOffsetOnAxis(ap=e.idx[r][:, 0:1], axis=0)).then_inc(got[r], 16)
        nc.gpsimd.tensor_copy(e.idx[0][:], e.src[:, 0:1]).then_inc(staged, 1)
        run(pool, body)

    def mend(pool):
        for r in range(4):
            ge(pool, put[r], 16 * group)
        pool.indirect_dma_start(fix, None, merged_dram,
                                bass.IndirectOffsetOnAxis(ap=e.fix_row[:, 0:1], axis=0)).then_inc(lasts, 16)
        ge(pool, fixed, 1)
        pool.indirect_dma_start(merged_dram, bass.IndirectOffsetOnAxis(ap=e.fix_row[:, 0:1], axis=0),
                                fix, None).then_inc(sent, 16)
        ge(pool, sent, 16)

    def vector(dve):
        def body(t):
            b, r = t.block(), t.slot(0, RING)
            if norm:
                dve.wait_ge(got[r], 16 * (t.round(0, RING) + 1))
                nc.vector.tensor_tensor(G[r], G[r], k.scale[:], ALU.mult).then_inc(scaled, 1)
            ge(dve, merged, b - 1)
            nc.vector.tensor_scalar(e.same[r % 2][:], e.rows[:, bass.ds(b * P, P)], e.skey[:, bass.ds(b, 1)],
                                    None, ALU.is_equal).then_inc(sel, 1)
            if norm:
                dve.wait_ge(scaled, b + 1)
                nc.vector.tensor_tensor(G[r], G[r], k.shift[:], ALU.add).then_inc(shifted, 1)
        if norm:
            dve.wait_ge(ready.out, 2)
        run(dve, body)

    def mend_rows(dve):
        dve.wait_ge(fix_ps, 1)
        dve.wait_ge(lasts, 16)
        nc.vector.tensor_tensor(fix, fix, k.ps_b[0][0:ET, :], ALU.add).then_inc(fixed, 1)

    def scalar(act):
        def body(t):
            if t.runs(0):
                b, r = t.block(), t.slot(0, RING)
                if norm:
                    act.wait_ge(shifted, b + 1)
                else:
                    act.wait_ge(got[r], 16 * (t.round(0, RING) + 1))
                nc.scalar.activation(G[r], G[r], ACT.Relu if norm else ACT.Copy,
                                     scale=e.dsrc[:, bass.ds(b, 1)]).then_inc(weighted, 1)
            if t.runs(-1):
                b, r = t.block(-1), t.slot(-1, 4)
                act.wait_ge(merged, b + 1)
                ge(act, put[r], 16 * t.round(-1, 4))
                nc.scalar.copy(O[r], k.ps_a[r % 2][:]).then_inc(copied, 1)
        run(act, body, 1)

    def tensor(pe):
        def body(t):
            b, r = t.block(), t.slot(0, RING)
            pe.wait_ge(weighted, b + 1)
            pe.wait_ge(sel, b + 1)
            ge(pe, copied, b - 1)
            nc.tensor.matmul(k.ps_a[r % 2][:], e.same[r % 2][:], G[r], start=True, stop=True).then_inc(merged, 1)
        pe.wait_ge(ready.lo, m.C)
        if norm:
            pe.wait_ge(ready.out, 2)
        run(pe, body)
        pe.wait_ge(lacking, 16)
        nc.tensor.matmul(k.ps_b[0][0:ET, :], e.lacks[:], last_rows, start=True, stop=True).then_inc(fix_ps, 1)

    def sync(sp):
        def body(t):
            b, r = t.block(), t.slot(0, 4)
            sp.wait_ge(copied, b + 1)
            sp.dma_start(at(m_rows, b), O[r]).then_inc(put[r], 16)
        run(sp, body)
        for r in range(4):
            sp.wait_ge(put[r], 16 * group)
        sp.dma_start(last_rows, m_rows[:, P - 1, :]).then_inc(lacking, 16)
        sp.wait_ge(lacking, 16)

    part = Part(sync, gpsimd, vector, scalar, tensor)
    part.mend, part.mend_rows, part.copied, part.put = mend, mend_rows, copied, put
    return part


def dense(m, k, layer, table, out_table, merged_dram, scatter, ready, merging):
    nc, C, D, NB, tag = m.nc, m.C, m.D, m.NB, f"dense{layer}"
    norm = layer > 0
    n = k.node
    scaled, shifted, weighted, joined = (m.sem(f"{tag}_{s}") for s in ("scaled", "shifted", "weighted", "joined"))
    turned, hi, lo, product = (m.sem(f"{tag}_{s}") for s in ("turned", "hi", "lo", "product"))
    copied, counted, back, rows = (m.sem(f"{tag}_{s}") for s in ("copied", "counted", "back", "rows"))
    staged = m.sem(f"{tag}_staged")
    read = [m.sem(f"{tag}_read{r}") for r in range(4)]
    got = [m.sem(f"{tag}_got{r}") for r in range(2)]
    put = [m.sem(f"{tag}_put{r}") for r in range(2)]
    src = block_rows(table[0:(NB - 1) * m.BLK, :], m) if layer == 0 else block_rows(table, m)
    dst = block_rows(out_table, m)
    quarter = [slice(j * D, (j + 1) * D) for j in range(4)]

    def run(engine, body):
        turns(engine, body, -4, NB, 4, (NB - 8) // 4, NB)

    def preload(sp):
        sp.wait_ge(ready.read, C)
        if norm:
            sp.wait_ge(ready.spread, 2)
        for b in range(4):
            sp.dma_start(k.R[b][:], src[b]).then_inc(read[b], 16)

    def sync(sp):
        def body(t):
            if t.runs(4) and (not isinstance(t.group, int) or t.block() >= 0):
                r = t.slot(4, 4)
                ge(sp, turned, 4 * (t.block() + 1))
                if layer == 0 and isinstance(t.group, int) and t.block(4) == NB - 1:
                    sp.dma_start(k.R[r][0:m.TP, :], table[(NB - 1) * m.BLK:m.N, :]
                                 .rearrange("(p j) f -> p (j f)", j=4)).then_inc(read[r], 16)
                else:
                    sp.dma_start(k.R[r][:], at(src, t.block(4))).then_inc(read[r], 16)
            if t.runs(-1):
                q = t.slot(-1, 2)
                sp.wait_ge(rows, 4 * (t.block(-1) + 1))
                sp.dma_start(at(dst, t.block(-1)), k.rows_out[q][:]).then_inc(put[q], 16)
        turns(sp, body, 0, NB, 4, (NB - 12) // 4, NB)
        for q in range(2):
            sp.wait_ge(put[q], 16 * (NB // 2))

    def gpsimd(pool):
        def shift(t):
            r = t.slot(3, 4)
            for j in range(4):
                ge(pool, scaled, 4 * t.block(3) + j + 1)
                nc.gpsimd.tensor_tensor(k.R[r][:, quarter[j]], k.R[r][:, quarter[j]], k.shift[:],
                                        ALU.add).then_inc(shifted, 1)

        def body(t):
            if not t.runs(3):
                return
            b, q = t.block(3), t.slot(3, 2)
            first = isinstance(t.group, int) and b == 0
            if first and norm:
                shift(t)
            if first:
                merging.mend(pool)
            ge(pool, staged, b + 1)
            ge(pool, joined, 4 * (b - 1))
            if t.runs(4):
                nc.gpsimd.tensor_copy(n.idx[t.slot(4, 4)][:], n.row[:, bass.ds(4 * (b + 1), 4)]).then_inc(staged, 1)
            for j in range(4):
                pool.indirect_dma_start(k.Cb[q][:, quarter[j]], None, merged_dram,
                                        bass.IndirectOffsetOnAxis(ap=n.idx[t.slot(3, 4)][:, j:j + 1], axis=0),
                                        bounds_check=m.EPAD - 1, oob_is_err=False).then_inc(got[q], 16)
            if norm and not first:
                shift(t)
            if scatter is not None:
                scatter.pair(pool, t, 3)
        nc.gpsimd.tensor_copy(n.idx[0][:], n.row[:, 0:4]).then_inc(staged, 1)
        if scatter is not None:
            scatter.begin(m, pool)
        run(pool, body)
        if scatter is not None:
            scatter.finish(pool)

    def vector(dve):
        def body(t):
            if isinstance(t.group, int) and t.s == -2:
                merging.mend_rows(dve)
            for j in range(4):
                if t.runs(1):
                    b, q = t.block(1), t.slot(1, 2)
                    dve.wait_ge(hi, 4 * b + j + 1)
                    nc.vector.tensor_tensor(k.ylo[q][:, :, j * P:(j + 1) * P],
                                            k.ps_a[j % 2][:].rearrange("p (c n) -> p c n", c=C),
                                            k.yhi[q][:, :, j * P:(j + 1) * P].bitcast(F32),
                                            ALU.subtract).then_inc(lo, 1)
                if norm and t.runs(3):
                    r = t.slot(3, 4)
                    if j == 0:
                        dve.wait_ge(read[r], 16 * (t.round(3, 4) + 1))
                    nc.vector.tensor_tensor(k.R[r][:, quarter[j]], k.R[r][:, quarter[j]], k.scale[:],
                                            ALU.mult).then_inc(scaled, 1)
                if t.runs(2):
                    b, r, q = t.block(2), t.slot(2, 4), t.slot(2, 2)
                    if j == 0:
                        dve.wait_ge(got[q], 64 * (t.round(2, 2) + 1))
                    dve.wait_ge(weighted, 4 * b + j + 1)
                    nc.vector.scalar_tensor_tensor(k.R[r][:, quarter[j]], k.Cb[q][:, quarter[j]],
                                                   n.edge_w[:, bass.ds(4 * b + j, 1)], k.R[r][:, quarter[j]],
                                                   ALU.mult, ALU.add).then_inc(joined, 1)
                if t.runs(0):
                    b = t.block()
                    dve.wait_ge(copied, 4 * b + j + 1)
                    view = k.aggT[t.slot(0, 2)][:, j, :]
                    if isinstance(t.group, int) and b == NB - 1:
                        view = view.rearrange("p (j n) -> p j n", j=4)[:, :, 0:m.TP]
                    nc.vector.bn_stats(k.stat[:, j, bass.ds(6 * b, 6)], view).then_inc(counted, 1)
        run(dve, body)
        dve.wait_ge(counted, 4 * NB)

    def scalar(act):
        def body(t):
            for j in range(4):
                if t.runs(1):
                    b, q = t.block(1), t.slot(1, 2)
                    act.wait_ge(turned, 4 * b + j + 1)
                    ge(act, product, 4 * (b - 1))
                    nc.scalar.copy(k.yhi[q][:, :, j * P:(j + 1) * P],
                                   k.ps_a[j % 2][:].rearrange("p (c n) -> p c n", c=C)).then_inc(hi, 1)
                if t.runs(2):
                    b, r = t.block(2), t.slot(2, 4)
                    if norm:
                        act.wait_ge(shifted, 4 * b + j + 1)
                    else:
                        act.wait_ge(read[r], 16 * (t.round(2, 4) + 1))
                    nc.scalar.activation(k.R[r][:, quarter[j]], k.R[r][:, quarter[j]],
                                         ACT.Relu if norm else ACT.Copy,
                                         scale=n.self_w[:, bass.ds(4 * b + j, 1)]).then_inc(weighted, 1)
                if t.runs(0):
                    b, q = t.block(), t.slot(0, 2)
                    act.wait_ge(product, 4 * b + j + 1)
                    ge(act, back, 4 * (b - 1))
                    ge(act, counted, 4 * (b - 1))
                    nc.scalar.copy(k.aggT[q][:, j, :], k.ps_b[j % 2][:]).then_inc(copied, 1)
                if t.runs(-1):
                    b, q = t.block(-1), t.slot(-1, 2)
                    act.wait_ge(back, 4 * b + j + 1)
                    if isinstance(t.group, int) and b == 0 and j == 0:
                        for p in merging.put:
                            act.wait_ge(p, 16 * (m.ET // 4))
                    ge(act, put[q], 16 * t.round(-1, 2))
                    nc.scalar.copy(k.rows_out[q][:, quarter[j]], k.ps_c[j % 2][:]).then_inc(rows, 1)
        run(act, body)

    def tensor(pe):
        def body(t):
            for j in range(4):
                if t.runs(1):
                    b, r = t.block(1), t.slot(1, 4)
                    pe.wait_ge(joined, 4 * b + j + 1)
                    ge(pe, lo, 4 * b + j - 1)
                    for c in range(C):
                        i = nc.tensor.transpose(k.ps_a[j % 2][:, c * P:(c + 1) * P],
                                                k.R[r][:, j * D + c * P:j * D + (c + 1) * P], k.ident[:])
                    i.then_inc(turned, 1)
                if t.runs(0):
                    b, q = t.block(), t.slot(0, 2)
                    if j == 0:
                        pe.wait_ge(lo, 4 * (b + 1))
                    ge(pe, copied, 4 * b + j - 1)
                    parts = [(k.whi, k.yhi[q]), (k.whi, k.ylo[q]), (k.wlo, k.yhi[q])]
                    for c in range(C):
                        for i, (wt, y) in enumerate(parts):
                            mm = nc.tensor.matmul(k.ps_b[j % 2][:], wt[:, c, j * P:(j + 1) * P], y[:, c, :],
                                                  start=(c == 0 and i == 0), stop=(c == C - 1 and i == 2))
                    mm.then_inc(product, 1)
                if t.runs(-1):
                    b, q = t.block(-1), t.slot(-1, 2)
                    if j == 0:
                        pe.wait_ge(copied, 4 * (b + 1))
                    ge(pe, rows, 4 * b + max(j - 1, 0))
                    for c in range(C):
                        i = nc.tensor.transpose(k.ps_c[j % 2][:, c * P:(c + 1) * P],
                                                k.aggT[q][:, c, j * P:(j + 1) * P], k.ident[:])
                    i.then_inc(back, 1)
        pe.wait_ge(merging.copied, m.ET)
        run(pe, body)

    part = Part(sync, gpsimd, vector, scalar, tensor)
    part.preload = preload
    return part


class Part:

    def __init__(self, sync, gpsimd, vector, scalar, tensor):
        self.sync, self.gpsimd, self.vector, self.scalar, self.tensor = sync, gpsimd, vector, scalar, tensor


@stage
def layer_stage(m, k, layer, dinv_dram, by_dst, w_dram, table, out_table, merged_dram, scatter):
    tables = edge_tables(m, k, dinv_dram, by_dst) if layer == 0 else None
    ready = prepare(m, k, layer, w_dram)
    merging = merge(m, k, layer, table, merged_dram, ready)
    main = dense(m, k, layer, table, out_table, merged_dram, scatter, ready, merging)
    with m.nc.Block() as block:
        @block.sync
        def _(sp):
            if tables:
                tables.sync(sp)
            ready.sync(sp)
            main.preload(sp)
            merging.sync(sp)
            main.sync(sp)

        @block.gpsimd
        def _(pool):
            if tables:
                tables.gpsimd(pool)
            merging.gpsimd(pool)
            if layer > 0:
                pool.wait_ge(ready.out, 2)
            main.gpsimd(pool)

        @block.vector
        def _(dve):
            ready.vector(dve)
            if tables:
                tables.vector(dve)
            merging.vector(dve)
            main.vector(dve)

        @block.scalar
        def _(act):
            ready.scalar(act)
            if tables:
                tables.scalar(act)
            merging.scalar(act)
            main.scalar(act)

        @block.tensor
        def _(pe):
            ready.tensor(pe)
            merging.tensor(pe)
            main.tensor(pe)


@stage
def finish_gcn(m, k, n_layers, table, x_dram, x2_dram, out_dram, prep):
    nc, D, NB = m.nc, m.D, m.NB
    f = k.fin
    tag = "fin"
    scaled, shifted, relued, summed = (m.sem(f"{tag}_{s}") for s in ("scaled", "shifted", "relued", "summed"))
    moments, root1, small, var2, root2, ready = (m.sem(f"{tag}_{s}") for s in ("moments", "root1", "small", "var2", "root2", "ready"))
    normed, outed = m.sem(f"{tag}_normed"), m.sem(f"{tag}_outed")
    read = [m.sem(f"{tag}_read{r}") for r in range(4)]
    xread = [m.sem(f"{tag}_xread{r}") for r in range(2)]
    put = [m.sem(f"{tag}_put{r}") for r in range(2)]
    src, x2 = block_rows(table, m), block_rows(x2_dram, m)
    full = (NB - 1) * m.BLK
    x_full, out_full = block_rows(x_dram[0:full, :], m), block_rows(out_dram[0:full, :], m)
    x_tail, out_tail = (a[full:m.N, :].rearrange("(p j) f -> p (j f)", j=4) for a in (x_dram, out_dram))
    quarter = [slice(j * D, (j + 1) * D) for j in range(4)]

    def tail(t, off):
        return isinstance(t.group, int) and t.block(off) == NB - 1

    def run(engine, body):
        turns(engine, body, -4, NB - 1, 4, (NB - 8) // 4, NB)

    prep.begin()
    norm = prepare(m, k, n_layers, None)
    with nc.Block() as block:
        @block.sync
        def _(sp):
            for b in range(2):
                sp.dma_start(k.Cb[b][:], at(x_full, b)).then_inc(xread[b], 16)
            sp.wait_ge(norm.spread, 2)
            for b in range(4):
                sp.dma_start(k.R[b][:], at(src, b)).then_inc(read[b], 16)
            prep.load(sp)

            def body(t):
                if t.runs(2) and (not isinstance(t.group, int) or t.block() >= 0):
                    q = t.slot(2, 2)
                    ge(sp, summed, 4 * (t.block(2) - 1))
                    if tail(t, 2):
                        sp.dma_start(k.Cb[q][0:m.TP, :], x_tail).then_inc(xread[q], 16)
                    else:
                        sp.dma_start(k.Cb[q][:], at(x_full, t.block(2))).then_inc(xread[q], 16)
                if t.runs(4) and (not isinstance(t.group, int) or t.block() >= 0):
                    ge(sp, normed, 4 * (t.block() + 1))
                    sp.dma_start(k.R[t.slot(4, 4)][:], at(src, t.block(4))).then_inc(read[t.slot(4, 4)], 16)
            run(sp, body)
            for q in range(2):
                sp.wait_ge(put[q], 32 * (NB // 2))

        @block.gpsimd
        def _(pool):
            def body(t):
                if t.runs(3):
                    r = t.slot(3, 4)
                    for j in range(4):
                        ge(pool, scaled, 4 * t.block(3) + j + 1)
                        nc.gpsimd.tensor_tensor(k.R[r][:, quarter[j]], k.R[r][:, quarter[j]], k.shift[:],
                                                ALU.add).then_inc(shifted, 1)
            pool.wait_ge(norm.out, 2)
            run(pool, body)

        @block.vector
        def _(dve):
            prep.zero(dve)
            norm.vector(dve)
            dve.wait_ge(norm.out, 2)

            def body(t):
                prep.vector_early(dve, t)
                if t.runs(1):
                    b, q = t.block(1), t.slot(1, 2)
                    dve.wait_ge(root1, b + 1)
                    ge(dve, normed, 4 * (b - 1))
                    ge(dve, outed, 4 * (b - 1))
                    nc.vector.reciprocal(f.rstd[q][:], f.std[q][:]).then_inc(small, 1)
                    dve.wait_ge(small, 3 * b + 1)
                    nc.vector.scalar_tensor_tensor(f.nmr[q][:], f.mv[q][:, :, 0], -1.0, f.rstd[q][:],
                                                   ALU.mult, ALU.mult).then_inc(small, 1)
                    nc.vector.tensor_tensor(f.v2[q][:], f.mv[q][:, :, 1], f.rstd[q][:], ALU.mult).then_inc(small, 1)
                    dve.wait_ge(small, 3 * b + 3)
                    nc.vector.tensor_tensor(f.v2[q][:], f.v2[q][:], f.rstd[q][:], ALU.mult).then_inc(var2, 1)
                if t.runs(2):
                    b, r, q = t.block(2), t.slot(2, 4), t.slot(2, 2)
                    dve.wait_ge(xread[q], 16 * (t.round(2, 2) + 1))
                    for j in range(4):
                        dve.wait_ge(relued, 4 * b + j + 1)
                        nc.vector.tensor_tensor(k.R[r][:, quarter[j]], k.R[r][:, quarter[j]], k.Cb[q][:, quarter[j]],
                                                ALU.add).then_inc(summed, 1)
                    for j in range(4):
                        dve.wait_ge(summed, 4 * b + j + 1)
                        nc.vector.bn_stats(f.st[:, j, :], k.R[r][:, quarter[j]])
                    dve.drain()
                    for j in range(4):
                        nc.vector.bn_aggr(f.mv[q][:, j, :], f.st[:, j, :]).then_inc(moments, 1)
                if t.runs(1):
                    b, q = t.block(1), t.slot(1, 2)
                    dve.wait_ge(root2, b + 1)
                    nc.vector.reciprocal(f.rstd2[q][:], f.std2[q][:]).then_inc(ready, 1)
                if t.runs(3):
                    r = t.slot(3, 4)
                    dve.wait_ge(read[r], 16 * (t.round(3, 4) + 1))
                    for j in range(4):
                        nc.vector.tensor_tensor(k.R[r][:, quarter[j]], k.R[r][:, quarter[j]], k.scale[:],
                                                ALU.mult).then_inc(scaled, 1)
                prep.vector_late(dve, t)
            run(dve, body)
            prep.vector_end(dve)

        @block.scalar
        def _(act):
            norm.scalar(act)

            def body(t):
                prep.scalar_turn(act, t)
                if t.runs(1):
                    b, q = t.block(1), t.slot(1, 2)
                    act.wait_ge(moments, 4 * b + 4)
                    nc.scalar.activation(f.std[q][:], f.mv[q][:, :, 1], ACT.Sqrt, bias=k.eps[:, 0:1]).then_inc(root1, 1)
                if t.runs(2):
                    b, r = t.block(2), t.slot(2, 4)
                    for j in range(4):
                        act.wait_ge(shifted, 4 * b + j + 1)
                        nc.scalar.activation(k.R[r][:, quarter[j]], k.R[r][:, quarter[j]], ACT.Relu).then_inc(relued, 1)
                if t.runs(1):
                    b, q = t.block(1), t.slot(1, 2)
                    act.wait_ge(var2, b + 1)
                    nc.scalar.activation(f.std2[q][:], f.v2[q][:], ACT.Sqrt, bias=k.eps[:, 0:1]).then_inc(root2, 1)
                if t.runs(0):
                    b, r, q = t.block(), t.slot(0, 4), t.slot(0, 2)
                    act.wait_ge(ready, b + 1)
                    ge(act, put[q], 32 * t.round(0, 2))
                    for j in range(4):
                        nc.scalar.activation(k.rows_out[q][:, quarter[j]], k.R[r][:, quarter[j]], ACT.Identity,
                                             scale=f.rstd[q][:, j:j + 1], bias=f.nmr[q][:, j:j + 1]).then_inc(normed, 1)
                    act.wait_ge(normed, 4 * b + 4)
                    act.dma_start(at(x2, b), k.rows_out[q][:]).then_inc(put[q], 16)
                    for j in range(4):
                        nc.scalar.activation(f.out[q][:, quarter[j]], k.rows_out[q][:, quarter[j]], ACT.Copy,
                                             scale=f.rstd2[q][:, j:j + 1]).then_inc(outed, 1)
                    act.wait_ge(outed, 4 * b + 4)
                    if tail(t, 0):
                        act.dma_start(out_tail, f.out[q][0:m.TP, :]).then_inc(put[q], 16)
                    else:
                        act.dma_start(at(out_full, b), f.out[q][:]).then_inc(put[q], 16)
            run(act, body)
            prep.scalar_end(act)

        @block.tensor
        def _(pe):
            norm.tensor(pe)
            pe.wait_ge(norm.out, 2)
            prep.tensor(pe)


class EdgePrep:

    def __init__(self, m, k, l, w, sorted_dram):
        self.m, self.k, self.l, self.w, self.sorted = m, k, l, w, sorted_dram
        self.nbr, self.f_in, self.groups = w["Wf1"].shape[0], 6, m.ET // 4

    def scratch(self):
        m, l = self.m, self.l
        l.big = m.sb("l_big", [P, m.EPAD])
        l.W2v, l.W1v, l.W1vT, l.Wf1 = m.sb("l_W2v", [P, P]), m.sb("l_W1v", [P, 2, P]), m.sb("l_W1vT", [P, 2, P]), m.sb("l_Wf1", [P, 4, P])
        l.fst, l.fT, l.diag = ([m.sb(f"l_{n}{q}", s) for q in range(2)] for n, s in (("fst", [P, 4, 32]), ("fT", [P, P]), ("diag", [P, 4, P])))

    def begin(self):
        names = ("zeroed", "loaded", "rows", "nexts", "own", "squares", "root", "wt", "wps", "wout", "wprod", "staged",
                 "turned", "tout", "hps", "absd", "relu", "diag", "spread", "keys", "exp", "log", "made")
        self.s = {n: self.m.sem(f"prep_{n}") for n in names}
        l, w = self.l, self.w
        self.loads = [(l.Ws[:], w["W_in2f_s"]), (l.Wv[:], w["W_in2f_v"]), (l.W2s[:], w["W2_s"]), (l.W2v[:], w["W2_v"]),
                      (l.W1s[:], w["W1_s"].rearrange("(f c) o -> f c o", c=2)),
                      (l.W1v[:], w["W1_v"].rearrange("(f c) o -> f c o", c=2)),
                      (l.Wf2[:], w["Wf2"][:, 0:4 * P]), (l.bf1[:], w["bf1"].rearrange("(f o) -> f o", o=1)),
                      (l.bf2[:], w["bf2"][0:4 * P].rearrange("(o f) -> o f", o=1).to_broadcast([P, 4 * P]))]
        self.loads += [(l.Wf1[32 * g:32 * g + self.nbr, g, :], w["Wf1"]) for g in range(4)]

    def load(self, sp):
        m, l, s = self.m, self.l, self.s
        with m.nc.allow_non_contiguous_dma(reason="one word of each sorted row, small weights"):
            sp.dma_start(l.edges[:], self.sorted[0:m.EPAD, :].rearrange("(t p) w -> p t w", p=P)).then_inc(s["rows"], 16)
            sp.dma_start(l.nexti[:], self.sorted[1:m.EPAD + 1, :].rearrange("(t p) w -> p t w", p=P)[:, :, 0]).then_inc(s["nexts"], 16)
            sp.wait_ge(s["zeroed"], 1)
            for dst, src in self.loads:
                sp.dma_start(dst, src).then_inc(s["loaded"], 16)

    def starts(self, t):
        return isinstance(t.group, int) and t.s == 0

    def unit(self, t):
        return 2 * t.group + t.s // 2, (t.s // 2) % 2

    def zero(self, dve):
        self.m.nc.vector.memset(self.l.Wf1[:], 0.0).then_inc(self.s["zeroed"], 1)

    def vector_early(self, dve, t):
        nc, k, l, s = self.m.nc, self.k, self.l, self.s
        if self.starts(t):
            self.coefficients(dve)
        if not t.runs(0):
            return
        g, q = self.unit(t)
        if t.s % 2 == 0:
            nc.vector.tensor_copy(l.fst[q][:, :, 0:self.nbr],
                                  l.pay[:, bass.ds(4 * g, 4), self.f_in:self.f_in + self.nbr]).then_inc(s["staged"], 1)
        else:
            dve.wait_ge(s["turned"], g + 1)
            nc.vector.tensor_copy(l.fT[q][:], k.ps_b[q][:, 0:P]).then_inc(s["tout"], 1)
            ge(dve, s["spread"], g - 1)
            nc.vector.tensor_tensor(l.diag[q][:], k.ident[:].unsqueeze(1).to_broadcast([P, 4, P]),
                                    l.skey[:, bass.ds(4 * g, 4)].unsqueeze(2).to_broadcast([P, 4, P]),
                                    ALU.mult).then_inc(s["diag"], 1)

    def hidden(self, dve, g, q):
        l, s = self.l, self.s
        dve.wait_ge(s["absd"], g + 1)
        self.m.nc.vector.tensor_scalar(l.hT[:, bass.ds(4 * P * g, 4 * P)], self.k.ps_c[q][:], l.bf1[:, 0:1], 0.0,
                                       ALU.add, ALU.max).then_inc(s["relu"], 1)

    def vector_late(self, dve, t):
        if t.runs(0) and t.s % 2 == 0 and not self.starts(t):
            g, q = self.unit(t)
            self.hidden(dve, g - 1, 1 - q)

    def vector_end(self, dve):
        nc, m, l, s = self.m.nc, self.m, self.l, self.s
        self.hidden(dve, self.groups - 1, (self.groups - 1) % 2)
        dve.wait_ge(s["relu"], self.groups)
        for i in range(4):
            part = slice(i * m.EPAD // 4, (i + 1) * m.EPAD // 4)
            dve.wait_ge(s["log"], i + 1)
            nc.vector.scalar_tensor_tensor(l.hT[:, part], l.big[:, part], -LOG2, l.hT[:, part], ALU.add, ALU.add).then_inc(s["made"], 1)
        dve.wait_ge(s["made"], 4)

    def coefficients(self, dve):
        nc, k, l, s, ET = self.m.nc, self.k, self.l, self.s, self.m.ET
        v = Steps(dve, s["own"])
        dve.wait_ge(s["rows"], 16)
        dve.wait_ge(s["nexts"], 16)
        for dst, src in ((l.skey, l.edges[:, :, 0]), (l.src, l.edges[:, :, 0]), (l.dst, l.edges[:, :, 1]), (l.next, l.nexti[:])):
            v.link(nc.vector.tensor_copy(dst[:], src))
        v.link(nc.vector.memset(l.rows[:, 0:4], -1.0))
        for q in range(2):
            v.link(nc.vector.memset(l.fst[q][:], 0.0))
        r = l.pay[:, :, 3:6]
        v.link(nc.vector.tensor_tensor(l.yv[:], r, r, ALU.mult))
        nc.vector.tensor_reduce(l.n2[:], l.yv[:], axis=AX.X, op=ALU.add).then_inc(s["squares"], 1)
        dve.wait_ge(s["loaded"], 16 * len(self.loads))
        root_c, root_2f = 1.0 / float(np.sqrt(P)), 1.0 / float(np.sqrt(2 * P))
        for w, c in ((l.Ws, root_c), (l.Wv, root_c), (l.W2s, root_c), (l.W2v, root_c), (l.W1s, root_2f), (l.W1v, root_2f)):
            nc.vector.tensor_scalar(w[:], w[:], c, None, ALU.mult).then_inc(s["wt"], 1)
        dve.wait_ge(s["root"], 1)
        v.link(nc.vector.reciprocal(l.n2[:], l.norm[:]))
        v.link(nc.vector.tensor_tensor(l.yv[:], r, l.n2[:].unsqueeze(2).to_broadcast([P, ET, 3]), ALU.mult))
        v.link(nc.vector.tensor_scalar(l.yv[:], l.yv[:], Y1_SCALE, None, ALU.mult))
        v.link(nc.vector.tensor_tensor(l.c_v[:], l.yv[:], l.pay[:, :, 2:3].to_broadcast([P, ET, 3]), ALU.mult))
        v.link(nc.vector.tensor_scalar(l.c_s[:], l.c_v[:], 1.0 / float(np.sqrt(3.0)), None, ALU.mult))
        v.link(nc.vector.tensor_scalar(l.c_0[:], l.pay[:, :, 2], Y0, None, ALU.mult))
        dve.wait_ge(s["wps"], 1)
        nc.vector.tensor_copy(l.W1vT[:], k.ps_b[0][:, 0:2 * P].rearrange("p (a b) -> p a b", a=2)).then_inc(s["wout"], 1)
        dve.wait_ge(s["wprod"], 1)
        v.link(nc.vector.tensor_copy(l.Wvv[:], k.ps_b[1][:, 0:2 * P].rearrange("p (a b) -> p a b", a=2)))

    def leave(self, act, g, q):
        nc, l, s, k = self.m.nc, self.l, self.s, self.k
        act.wait_ge(s["hps"], g + 1)
        nc.scalar.activation(l.big[:, bass.ds(4 * P * g, 4 * P)], k.ps_c[q][:], ACT.Abs, bias=l.bf1[:, 0:1]).then_inc(s["absd"], 1)
        act.wait_ge(s["spread"], g + 1)
        nc.scalar.copy(l.rows[:, bass.ds(4 * P * g + 4, 4 * P)], k.ps_a[q][:]).then_inc(s["keys"], 1)

    def scalar_turn(self, act, t):
        if self.starts(t):
            act.wait_ge(self.s["squares"], 1)
            self.m.nc.scalar.activation(self.l.norm[:], self.l.n2[:], ACT.Sqrt).then_inc(self.s["root"], 1)
        elif t.runs(0) and t.s % 2 == 0:
            g, q = self.unit(t)
            self.leave(act, g - 1, 1 - q)

    def scalar_end(self, act):
        nc, m, k, l, s = self.m.nc, self.m, self.k, self.l, self.s
        self.leave(act, self.groups - 1, (self.groups - 1) % 2)
        act.wait_ge(s["absd"], self.groups)
        part = [slice(i * m.EPAD // 4, (i + 1) * m.EPAD // 4) for i in range(4)]
        for i in range(4):
            nc.scalar.activation(l.big[:, part[i]], l.big[:, part[i]], ACT.Exp, scale=-1.0).then_inc(s["exp"], 1)
        for i in range(4):
            act.wait_ge(s["exp"], i + 1)
            nc.scalar.activation(l.big[:, part[i]], l.big[:, part[i]], ACT.Ln, bias=k.ones[:, 0:1]).then_inc(s["log"], 1)
        act.wait_ge(s["keys"], self.groups)

    def tensor(self, pe):
        nc, k, l, s = self.m.nc, self.k, self.l, self.s
        pe.wait_ge(s["wt"], 6)
        for a in range(2):
            i = nc.tensor.transpose(k.ps_b[0][:, a * P:(a + 1) * P], l.W1v[:, a, :], k.ident[:])
        i.then_inc(s["wps"], 1)
        pe.wait_ge(s["wout"], 1)
        for a in range(2):
            i = nc.tensor.matmul(k.ps_b[1][:, a * P:(a + 1) * P], l.W1vT[:, a, :], l.W2v[:], start=True, stop=True)
        i.then_inc(s["wprod"], 1)

        def group(g, q):
            pe.wait_ge(s["staged"], g + 1)
            nc.tensor.transpose(k.ps_b[q][:, 0:P], l.fst[q][:].rearrange("p a b -> p (a b)"), k.ident[:]).then_inc(s["turned"], 1)
            pe.wait_ge(s["tout"], g + 1)
            ge(pe, s["relu"], g - 1)
            for a in range(4):
                i = nc.tensor.matmul(k.ps_c[q][:, a * P:(a + 1) * P], l.Wf1[:, a, :], l.fT[q][:], start=True, stop=True)
            i.then_inc(s["hps"], 1)
            pe.wait_ge(s["diag"], g + 1)
            ge(pe, s["keys"], g - 1)
            nc.tensor.matmul(k.ps_a[q][:], k.ones[:], l.diag[q][:].rearrange("p a b -> p (a b)"),
                             start=True, stop=True).then_inc(s["spread"], 1)
        group(0, 0)
        group(1, 1)
        with pe.Fori(1, self.groups // 2) as g:
            group(2 * g, 0)
            group(2 * g + 1, 1)


@stage
def messages(m, k, l, x2_dram):
    nc, ET, D = m.nc, m.ET, m.D
    names = ("staged", "turned", "xT", "hcopy", "filt", "maps", "wb", "gate", "same", "u", "dot", "side",
             "msg", "sums", "agg", "outs", "scalars", "kept", "own_staged", "none")
    s = {n: m.sem(f"msg_{n}") for n in names}
    got, own_got = ([m.sem(f"msg_{n}{r}") for r in range(4)] for n in ("got", "own_got"))
    G, own = ([a[r][:] for r in range(4)] for a in (l.G, l.own))

    def run(engine, body, first=-3, last=ET):
        turns(engine, body, first, last, 4, ET // 4 - 2, ET)

    with nc.Block() as block:
        @block.gpsimd
        def _(pool):
            def body(t):
                if t.runs(3):
                    b, r = t.block(3), t.slot(3, 4)
                    ge(pool, s["staged"], b + 1)
                    ge(pool, s["turned"], b - 2)
                    if t.runs(4):
                        nc.gpsimd.tensor_copy(l.idx[t.slot(4, 4)][:], l.dst[:, bass.ds(b + 1, 1)]).then_inc(s["staged"], 1)
                    pool.indirect_dma_start(G[r], None, x2_dram,
                                            bass.IndirectOffsetOnAxis(ap=l.idx[r][:, 0:1], axis=0)).then_inc(got[r], 16)
                if t.runs(1):
                    b, r = t.block(1), t.slot(1, 4)
                    ge(pool, s["own_staged"], b + 1)
                    ge(pool, s["scalars"], 2 * (b - 2))
                    ge(pool, s["kept"], b - 2)
                    if t.runs(2):
                        nc.gpsimd.tensor_copy(l.idx2[t.slot(2, 4)][:], l.src[:, bass.ds(b + 1, 1)]).then_inc(s["own_staged"], 1)
                    pool.indirect_dma_start(own[r], None, x2_dram,
                                            bass.IndirectOffsetOnAxis(ap=l.idx2[r][:, 0:1], axis=0)).then_inc(own_got[r], 16)
            nc.gpsimd.tensor_copy(l.idx[0][:], l.dst[:, 0:1]).then_inc(s["staged"], 1)
            nc.gpsimd.tensor_copy(l.idx2[0][:], l.src[:, 0:1]).then_inc(s["own_staged"], 1)
            run(pool, body)

        @block.tensor
        def _(pe):
            def body(t):
                if t.runs(0):
                    b, q = t.block(), t.slot(0, 2)
                    pe.wait_ge(s["msg"], b + 1)
                    pe.wait_ge(s["side"], 3 * (b + 1))
                    pe.wait_ge(s["same"], 2 * b + 1)
                    ge(pe, s["agg"], 8 * b)
                    for c in range(8):
                        i = nc.tensor.matmul(l.ps[4 + c // 4][:, (c % 4) * P:(c % 4 + 1) * P], l.msg[q][:, c, :],
                                             l.same[q][:], start=True, stop=True)
                    i.then_inc(s["sums"], 1)
                if t.runs(-1):
                    b, q = t.block(-1), t.slot(-1, 2)
                    pe.wait_ge(s["agg"], 8 * (b + 1))
                    ge(pe, s["scalars"], 2 * b)
                    ge(pe, s["kept"], b)
                    o = l.ps[6]
                    for c in range(2):
                        nc.tensor.matmul(l.ps[7][:, 0:P], l.W1s[:, c, :], l.agg[q][:, c, :], start=(c == 0), stop=(c == 1))
                    for i in range(3):
                        for c in range(2):
                            x = nc.tensor.matmul(o[:, i * P:(i + 1) * P], l.agg[q][:, 2 + 3 * c + i, :], l.Wvv[:, c, :],
                                                 start=(c == 0), stop=(c == 1))
                    x.then_inc(s["outs"], 1)
                if t.runs(2):
                    b, q, r = t.block(2), t.slot(2, 2), t.slot(2, 4)
                    pe.wait_ge(got[r], 16 * (t.round(2, 4) + 1))
                    ge(pe, s["xT"], b)
                    for c in range(4):
                        src = G[r][:, 0:P] if c == 0 else G[r][:, P:D].rearrange("p (c i) -> p i c", i=3)[:, c - 1, :]
                        i = nc.tensor.transpose(l.ps[0][:, c * P:(c + 1) * P], src, k.ident[:])
                    i.then_inc(s["turned"], 1)
                    pe.wait_ge(s["hcopy"], b + 1)
                    ge(pe, s["wb"], b)
                    nc.tensor.matmul(l.ps[1][:], l.hb[q][:], l.Wf2[:], start=True, stop=True).then_inc(s["filt"], 1)
                    pe.wait_ge(s["xT"], b + 1)
                    ge(pe, s["msg"], b - 1)
                    for c in range(4):
                        i = nc.tensor.matmul(l.ps[2 + q][:, c * P:(c + 1) * P], l.xT[q][:, c, :],
                                             (l.Ws if c == 0 else l.Wv)[:], start=True, stop=True)
                    i.then_inc(s["maps"], 1)
            run(pe, body)

        @block.scalar
        def _(act):
            def body(t):
                if t.runs(2):
                    b, q = t.block(2), t.slot(2, 2)
                    ge(act, s["filt"], b - 1)
                    nc.scalar.copy(l.hb[q][:], l.hT[:, bass.ds(P * b, P)]).then_inc(s["hcopy"], 1)
                if t.runs(1):
                    b, q = t.block(1), t.slot(1, 2)
                    act.wait_ge(s["wb"], b + 1)
                    ge(act, s["msg"], b - 1)
                    nc.scalar.activation(l.gate[q][:], l.Wb[q][:, 2 * P:4 * P].rearrange("p (f c) -> p c f", c=2)[:, 1, :],
                                         ACT.Copy, scale=l.c_0[:, bass.ds(b, 1)]).then_inc(s["gate"], 1)
                    act.wait_ge(s["u"], b + 1)
                    ge(act, s["sums"], b - 1)
                    for i in range(3):
                        nc.scalar.activation(l.msg[q][:, 2 + i, :], l.u[q][:], ACT.Copy,
                                             scale=l.c_v[:, bass.ds(b, 1), i]).then_inc(s["side"], 1)
                if t.runs(-1):
                    b, r = t.block(-1), t.slot(-1, 4)
                    act.wait_ge(s["outs"], b + 1)
                    nc.scalar.copy(l.sT[:, bass.ds(P * b, P)], l.ps[7][:, 0:P]).then_inc(s["scalars"], 1)
                    act.wait_ge(own_got[r], 16 * (t.round(-1, 4) + 1))
                    nc.scalar.copy(l.X[:, bass.ds(b, 1), 0:P].rearrange("p a f -> p (a f)"), own[r][:, 0:P]).then_inc(s["scalars"], 1)
                if t.runs(2):
                    b, q = t.block(2), t.slot(2, 2)
                    act.wait_ge(s["turned"], b + 1)
                    ge(act, s["maps"], b - 1)
                    nc.scalar.copy(l.xT[q][:], l.ps[0][:].rearrange("p (c n) -> p c n", c=4)).then_inc(s["xT"], 1)
            run(act, body)
            act.wait_ge(s["scalars"], 2 * ET)

        @block.vector
        def _(dve):
            def body(t):
                if t.runs(1):
                    b, q = t.block(1), t.slot(1, 2)
                    ge(dve, s["sums"], b - 1)
                    nc.vector.tensor_scalar(l.same[q][:], l.rows[:, bass.ds(P * b + 4, P)], l.skey[:, bass.ds(b, 1)],
                                            None, ALU.is_equal).then_inc(s["same"], 1)
                    ge(dve, s["agg"], 8 * (b - 1))
                    nc.vector.tensor_scalar(l.cont[q][:], l.rows[:, bass.ds(P * b + 4, P)], l.rows[:, bass.ds(P * b + 3, 1)],
                                            None, ALU.is_equal).then_inc(s["same"], 1)
                    dve.wait_ge(s["wb"], b + 1)
                    dve.wait_ge(s["maps"], b + 1)
                    sj = l.ps[2 + q][:, 0:P]
                    v = [l.ps[2 + q][:, (i + 1) * P:(i + 2) * P] for i in range(3)]
                    fs = l.Wb[q][:, 0:2 * P].rearrange("p (f c) -> p c f", c=2)
                    fv = l.Wb[q][:, 2 * P:4 * P].rearrange("p (f c) -> p c f", c=2)
                    ge(dve, s["side"], 3 * (b - 1))
                    nc.vector.tensor_tensor(l.u[q][:], sj, fv[:, 0, :], ALU.mult).then_inc(s["u"], 1)
                    ge(dve, s["msg"], b)
                    nc.vector.tensor_scalar(l.dot[:], v[0], l.c_s[:, bass.ds(b, 1), 0], None, ALU.mult).then_inc(s["dot"], 1)
                    nc.vector.scalar_tensor_tensor(l.msg[q][:, 0, :], sj, l.c_0[:, bass.ds(b, 1)], fs[:, 0, :], ALU.mult, ALU.mult)
                    dve.wait_ge(s["dot"], 3 * b + 1)
                    nc.vector.scalar_tensor_tensor(l.dot[:], v[1], l.c_s[:, bass.ds(b, 1), 1], l.dot[:], ALU.mult, ALU.add).then_inc(s["dot"], 1)
                    dve.wait_ge(s["gate"], b + 1)
                    nc.vector.tensor_tensor(l.msg[q][:, 5:8, :], l.ps[2 + q][:, P:4 * P].rearrange("p (i f) -> p i f", i=3),
                                            l.gate[q][:].unsqueeze(1).to_broadcast([P, 3, P]), ALU.mult)
                    dve.wait_ge(s["dot"], 3 * b + 2)
                    nc.vector.scalar_tensor_tensor(l.dot[:], v[2], l.c_s[:, bass.ds(b, 1), 2], l.dot[:], ALU.mult, ALU.add).then_inc(s["dot"], 1)
                    dve.wait_ge(s["dot"], 3 * b + 3)
                    nc.vector.tensor_tensor(l.msg[q][:, 1, :], l.dot[:], fs[:, 1, :], ALU.mult).then_inc(s["msg"], 1)
                if t.runs(0):
                    b, q = t.block(), t.slot(0, 2)
                    dve.wait_ge(s["sums"], b + 1)
                    dve.wait_ge(s["same"], 2 * b + 2)
                    ge(dve, s["outs"], b - 1)
                    ge(dve, s["agg"], 8 * b)
                    for c in range(8):
                        nc.vector.scalar_tensor_tensor(l.agg[q][:, c, :], l.cont[q][:], l.agg[1 - q][:, c, P - 1:P],
                                                       l.ps[4 + c // 4][:, (c % 4) * P:(c % 4 + 1) * P],
                                                       ALU.mult, ALU.add).then_inc(s["agg"], 1)
                if t.runs(-1):
                    b, r = t.block(-1), t.slot(-1, 4)
                    dve.wait_ge(s["outs"], b + 1)
                    dve.wait_ge(own_got[r], 16 * (t.round(-1, 4) + 1))
                    nc.vector.tensor_tensor(l.X[:, bass.ds(b, 1), P:D].rearrange("p a (d i) -> p (a d) i", i=3),
                                            own[r][:, P:D].rearrange("p (d i) -> p d i", i=3),
                                            l.ps[6][:, 0:3 * P].rearrange("p (i d) -> p d i", i=3), ALU.add).then_inc(s["kept"], 1)
                if t.runs(2):
                    b, q = t.block(2), t.slot(2, 2)
                    dve.wait_ge(s["filt"], b + 1)
                    nc.vector.tensor_tensor(l.Wb[q][:], l.ps[1][:], l.bf2[:], ALU.add).then_inc(s["wb"], 1)
            nc.vector.memset(l.agg[1][:], 0.0).then_inc(s["none"], 1)
            dve.wait_ge(s["none"], 1)
            run(dve, body)
            dve.wait_ge(s["kept"], ET)


@stage
def touched(m, k, l, out_dram):
    nc, ET = m.nc, m.ET
    mag = l.rows[:, 0:m.EPAD]
    names = ("mag", "exp", "log", "pos", "plus", "vec", "hcopy", "prod", "ysum", "stats", "aggr", "root", "rec", "nmr", "done", "idx2")
    s = {n: m.sem(f"tch_{n}") for n in names}
    RING = 8
    put = [m.sem(f"tch_put{r}") for r in range(RING)]
    parts = 4
    part = [slice(i * m.EPAD // parts, (i + 1) * m.EPAD // parts) for i in range(parts)]

    def x_row(b):
        return l.X[:, bass.ds(b, 1), :].rearrange("p a f -> p (a f)")

    def run(engine, body, first=-3, last=ET):
        turns(engine, body, first, last, 8, ET // 8 - 2, ET, 8)

    with nc.Block() as block:
        @block.scalar
        def _(act):
            for i in range(parts):
                nc.scalar.activation(mag[:, part[i]], l.sT[:, part[i]], ACT.Abs).then_inc(s["mag"], 1)
            for i in range(parts):
                act.wait_ge(s["mag"], i + 1)
                nc.scalar.activation(mag[:, part[i]], mag[:, part[i]], ACT.Exp, scale=-1.0).then_inc(s["exp"], 1)
            for i in range(parts):
                act.wait_ge(s["exp"], i + 1)
                nc.scalar.activation(mag[:, part[i]], mag[:, part[i]], ACT.Ln, bias=k.ones[:, 0:1]).then_inc(s["log"], 1)
            act.wait_ge(s["plus"], parts)

            def body(t):
                if t.runs(3):
                    b, q = t.block(3), t.slot(3, 2)
                    ge(act, s["prod"], b - 1)
                    nc.scalar.copy(l.hb[q][:], l.sT[:, bass.ds(P * b, P)]).then_inc(s["hcopy"], 1)
                if t.runs(0):
                    b, q = t.block(), t.slot(0, 2)
                    act.wait_ge(s["aggr"], b + 1)
                    nc.scalar.activation(l.std[q][:], l.mv[q][:, 1:2], ACT.Sqrt, bias=k.eps[:, 0:1]).then_inc(s["root"], 1)
                if t.runs(-1):
                    b, q, r = t.block(-1), t.slot(-1, 2), t.slot(-1, RING)
                    act.wait_ge(s["nmr"], b + 1)
                    ge(act, put[r], 16 * t.round(-1, RING))
                    nc.scalar.activation(l.Y[r], x_row(b), ACT.Identity, scale=l.rstd[q][:], bias=l.nmr[q][:]).then_inc(s["done"], 1)
            run(act, body)

        @block.gpsimd
        def _(pool):
            ge(pool, s["vec"], 3)

            def body(t):
                if t.runs(-1):
                    b, r, r_next = t.block(-1), t.slot(-1, RING), t.slot(0, RING)
                    ge(pool, s["idx2"], b + 1)
                    ge(pool, s["done"], b + 1)
                    ge(pool, put[r_next], 16 * t.round(0, RING))
                    if t.runs(0):
                        nc.gpsimd.tensor_copy(l.idx2[r_next][:], l.row[:, bass.ds(b + 1, 1)]).then_inc(s["idx2"], 1)
                    pool.indirect_dma_start(out_dram, bass.IndirectOffsetOnAxis(ap=l.idx2[r][:, 0:1], axis=0), l.Y[r], None,
                                            bounds_check=m.N - 1, oob_is_err=False).then_inc(put[r], 16)
            nc.gpsimd.tensor_copy(l.idx2[0][:], l.row[:, 0:1]).then_inc(s["idx2"], 1)
            run(pool, body)
            for r in range(RING):
                ge(pool, put[r], 16 * (ET // RING))

        @block.tensor
        def _(pe):
            def body(t):
                if t.runs(3):
                    b, q = t.block(3), t.slot(3, 2)
                    pe.wait_ge(s["hcopy"], b + 1)
                    ge(pe, s["ysum"], b - 1)
                    nc.tensor.matmul(l.ps[q][:, 0:P], l.hb[q][:], l.W2s[:], start=True, stop=True).then_inc(s["prod"], 1)
            run(pe, body)

        @block.vector
        def _(dve):
            v = Steps(dve, s["vec"])
            v.link(nc.vector.tensor_tensor(l.more[:], l.skey[:], l.next[:], ALU.is_equal))
            v.link(nc.vector.scalar_tensor_tensor(l.rowf[:], l.more[:], float(SKIP), l.skey[:], ALU.mult, ALU.add))
            v.link(nc.vector.tensor_copy(l.row[:], l.rowf[:]))
            for i in range(parts):
                dve.wait_ge(s["mag"], i + 1)
                nc.vector.tensor_scalar(l.sT[:, part[i]], l.sT[:, part[i]], 0.0, None, ALU.max).then_inc(s["pos"], 1)
            dve.wait_ge(s["pos"], parts)
            for i in range(parts):
                dve.wait_ge(s["log"], i + 1)
                nc.vector.scalar_tensor_tensor(l.sT[:, part[i]], mag[:, part[i]], -LOG2, l.sT[:, part[i]],
                                               ALU.add, ALU.add).then_inc(s["plus"], 1)

            def body(t):
                b = t.block()
                if t.runs(1):
                    dve.wait_ge(s["ysum"], b + 2)
                if t.runs(0):
                    dve.wait_ge(s["stats"], b + 1)
                    ge(dve, s["aggr"], b)
                    ge(dve, s["nmr"], b - 1)
                if t.runs(2):
                    x = l.X[:, bass.ds(b + 2, 1), 0:P].rearrange("p a f -> p (a f)")
                    dve.wait_ge(s["prod"], b + 3)
                    nc.vector.tensor_tensor(x, x, l.ps[t.slot(2, 2)][:, 0:P], ALU.add).then_inc(s["ysum"], 1)
                if t.runs(1):
                    nc.vector.bn_stats(l.st[t.slot(1, 2)][:], x_row(b + 1)).then_inc(s["stats"], 1)
                if t.runs(0):
                    q = t.slot(0, 2)
                    nc.vector.bn_aggr(l.mv[q][:], l.st[q][:]).then_inc(s["aggr"], 1)
                if t.runs(-1):
                    b, q = t.block(-1), t.slot(-1, 2)
                    dve.wait_ge(s["root"], b + 1)
                    ge(dve, s["done"], b - 1)
                    nc.vector.reciprocal(l.rstd[q][:], l.std[q][:]).then_inc(s["rec"], 1)
                    dve.wait_ge(s["rec"], b + 1)
                    nc.vector.scalar_tensor_tensor(l.nmr[q][:], l.mv[q][:, 0:1], -1.0, l.rstd[q][:], ALU.mult, ALU.mult).then_inc(s["nmr"], 1)
            run(dve, body)


class Bag:
    pass


def build(nc, x, src, dst, attr20, attr3, weight, W, b, gamma, beta, net, out):
    n_nodes, d = x.shape
    n_edges, = src.shape
    n_layers = W.shape[0]
    n_rbf = attr20.shape[1]
    with ExitStack() as whole:
        m = Machine(nc, whole, n_nodes, n_edges, d)
        ET, NC, EPAD = m.ET, m.NCOL, m.EPAD
        width = 6 + n_rbf
        agg = [m.dram(f"agg{i}", [m.NPAD, d]) for i in range(2)]
        merged_dram = m.dram("merged", [EPAD, d])
        x2_dram = m.dram("x2", [m.NPAD, d])
        dinv_dram = m.dram("dinv_rows", [m.NPAD, 1])
        by_dst = m.dram("by_dst", [EPAD, 2], I32)
        by_src = m.dram("by_src", [EPAD + 1, width], I32)

        k = Bag()
        k.ident, k.ones, k.before, k.after, k.count = (m.sb(n, [P, P]) for n in ("ident", "ones", "before", "after", "count"))
        k.part, k.eps = m.sb("part", [P, 1]), m.sb("eps", [P, 1])
        constants(m, k)
        k.node = n = Bag()
        n.dinv, n.self_w, n.edge_w = (m.sb(f"node_{s}", [P, NC]) for s in ("dinv", "self_w", "edge_w"))
        n.row = m.sb("node_row", [P, NC], I32)
        n.idx = [m.sb(f"node_idx{q}", [P, 4], I32) for q in range(4)]
        bn = k.bn = Bag()
        bn.mv = m.sb("bn_mv", [P, m.C, 2])
        bn.std, bn.mean, bn.scale, bn.shift = (m.sb(f"bn_{s}", [P, m.C]) for s in ("std", "mean", "scale", "shift"))
        k.param = m.sb("param", [P, 3, n_layers * m.C])

        l = Bag()
        l.edges = m.sb("l_edges", [P, ET, width], I32)
        l.pay = l.edges[:].bitcast(F32)
        l.rows, l.hT = m.sb("l_rows", [P, EPAD + 4]), m.sb("l_hT", [P, EPAD])
        l.skey, l.next, l.more, l.rowf = (m.sb(f"l_{s}", [P, ET]) for s in ("skey", "next", "more", "rowf"))
        l.src, l.dst, l.row, l.nexti = (m.sb(f"l_{s}", [P, ET], I32) for s in ("src", "dst", "row", "nexti"))
        l.Ws, l.Wv, l.W2s = (m.sb(f"l_{s}", [P, P]) for s in ("Ws", "Wv", "W2s"))
        l.W1s, l.Wvv = (m.sb(f"l_{s}", [P, 2, P]) for s in ("W1s", "Wvv"))
        l.Wf2 = m.sb("l_Wf2", [P, 4 * P])
        l.bf1, l.bf2 = m.sb("l_bf1", [P, 1]), m.sb("l_bf2", [P, 4 * P])
        l.yv, l.c_v, l.c_s = (m.sb(f"l_{s}", [P, ET, 3]) for s in ("yv", "c_v", "c_s"))
        l.n2, l.norm, l.c_0 = (m.sb(f"l_{s}", [P, ET]) for s in ("n2", "norm", "c_0"))
        prep = EdgePrep(m, k, l, net, by_src)
        edge_sort = ExitStack()
        m.ctx = edge_sort
        payload = m.sb("payload", [P, ET, width], I32)
        place_dst, place_src = (m.sb(f"place_{s}", [P, ET], I32) for s in ("dst", "src"))
        bufs = [m.sb(f"scatter_idx{r}", [P, 1], I32) for r in range(4)], [m.sb(f"scatter_row{r}", [P, width], I32) for r in range(4)]
        rows_by_dst = Scatter(m, "by_dst", payload, 2, place_dst, bufs, by_dst)
        rows_by_src = Scatter(m, "by_src", payload, width, place_src, bufs, by_src)

        with ExitStack() as part:
            m.ctx = part
            w = k.sort = Bag()
            w.key, w.tmp, w.tmp2 = (m.sb(f"sort_{s}", [P, ET], I32) for s in ("key", "tmp", "tmp2"))
            w.keyf, w.lof, w.colf, w.rank, w.pos = (m.sb(f"sort_{s}", [P, ET]) for s in ("keyf", "lof", "colf", "rank", "pos"))
            w.hot_col, w.hot_lo = m.sb("hot_col", [P, ET, NC], BF16), m.sb("hot_lo", [P, ET, P], BF16)
            w.keyrow, w.hot_loT = m.sb("keyrow", [P, EPAD]), m.sb("hot_loT", [P, EPAD])
            w.diag = [m.sb(f"diag{q}", [P, 4, P]) for q in range(2)]
            w.cnt, w.end, w.has, w.tmpn, w.tmpn2 = (m.sb(f"sort_{s}", [P, NC]) for s in ("cnt", "end", "has", "tmpn", "tmpn2"))
            w.rowsum, w.rowsum2, w.scan = (m.sb(f"sort_{s}", [P, m.NB]) for s in ("rowsum", "rowsum2", "scan"))
            w.pre = m.sb("sort_pre", [P, 2 * m.NB])
            w.base = [m.sb(f"sort_base{r}", [P, NC]) for r in range(4)]
            w.lt = [m.sb(f"sort_lt{r}", [P, P]) for r in range(4)]
            w.junk, w.junk2 = m.sb("sort_junk", [P, P]), m.sb("sort_junk2", [P, NC])
            w.ps_row = [m.ps(f"ps_row{q}", [P, 512]) for q in range(2)]
            w.ps_cnt = m.ps("ps_cnt", [P, 512])
            w.ps_new = [m.ps(f"ps_new{q}", [P, 512]) for q in range(2)]
            w.ps_look = [m.ps(f"ps_look{q}", [P, 512]) for q in range(2)]
            w.ps_pre = m.ps("ps_pre", [P, 512])
            load_edges(m, k, payload, (src, dst, weight, attr3, attr20), (b, gamma, beta), by_src, n_layers)
            sort_by(m, k, "dst", dst, place_dst, n, None)
            sort_by(m, k, "src", src, place_src, None, rows_by_dst)

        with ExitStack() as part:
            m.ctx = part
            w = k.sort = Bag()
            e = k.edge = Bag()
            e.pair = m.sb("edge_pair", [P, ET, 2], I32)
            e.src = m.sb("edge_src", [P, ET], I32)
            e.skey, e.dsrc = m.sb("edge_key", [P, ET]), m.sb("edge_dsrc", [P, ET])
            e.rows = l.rows[:, 4:EPAD + 4]
            e.tiles = m.sb("edge_tiles", [ET, 2 * P], I32)
            e.tkey, e.tjunk = m.sb("edge_tkey", [ET, P]), m.sb("edge_tjunk", [ET, P])
            e.run, e.run2 = m.sb("edge_run", [ET, 1]), m.sb("edge_run2", [ET, 1])
            e.fix_row = m.sb("edge_fix_row", [ET, 1], I32)
            e.lacks = m.sb("edge_lacks", [ET, ET])
            e.idx = [m.sb(f"edge_idx{q}", [P, 1], I32) for q in range(8)]
            e.val = [m.sb(f"edge_val{q}", [P, 1]) for q in range(4)]
            e.same = [m.sb(f"edge_same{q}", [P, P]) for q in range(2)]
            k.R = [m.sb(f"R{r}", [P, 4 * d]) for r in range(4)]
            k.Cb = [m.sb(f"Cb{r}", [P, 4 * d]) for r in range(2)]
            k.rows_out = [m.sb(f"rows_out{r}", [P, 4 * d]) for r in range(2)]
            k.scale, k.shift = m.sb("scale", [P, d]), m.sb("shift", [P, d])
            k.stat = m.sb("stat", [P, m.C, 6 * m.NB])
            k.ps_a, k.ps_b, k.ps_c = ([m.ps(f"ps_{s}{q}", [P, 512]) for q in range(2)] for s in "abc")
            w.diag = [k.rows_out[q][:, 0:4 * P].rearrange("p (a b) -> p a b", a=4) for q in range(2)]
            w.ps_row = k.ps_a
            sorted_edges(m, k, "dst", by_dst, 2, 1, e.rows, e.skey, e.pair)
            with ExitStack() as inner:
                m.ctx = inner
                k.whi, k.wlo = m.sb("whi", [P, m.C, d], F32R), m.sb("wlo", [P, m.C, d], F32R)
                k.yhi = [m.sb(f"yhi{q}", [P, m.C, 4 * P], F32R) for q in range(2)]
                k.ylo = [m.sb(f"ylo{q}", [P, m.C, 4 * P], F32R) for q in range(2)]
                k.aggT = [m.sb(f"aggT{q}", [P, m.C, 4 * P]) for q in range(2)]
                table = x
                for layer in range(n_layers):
                    layer_stage(m, k, layer, dinv_dram, by_dst, W, table, agg[layer % 2], merged_dram, rows_by_src if layer == 0 else None)
                    table = agg[layer % 2]
            m.ctx = part
            f = k.fin = Bag()
            f.out = [m.sb(f"fin_out{q}", [P, 4 * d]) for q in range(2)]
            f.st = m.sb("fin_st", [P, 4, 6])
            f.mv = [m.sb(f"fin_mv{q}", [P, 4, 2]) for q in range(2)]
            f.std, f.rstd, f.nmr, f.v2, f.std2, f.rstd2 = ([m.sb(f"fin_{s}{q}", [P, 4]) for q in range(2)]
                                                           for s in ("std", "rstd", "nmr", "v2", "std2", "rstd2"))
            prep.scratch()
            finish_gcn(m, k, n_layers, table, x, x2_dram, out, prep)

        edge_sort.close()

        with ExitStack() as part:
            m.ctx = part
            l.sT = m.sb("l_sT", [P, EPAD])
            l.X = m.sb("l_X", [P, ET, d])
            l.G = [m.sb(f"l_G{r}", [P, d]) for r in range(4)]
            l.idx = [m.sb(f"l_idx{r}", [P, 1], I32) for r in range(4)]
            l.idx2 = [m.sb(f"l_idx2{r}", [P, 1], I32) for r in range(8)]
            l.own = [m.sb(f"l_own{r}", [P, d]) for r in range(4)]
            two = lambda s, shape: [m.sb(f"l_{s}{q}", shape) for q in range(2)]
            l.same, l.cont, l.u, l.hb, l.gate = (two(s, [P, P]) for s in ("same", "cont", "u", "hb", "gate"))
            l.xT, l.Wb = two("xT", [P, 4, P]), two("Wb", [P, 4 * P])
            l.msg, l.agg = two("msg", [P, 8, P]), two("agg", [P, 8, P])
            l.dot = m.sb("l_dot", [P, P])
            l.st, l.mv = two("st", [P, 6]), two("mv", [P, 2])
            l.std, l.rstd, l.nmr = (two(s, [P, 1]) for s in ("std", "rstd", "nmr"))
            l.Y = [a[:, 4 * h:4 * h + 4, :].rearrange("p a b -> p (a b)") for a in l.msg + l.agg for h in range(2)]
            l.ps = [m.ps(f"l_ps{i}", [P, 512]) for i in range(8)]
            messages(m, k, l, x2_dram)
            touched(m, k, l, out)


@stage
def load_edges(m, k, payload, arrays, params, by_src, n_layers):
    nc, ET = m.nc, m.ET
    filled, loaded = m.sem("pay_filled"), m.sem("pay_loaded")
    with ExitStack() as stack, nc.Block() as block:
        @block.vector
        def _(dve):
            nc.vector.memset(payload[:].bitcast(F32), 1.0).then_inc(filled, 1)
            nc.vector.memset(k.eps[:], LN_EPS).then_inc(filled, 1)
            dve.wait_ge(filled, 2)
            nc.vector.memset(payload[:, :, 0:2], m.NPAD - 1).then_inc(filled, 1)
            nc.vector.memset(k.sort.key[:], -1).then_inc(filled, 1)

        @block.sync
        def _(sp):
            stack.enter_context(nc.allow_non_contiguous_dma(reason="edge payloads and parameters, once"))
            n, at_word = 0, 0
            sp.wait_ge(filled, 4)
            for a in arrays:
                if len(a.shape) == 1:
                    a = a.rearrange("(e o) -> e o", o=1)
                wide = a.shape[1]
                to = payload[0:m.EP, :, at_word:at_word + wide]
                if a.dtype == F32:
                    to = to.bitcast(F32)
                sp.dma_start(to, a.rearrange("(p t) w -> p t w", t=ET)).then_inc(loaded, 16)
                at_word += wide
                n += 16
            for i, a in enumerate(params):
                for layer in range(n_layers):
                    sp.dma_start(k.param[:, i, layer * m.C:(layer + 1) * m.C],
                                 a[layer].rearrange("(c p) -> p c", p=P)).then_inc(loaded, 16)
                    n += 16
            sp.dma_start(by_src[m.EPAD:m.EPAD + 1, 0:2], k.sort.key[0:1, 0:2]).then_inc(loaded, 16)
            sp.wait_ge(loaded, n + 16)


NET = ["W_in2f_s", "W_in2f_v", "Wf1", "bf1", "Wf2", "bf2", "W1_s", "W1_v", "W2_s", "W2_v"]
_INS = ["x", "src", "dst", "edge_attr_20", "edge_attr_3", "edge_weight", "L0_gnn_W", "L0_gnn_b",
        "L0_gnn_gamma", "L0_gnn_beta"] + ["L1_gnn_" + n for n in NET]


def program(nc, a, out):
    build(nc, a["x"], a["src"], a["dst"], a["edge_attr_20"], a["edge_attr_3"], a["edge_weight"],
          a["L0_gnn_W"], a["L0_gnn_b"], a["L0_gnn_gamma"], a["L0_gnn_beta"],
          {n: a["L1_gnn_" + n] for n in NET}, out)


def kernel(**inputs):
    import concourse.bacc as _bacc
    from concourse import mybir as _mybir
    from concourse.bass_utils import run_bass_kernel_spmd as _run

    nc = _bacc.Bacc("TRN2", target_bir_lowering=False, num_devices=1)
    arrays, args = {}, {}
    for name in _INS:
        a = np.ascontiguousarray(inputs[name])
        arrays[f"in_{name}"] = a
        args[name] = nc.dram_tensor(f"in_{name}", a.shape, _mybir.dt.from_np(a.dtype), kind="ExternalInput").ap()
    out = nc.dram_tensor("out_0", inputs["x"].shape, F32, kind="ExternalOutput").ap()
    program(nc, args, out)
    r = _run(nc, [arrays], core_ids=[0])
    return r.results[0]["out_0"]
```
